# Optimizing a Trainium2 kernel written in Bass

```python
import numpy as np
import jax
import jax.numpy as jnp

def _softmax(x, axis=-1):
    return jax.nn.softmax(x, axis=axis)

def _gelu(x):
    return jax.nn.gelu(x, approximate=True)

def _silu(x):
    return jax.nn.silu(x)

def _sigmoid(x):
    return jax.nn.sigmoid(x)

def _layernorm(x, axis=-1, eps=1e-05):
    m = jnp.mean(x, axis=axis, keepdims=True)
    v = jnp.var(x, axis=axis, keepdims=True)
    return (x - m) / jnp.sqrt(v + eps)

def _scatter_add(tgt, idx, src, axis=0):
    return tgt.at[idx].add(src)

def _segment_sum(src, seg, n):
    return jax.ops.segment_sum(src, seg, n)
kernel_name = 'mk_decoder_preln_d2_seqx_r4_991326'

def setup_inputs(seed: int=0):
    np.random.seed(seed)
    _w = jnp.asarray

    def _rec_inputs():
        import jax
        import jax.numpy as jnp
        _rk = jax.random.key(seed)
        x = -0.0005207 + 1.001 * jax.random.normal(jax.random.fold_in(_rk, 1), (4, 512, 256), jnp.float32)
        _lenS = 512 - jax.random.randint(jax.random.fold_in(_rk, 7), (4,), 0, max(1, 512 // 4) + 1, jnp.int32)
        _lenS2 = 1601 - jax.random.randint(jax.random.fold_in(_rk, 8), (4,), 0, max(1, 1601 // 4) + 1, jnp.int32)
        _ctx_1024P = jax.random.normal(jax.random.fold_in(_rk, 11), (4, 16, 256), jnp.float32)
        _ctx_1024c = jax.random.dirichlet(jax.random.fold_in(_rk, 511), 0.3 * jnp.ones((16,), jnp.float32), (4, 1601))
        _ctx_1024t = jnp.einsum('bsk,bkd->bsd', _ctx_1024c, _ctx_1024P)
        _ctx_1024t = _ctx_1024t * jax.lax.rsqrt(jnp.mean(jnp.square(_ctx_1024t)) + 1e-12) * 0.953939
        ctx_1024 = 2.81802e-05 + 1.00001 * (_ctx_1024t + 0.3 * jax.random.normal(jax.random.fold_in(_rk, 611), (4, 1601, 256), jnp.float32))
        return (x, ctx_1024)
    x, ctx_1024 = _rec_inputs()

    def _L0_attn_setup():
        import jax, jax.numpy as jnp
        import numpy as np
        D_MODEL = 256
        D_STATE = 16
        EXPAND = 2
        D_CONV = 4
        D_INNER = EXPAND * D_MODEL
        BATCH = 1
        SEQLEN = 512
        key = jax.random.key(seed)
        ks = jax.random.split(key, 8)
        s = 0.02
        x = jax.random.normal(ks[0], (BATCH, SEQLEN, D_MODEL), jnp.float32)
        W_in = jax.random.normal(ks[1], (2 * D_INNER, D_MODEL), jnp.float32) * s
        conv_w = jax.random.normal(ks[2], (D_INNER, 1, D_CONV), jnp.float32) * s
        conv_b = jnp.zeros((D_INNER,), jnp.float32)
        A_log = jnp.log(jnp.tile(jnp.arange(1, D_STATE + 1, dtype=jnp.float32), (D_INNER, 1)))
        D_param = jnp.ones((D_INNER,), jnp.float32)
        W_x = jax.random.normal(ks[3], (2 * D_STATE, D_INNER), jnp.float32) * s
        W_dt = jax.random.normal(ks[4], (D_INNER, D_INNER), jnp.float32) * s
        b_dt = jnp.zeros((D_INNER,), jnp.float32)
        W_out = jax.random.normal(ks[5], (D_MODEL, D_INNER), jnp.float32) * s
        return {'x': x, 'W_in': W_in, 'conv_w': conv_w, 'conv_b': conv_b, 'A_log': A_log, 'D_param': D_param, 'W_x': W_x, 'W_dt': W_dt, 'b_dt': b_dt, 'W_out': W_out}
    _L0_attn_all = _L0_attn_setup()
    _L0_attn_in = {k: v for k, v in _L0_attn_all.items() if k in ('W_in', 'conv_w', 'conv_b', 'A_log', 'D_param', 'W_x', 'W_dt', 'b_dt', 'W_out')}
    del _L0_attn_all

    def _L0_xattn_setup():
        import jax, jax.numpy as jnp
        import numpy as np
        E = 256
        H = 16
        D = E // H
        key = jax.random.key(seed)
        ks = jax.random.split(key, 12)
        B, Tq, Tk = (2, 256, 2048)
        s = 0.02
        return {'hidden_states': jax.random.normal(ks[0], (B, Tq, E), jnp.float32), 'key_value_states': jax.random.normal(ks[1], (B, Tk, E), jnp.float32), 'Wq': jax.random.normal(ks[2], (E, E), jnp.float32) * s, 'bq': jnp.zeros((E,), jnp.float32), 'Wk': jax.random.normal(ks[3], (E, E), jnp.float32) * s, 'bk': jnp.zeros((E,), jnp.float32), 'Wv': jax.random.normal(ks[4], (E, E), jnp.float32) * s, 'bv': jnp.zeros((E,), jnp.float32), 'Wo': jax.random.normal(ks[5], (E, E), jnp.float32) * s, 'bo': jnp.zeros((E,), jnp.float32), 'stride': 16}
    _L0_xattn_all = _L0_xattn_setup()
    _L0_xattn_in = {k: v for k, v in _L0_xattn_all.items() if k in ('Wq', 'bq', 'Wk', 'bk', 'Wv', 'bv', 'Wo', 'bo')}
    del _L0_xattn_all

    def _L0_ffn_setup():
        import jax, jax.numpy as jnp
        import numpy as np
        H = 256
        I = 128
        E = 64
        G = 8
        TOPK_GROUP = 4
        K = 8
        I_SH = 256
        SCALE = 2.5

        def _route(x, router_w, e_bias):
            T = x.shape[0]
            scores = jax.nn.sigmoid(x.astype(jnp.float32) @ router_w.T.astype(jnp.float32))
            sfc = jax.lax.stop_gradient(scores) + e_bias[None, :]
            group_scores = jax.lax.top_k(sfc.reshape(T, G, E // G), 2)[0].sum(-1)
            _, gidx = jax.lax.top_k(group_scores, TOPK_GROUP)
            gmask = jax.nn.one_hot(gidx, G, dtype=sfc.dtype).sum(1)
            smask = jnp.repeat(gmask, E // G, axis=1)
            masked = jnp.where(smask > 0, sfc, 0.0)
            _, topk_idx = jax.lax.top_k(masked, K)
            w = jnp.take_along_axis(scores, topk_idx, axis=1)
            w = w / (w.sum(-1, keepdims=True) + 1e-20)
            return (topk_idx, w * SCALE)
        key = jax.random.key(seed)
        ks = jax.random.split(key, 9)
        s = 0.02
        return {'hidden_states': jax.random.normal(ks[0], (2, 256, H), jnp.float32), 'router_w': jax.random.normal(ks[1], (E, H), jnp.float32) * s, 'e_bias': jnp.zeros((E,), jnp.float32), 'Wg': jax.random.normal(ks[2], (E, H, I), jnp.float32) * s, 'Wu': jax.random.normal(ks[3], (E, H, I), jnp.float32) * s, 'Wd': jax.random.normal(ks[4], (E, I, H), jnp.float32) * s, 'SWg': jax.random.normal(ks[5], (H, I_SH), jnp.float32) * s, 'SWu': jax.random.normal(ks[6], (H, I_SH), jnp.float32) * s, 'SWd': jax.random.normal(ks[7], (I_SH, H), jnp.float32) * s}
    _L0_ffn_all = _L0_ffn_setup()
    _L0_ffn_in = {k: v for k, v in _L0_ffn_all.items() if k in ('router_w', 'e_bias', 'Wg', 'Wu', 'Wd', 'SWg', 'SWu', 'SWd')}
    del _L0_ffn_all

    def _L1_attn_setup():
        import jax, jax.numpy as jnp
        import numpy as np
        N_HEADS = 16
        MAX_LEN = 256
        key = jax.random.key(seed)
        ks = jax.random.split(key, 6)
        B, T, C = (4, 256, 256)
        scale = 0.02
        return {'x': jax.random.normal(ks[0], (B, T, C), dtype=jnp.float32), 'qkv_w': jax.random.normal(ks[1], (3 * C, C), dtype=jnp.float32) * scale, 'qkv_b': jax.random.normal(ks[2], (3 * C,), dtype=jnp.float32) * scale, 'proj_w': jax.random.normal(ks[3], (C, C), dtype=jnp.float32) * scale, 'proj_b': jax.random.normal(ks[4], (C,), dtype=jnp.float32) * scale, 'rel_pos_emb': jax.random.normal(ks[5], (2 * MAX_LEN - 1, C), dtype=jnp.float32) * scale}
    _L1_attn_all = _L1_attn_setup()
    _L1_attn_in = {k: v for k, v in _L1_attn_all.items() if k in ('qkv_w', 'qkv_b', 'proj_w', 'proj_b', 'rel_pos_emb')}
    del _L1_attn_all

    def _L1_xattn_setup():
        import jax, jax.numpy as jnp
        import numpy as np
        EMBED_DIM = 256
        N, L = (4, 1024)
        key = jax.random.key(seed)
        ks = jax.random.split(key, 9)
        s = 1.0 / np.sqrt(EMBED_DIM)
        return {'q': jax.random.normal(ks[0], (N, L, EMBED_DIM), jnp.float32), 'k': jax.random.normal(ks[1], (N, L, EMBED_DIM), jnp.float32), 'v': jax.random.normal(ks[2], (N, L, EMBED_DIM), jnp.float32), 'Wq': jax.random.normal(ks[3], (EMBED_DIM, EMBED_DIM), jnp.float32) * s, 'bq': jax.random.normal(ks[4], (EMBED_DIM,), jnp.float32) * s, 'Wk': jax.random.normal(ks[5], (EMBED_DIM, EMBED_DIM), jnp.float32) * s, 'bk': jax.random.normal(ks[6], (EMBED_DIM,), jnp.float32) * s, 'Wv': jax.random.normal(ks[7], (EMBED_DIM, EMBED_DIM), jnp.float32) * s, 'bv': jax.random.normal(ks[8], (EMBED_DIM,), jnp.float32) * s}
    _L1_xattn_all = _L1_xattn_setup()
    _L1_xattn_in = {k: v for k, v in _L1_xattn_all.items() if k in ('Wq', 'bq', 'Wk', 'bk', 'Wv', 'bv')}
    del _L1_xattn_all

    def _L1_ffn_setup():
        import jax, jax.numpy as jnp
        import numpy as np
        B, T, D = (2, 256, 256)
        H, DK, K = (8, 128, 8)
        NKEYS = 64
        NEXP = NKEYS * NKEYS

        def _rmsnorm(x, w, eps=1e-06):
            inv = jax.lax.rsqrt(jnp.mean(x * x, axis=-1, keepdims=True) + eps)
            return x * inv * w
        key = jax.random.key(seed)
        ks = jax.random.split(key, 5)
        return {'x': jax.random.normal(ks[0], (B, T, D), jnp.float32), 'w_q': jax.random.normal(ks[1], (H * 2 * DK, D), jnp.float32) * 0.02, 'keys': jax.random.normal(ks[2], (H, NKEYS, 2, DK), jnp.float32) * 0.02, 'expert_down': jax.random.normal(ks[3], (NEXP, D), jnp.float32) * 0.02, 'expert_up': jax.random.normal(ks[4], (NEXP, D), jnp.float32) * 0.02, 'norm_w': jnp.ones((D,), jnp.float32)}
    _L1_ffn_all = _L1_ffn_setup()
    _L1_ffn_in = {k: v for k, v in _L1_ffn_all.items() if k in ('w_q', 'keys', 'expert_down', 'expert_up', 'norm_w')}
    del _L1_ffn_all
    return {'x': x, 'ctx_1024': ctx_1024, 'L0_attn_W_in': _L0_attn_in['W_in'], 'L0_attn_conv_w': _L0_attn_in['conv_w'], 'L0_attn_conv_b': _L0_attn_in['conv_b'], 'L0_attn_A_log': _L0_attn_in['A_log'], 'L0_attn_D_param': _L0_attn_in['D_param'], 'L0_attn_W_x': _L0_attn_in['W_x'], 'L0_attn_W_dt': _L0_attn_in['W_dt'], 'L0_attn_b_dt': _L0_attn_in['b_dt'], 'L0_attn_W_out': _L0_attn_in['W_out'], 'L0_xattn_Wq': _L0_xattn_in['Wq'], 'L0_xattn_bq': _L0_xattn_in['bq'], 'L0_xattn_Wk': _L0_xattn_in['Wk'], 'L0_xattn_bk': _L0_xattn_in['bk'], 'L0_xattn_Wv': _L0_xattn_in['Wv'], 'L0_xattn_bv': _L0_xattn_in['bv'], 'L0_xattn_Wo': _L0_xattn_in['Wo'], 'L0_xattn_bo': _L0_xattn_in['bo'], 'L0_ffn_router_w': _L0_ffn_in['router_w'], 'L0_ffn_e_bias': _L0_ffn_in['e_bias'], 'L0_ffn_Wg': _L0_ffn_in['Wg'], 'L0_ffn_Wu': _L0_ffn_in['Wu'], 'L0_ffn_Wd': _L0_ffn_in['Wd'], 'L0_ffn_SWg': _L0_ffn_in['SWg'], 'L0_ffn_SWu': _L0_ffn_in['SWu'], 'L0_ffn_SWd': _L0_ffn_in['SWd'], 'L1_attn_qkv_w': _L1_attn_in['qkv_w'], 'L1_attn_qkv_b': _L1_attn_in['qkv_b'], 'L1_attn_proj_w': _L1_attn_in['proj_w'], 'L1_attn_proj_b': _L1_attn_in['proj_b'], 'L1_attn_rel_pos_emb': _L1_attn_in['rel_pos_emb'], 'L1_xattn_Wq': _L1_xattn_in['Wq'], 'L1_xattn_bq': _L1_xattn_in['bq'], 'L1_xattn_Wk': _L1_xattn_in['Wk'], 'L1_xattn_bk': _L1_xattn_in['bk'], 'L1_xattn_Wv': _L1_xattn_in['Wv'], 'L1_xattn_bv': _L1_xattn_in['bv'], 'L1_ffn_w_q': _L1_ffn_in['w_q'], 'L1_ffn_keys': _L1_ffn_in['keys'], 'L1_ffn_expert_down': _L1_ffn_in['expert_down'], 'L1_ffn_expert_up': _L1_ffn_in['expert_up'], 'L1_ffn_norm_w': _L1_ffn_in['norm_w']}

def reference(x, ctx_1024, L0_attn_W_in, L0_attn_conv_w, L0_attn_conv_b, L0_attn_A_log, L0_attn_D_param, L0_attn_W_x, L0_attn_W_dt, L0_attn_b_dt, L0_attn_W_out, L0_xattn_Wq, L0_xattn_bq, L0_xattn_Wk, L0_xattn_bk, L0_xattn_Wv, L0_xattn_bv, L0_xattn_Wo, L0_xattn_bo, L0_ffn_router_w, L0_ffn_e_bias, L0_ffn_Wg, L0_ffn_Wu, L0_ffn_Wd, L0_ffn_SWg, L0_ffn_SWu, L0_ffn_SWd, L1_attn_qkv_w, L1_attn_qkv_b, L1_attn_proj_w, L1_attn_proj_b, L1_attn_rel_pos_emb, L1_xattn_Wq, L1_xattn_bq, L1_xattn_Wk, L1_xattn_bk, L1_xattn_Wv, L1_xattn_bv, L1_ffn_w_q, L1_ffn_keys, L1_ffn_expert_down, L1_ffn_expert_up, L1_ffn_norm_w):
    import jax
    import jax.numpy as jnp

    def _L0_attn_ref(x, W_in, conv_w, conv_b, A_log, D_param, W_x, W_dt, b_dt, W_out):
        import jax, jax.numpy as jnp
        import numpy as np
        D_MODEL = 256
        D_STATE = 16
        EXPAND = 2
        D_CONV = 4
        D_INNER = EXPAND * D_MODEL
        BATCH = 1
        SEQLEN = 512
        B_, L, _ = x.shape
        xz = jnp.einsum('bld,ed->ble', x, W_in)
        x_inner, z = jnp.split(xz, 2, axis=-1)
        xc = jax.lax.conv_general_dilated(jnp.swapaxes(x_inner, 1, 2), conv_w, (1,), [(D_CONV - 1, 0)], feature_group_count=D_INNER, dimension_numbers=('NCH', 'OIH', 'NCH')) + conv_b[None, :, None]
        x_ssm = jnp.swapaxes(jax.nn.silu(xc), 1, 2)
        dt = jax.nn.softplus(jnp.einsum('ble,fe->blf', x_ssm, W_dt) + b_dt)
        x_dbl = jnp.einsum('ble,se->bls', x_ssm, W_x)
        B_mat, C_mat = jnp.split(x_dbl, 2, axis=-1)
        A = -jnp.exp(A_log)
        dA = jnp.exp(dt[..., None] * A)
        dBx = B_mat[:, :, None, :] * dt[..., None] * x_ssm[..., None]

        def step(h, inp):
            dA_t, dBx_t, C_t = inp
            h = dA_t * h + dBx_t
            y_t = jnp.einsum('bds,bs->bd', h, C_t)
            return (h, y_t)
        h0 = jnp.zeros((B_, D_INNER, D_STATE), x.dtype)
        _, ys = jax.lax.scan(step, h0, (jnp.swapaxes(dA, 0, 1), jnp.swapaxes(dBx, 0, 1), jnp.swapaxes(C_mat, 0, 1)))
        y = jnp.swapaxes(ys, 0, 1) + D_param * x_ssm
        y = y * jax.nn.silu(z)
        out = jnp.einsum('ble,de->bld', y, W_out)
        return out + x

    def _L0_xattn_ref(hidden_states, key_value_states, Wq, bq, Wk, bk, Wv, bv, Wo, bo, stride):
        import jax, jax.numpy as jnp
        import numpy as np
        E = 256
        H = 16
        D = E // H
        B, Tq, _ = hidden_states.shape
        Tk = key_value_states.shape[1]
        scaling = D ** (-0.5)
        Q = (hidden_states @ Wq.T + bq).reshape(B, Tq, H, D).transpose(0, 2, 1, 3)
        K = (key_value_states @ Wk.T + bk).reshape(B, Tk, H, D).transpose(0, 2, 1, 3)
        V = (key_value_states @ Wv.T + bv).reshape(B, Tk, H, D).transpose(0, 2, 1, 3)
        m = Tk // stride
        idx = jnp.arange(H)[:, None] + stride * jnp.arange(m)[None, :]
        gather = idx[None, :, :, None]
        Kg = jnp.take_along_axis(K, gather, axis=2)
        Vg = jnp.take_along_axis(V, gather, axis=2)
        scores = jnp.einsum('bhqd,bhkd->bhqk', Q, Kg) * scaling
        attn = jax.nn.softmax(scores, axis=-1)
        out = jnp.einsum('bhqk,bhkd->bhqd', attn, Vg)
        out = out.transpose(0, 2, 1, 3).reshape(B, Tq, E)
        return out @ Wo.T + bo

    def _L0_ffn_ref(hidden_states, router_w, e_bias, Wg, Wu, Wd, SWg, SWu, SWd):
        import jax, jax.numpy as jnp
        import numpy as np
        H = 256
        I = 128
        E = 64
        G = 8
        TOPK_GROUP = 4
        K = 8
        I_SH = 256
        SCALE = 2.5

        def _route(x, router_w, e_bias):
            T = x.shape[0]
            scores = jax.nn.sigmoid(x.astype(jnp.float32) @ router_w.T.astype(jnp.float32))
            sfc = jax.lax.stop_gradient(scores) + e_bias[None, :]
            group_scores = jax.lax.top_k(sfc.reshape(T, G, E // G), 2)[0].sum(-1)
            _, gidx = jax.lax.top_k(group_scores, TOPK_GROUP)
            gmask = jax.nn.one_hot(gidx, G, dtype=sfc.dtype).sum(1)
            smask = jnp.repeat(gmask, E // G, axis=1)
            masked = jnp.where(smask > 0, sfc, 0.0)
            _, topk_idx = jax.lax.top_k(masked, K)
            w = jnp.take_along_axis(scores, topk_idx, axis=1)
            w = w / (w.sum(-1, keepdims=True) + 1e-20)
            return (topk_idx, w * SCALE)
        orig_shape = hidden_states.shape
        x = hidden_states.reshape(-1, orig_shape[-1])
        T = x.shape[0]
        topk_idx, topk_w = _route(x, router_w, e_bias)
        coef = jnp.zeros((T, E), topk_w.dtype).at[jnp.arange(T)[:, None], topk_idx].add(topk_w)
        g = jnp.einsum('th,ehi->tei', x, Wg)
        u = jnp.einsum('th,ehi->tei', x, Wu)
        h = jax.nn.silu(g) * u * coef[:, :, None]
        moe_out = jnp.einsum('tei,eih->th', h, Wd)
        shared = jax.nn.silu(x @ SWg) * (x @ SWu) @ SWd
        return (moe_out + shared).reshape(orig_shape)

    def _L1_attn_ref(x, qkv_w, qkv_b, proj_w, proj_b, rel_pos_emb):
        import jax, jax.numpy as jnp
        import numpy as np
        N_HEADS = 16
        MAX_LEN = 256
        B, T, C = x.shape
        H = N_HEADS
        D = C // H
        qkv = (x @ qkv_w.T + qkv_b).reshape(B, T, 3, H, D)
        qkv = jnp.transpose(qkv, (2, 0, 3, 1, 4))
        q, k, v = (qkv[0], qkv[1], qkv[2])
        att = jnp.einsum('bhtd,bhsd->bhts', q, k) / np.sqrt(D).astype(np.float32)
        table = rel_pos_emb.reshape(2 * MAX_LEN - 1, H, D).sum(axis=-1)
        pos = jnp.arange(T)
        rel_idx = pos[:, None] - pos[None, :] + (MAX_LEN - 1)
        bias = jnp.transpose(table[rel_idx], (2, 0, 1))
        att = att + bias[None]
        causal = pos[None, :] > pos[:, None]
        att = jnp.where(causal[None, None], -jnp.inf, att)
        att = jax.nn.softmax(att, axis=-1)
        out = jnp.einsum('bhts,bhsd->bhtd', att, v)
        out = jnp.transpose(out, (0, 2, 1, 3)).reshape(B, T, C)
        return out @ proj_w.T + proj_b

    def _L1_xattn_ref(q, k, v, Wq, bq, Wk, bk, Wv, bv):
        import jax, jax.numpy as jnp
        import numpy as np
        EMBED_DIM = 256
        N, L = (4, 1024)
        scale = 1.0 / q.shape[-1] ** 0.5
        pq = jnp.einsum('nle,fe->nlf', q, Wq) + bq
        pk = jnp.einsum('nle,fe->nlf', k, Wk) + bk
        pv = jnp.einsum('nle,fe->nlf', v, Wv) + bv
        scores = jnp.einsum('nle,nme->nlm', pq, pk) * scale
        attn = jax.nn.softmax(scores, axis=-1)
        return jnp.einsum('nlm,nme->nle', attn, pv)

    def _L1_ffn_ref(x, w_q, keys, expert_down, expert_up, norm_w):
        import jax, jax.numpy as jnp
        import numpy as np
        B, T, D = (2, 256, 256)
        H, DK, K = (8, 128, 8)
        NKEYS = 64
        NEXP = NKEYS * NKEYS

        def _rmsnorm(x, w, eps=1e-06):
            inv = jax.lax.rsqrt(jnp.mean(x * x, axis=-1, keepdims=True) + eps)
            return x * inv * w
        b, t, d = x.shape
        xn = _rmsnorm(x, norm_w)
        q = (xn @ w_q.T).reshape(b, t, H, 2, DK)
        sim1 = jnp.einsum('bthd,hkd->bthk', q[..., 0, :], keys[:, :, 0, :])
        sim2 = jnp.einsum('bthd,hkd->bthk', q[..., 1, :], keys[:, :, 1, :])
        s1, i1 = jax.lax.top_k(sim1, K)
        s2, i2 = jax.lax.top_k(sim2, K)
        all_idx = (i1[..., :, None] * NKEYS + i2[..., None, :]).reshape(b, t, H, K * K)
        all_sc = (s1[..., :, None] + s2[..., None, :]).reshape(b, t, H, K * K)
        fs, pk = jax.lax.top_k(all_sc, K)
        fi = jnp.take_along_axis(all_idx, pk, axis=-1)
        wd = expert_down[fi]
        wu = expert_up[fi]
        hidden = jax.nn.gelu(jnp.einsum('btd,bthkd->bthk', xn, wd), approximate=False)
        hidden = hidden * jax.nn.relu(fs)
        return jnp.einsum('bthk,bthkd->btd', hidden, wu)
    x = x + _L0_attn_ref(_layernorm(x, axis=-1), L0_attn_W_in, L0_attn_conv_w, L0_attn_conv_b, L0_attn_A_log, L0_attn_D_param, L0_attn_W_x, L0_attn_W_dt, L0_attn_b_dt, L0_attn_W_out)
    x = x + _L0_xattn_ref(_layernorm(x, axis=-1), ctx_1024, L0_xattn_Wq, L0_xattn_bq, L0_xattn_Wk, L0_xattn_bk, L0_xattn_Wv, L0_xattn_bv, L0_xattn_Wo, L0_xattn_bo, 16)
    x = x + _L0_ffn_ref(_layernorm(x, axis=-1), L0_ffn_router_w, L0_ffn_e_bias, L0_ffn_Wg, L0_ffn_Wu, L0_ffn_Wd, L0_ffn_SWg, L0_ffn_SWu, L0_ffn_SWd)
    x = x + _L1_attn_ref(_layernorm(x, axis=-1), L1_attn_qkv_w, L1_attn_qkv_b, L1_attn_proj_w, L1_attn_proj_b, L1_attn_rel_pos_emb)
    x = x + _L1_xattn_ref(_layernorm(x, axis=-1), ctx_1024, ctx_1024, L1_xattn_Wq, L1_xattn_bq, L1_xattn_Wk, L1_xattn_bk, L1_xattn_Wv, L1_xattn_bv)
    x = x + _L1_ffn_ref(_layernorm(x, axis=-1), L1_ffn_w_q, L1_ffn_keys, L1_ffn_expert_down, L1_ffn_expert_up, L1_ffn_norm_w)
    return x

_drawn_inputs = setup_inputs


def setup_inputs(seed=0):
    import zlib

    import numpy as np

    out = dict(_drawn_inputs(seed))
    spreads = {'L0_attn_conv_b': (0.0, 0.8),
     'L0_attn_D_param': (1.0, 0.6),
     'L0_attn_b_dt': (0.0, 0.8),
     'L0_xattn_bq': (0.0, 2.0),
     'L0_xattn_bk': (0.0, 2.0),
     'L0_xattn_bv': (0.0, 1.851),
     'L0_xattn_bo': (0.0, 0.467),
     'L0_ffn_e_bias': (0.0, 0.8),
     'L1_ffn_norm_w': (1.0, 0.6)}
    factors = {'L0_attn_W_in': 8.0,
     'L0_attn_conv_w': 8.0,
     'L0_attn_A_log': 8.0,
     'L0_attn_W_x': 8.0,
     'L0_attn_W_dt': 8.0,
     'L0_attn_W_out': 8.0,
     'L0_xattn_Wq': 37.445,
     'L0_xattn_Wk': 32.684,
     'L0_ffn_router_w': 8.0,
     'L0_ffn_Wg': 8.0,
     'L0_ffn_Wu': 8.0,
     'L0_ffn_Wd': 8.0,
     'L0_ffn_SWg': 6.952,
     'L0_ffn_SWu': 6.865,
     'L0_ffn_SWd': 6.868,
     'L1_attn_qkv_w': 8.0,
     'L1_attn_qkv_b': 8.0,
     'L1_attn_proj_w': 7.458,
     'L1_attn_proj_b': 26.751,
     'L1_attn_rel_pos_emb': 8.0,
     'L1_xattn_bq': 42.045,
     'L1_xattn_bk': 200.0,
     'L1_ffn_w_q': 8.0,
     'L1_ffn_keys': 8.0,
     'L1_ffn_expert_down': 8.0,
     'L1_ffn_expert_up': 8.0,
     'L0_xattn_Wv': 3.944,
     'L0_xattn_Wo': 3.185,
     'L1_xattn_Wq': 3.552,
     'L1_xattn_Wk': 3.375,
     'L1_xattn_bv': 14.52}
    for name, (base, spread) in spreads.items():
        noise = np.random.default_rng([zlib.crc32(name.encode()), seed]).standard_normal(out[name].shape)
        drawn = base * np.exp(spread * noise) if base else spread * noise
        out[name] = jnp.asarray(drawn.astype(out[name].dtype))
    for name, factor in factors.items():
        out[name] = (out[name] * factor).astype(out[name].dtype)
    return out
```

```python
from contextlib import ExitStack

import concourse.bass as bass
from concourse import mybir

F32 = mybir.dt.float32
U32 = mybir.dt.uint32
ALU = mybir.AluOpType
ACT = mybir.ActivationFunctionType
AX = mybir.AxisListType
ds = bass.ds

P = 128
B, T, D = 4, 512, 256
QT = T // P
NT = B * QT
KC = D // P
BANK = 512
LN_EPS = 1e-5
DI, DS, DCONV = 512, 16, 4
DT = DI // P
SU = 8
H, DH = 16, 16
G = 4
STRIP = 32
CTX = 1601
STRIDE = 16
CK = CTX // STRIDE
NEG = -1.0e30

STAGES = ("ssm", "gather_attn", "moe", "self_attn", "cross_attn", "peer")


class Chain:

    def __init__(self, engine, sem):
        self.engine, self.sem, self.n = engine, sem, 0

    def __call__(self, instruction):
        self.n += 1
        instruction.then_inc(self.sem, 1)
        self.engine.wait_ge(self.sem, self.n)


class Core:

    def __init__(self, nc, ctx):
        self.nc, self.ctx = nc, ctx
        self.sems = {}
        self.x = ctx.enter_context(nc.sbuf_tensor("x_res", [P, NT, D], F32))
        self.ident = ctx.enter_context(nc.sbuf_tensor("ident", [P, P], F32))
        self.neg_half = ctx.enter_context(nc.sbuf_tensor("neg_half", [P, QT], F32))
        self.ps = ctx.enter_context(nc.psum_tensor("ps", [P, 8, BANK], F32))

    def sem(self, name):
        if name not in self.sems:
            self.sems[name] = self.ctx.enter_context(self.nc.semaphore(name))
        return self.sems[name]

    def fresh(self):
        nums = sorted(s.num for s in self.sems.values())
        lo, hi = nums[0], nums[-1] + 1
        assert nums == list(range(lo, hi))
        self.nc.vector.sem_clear(range(lo, hi))
        self.nc.all_engine_barrier()


def load_block(core, pairs):
    nc = core.nc
    loaded = core.sem("weights_loaded")
    loaded2 = core.sem("weights_loaded_act")
    with nc.Block() as block:
        @block.sync
        def _(sp):
            for out, in_ in pairs[0::2]:
                sp.dma_start(out, in_).then_inc(loaded, 16)
            sp.wait_ge(loaded, 16 * len(pairs[0::2]))

        @block.scalar
        def _(act):
            for out, in_ in pairs[1::2]:
                act.dma_start(out, in_).then_inc(loaded2, 16)
            if pairs[1::2]:
                act.wait_ge(loaded2, 16 * len(pairs[1::2]))
    core.fresh()


def norm_dve(core, dve, b, xn, stats, mv, rstd, keep_sum=False, extra=None):
    x = core.x
    chain = Chain(dve, core.sem("norm_chain"))
    for q in range(QT):
        last = dve.bn_stats(stats[:, q, :], x[:, ds(b * QT + q, 1), :])
    chain(last)
    for q in range(QT):
        last = dve.bn_aggr(mv[:, q, :], stats[:, q, :])
    chain(last)
    dve.tensor_scalar(rstd[:, :], mv[:, :, 1], LN_EPS, None, ALU.add).then_inc(core.sem("var_ready"), 1)
    dve.wait_ge(core.sem("rstd_ready"), 1)
    for q in range(QT):
        ins = dve.tensor_scalar(xn[:, q, :], x[:, ds(b * QT + q, 1), :], mv[:, q, 0:1], rstd[:, q:q + 1],
                                ALU.subtract, ALU.mult)
        if extra is None:
            ins.then_inc(core.sem("xn_ready"), 1)
    if extra is not None:
        chain(ins)
        extra(chain)
    elif keep_sum:
        dve.wait_ge(core.sem("xn_ready"), QT)
        xb = x[:, ds(b * QT, QT), :]
        dve.tensor_tensor(xb, xb, xn[:, :, :], ALU.add).then_inc(core.sem("x_plus_xn"), 1)


def norm_pool(core, pool, rstd):
    pool.wait_ge(core.sem("var_ready"), 1)
    pool.tensor_tensor(rstd[:, :], rstd[:, :], core.neg_half[:, :], ALU.pow)\
        .then_inc(core.sem("rstd_ready"), 1)


def norm_pe(core, pe, xn, banks=(0, 1)):
    for q in range(QT):
        pe.wait_ge(core.sem("xn_ready"), q + 1)
        for c in range(KC):
            last = pe.transpose(core.ps[:, banks[c], q * P:(q + 1) * P], xn[:, q, c * P:(c + 1) * P],
                                core.ident[:, :])
    last.then_inc(core.sem("xn_turned"), 1)


def norm_act(core, act, xT, banks=(0, 1)):
    act.wait_ge(core.sem("xn_turned"), 1)
    for c in range(KC):
        act.activation(xT[c], core.ps[:, banks[c], :], ACT.Copy).then_inc(core.sem("xT_ready"), 1)




def ssm_stage(core, w, scratch):
    nc = core.nc
    x, ps = core.x, core.ps
    with ExitStack() as ctx:
        def sb(name, shape, dt=F32):
            return ctx.enter_context(nc.sbuf_tensor("ssm_" + name, shape, dt))

        w_in = sb("w_in", [P, KC, 2 * DI])
        w_dt = sb("w_dt", [P, DT, DI])
        w_x = sb("w_x", [P, DT, 2 * DS])
        w_out = sb("w_out", [P, DT, D])
        conv_w = sb("conv_w", [P, DT, DCONV])
        conv_b = sb("conv_b", [P, DT])
        a_log = sb("a_log", [P, DT, DS])
        a_neg = sb("a_neg", [P, DT, DS])
        d_par = sb("d_par", [P, DT])
        b_dt = sb("b_dt", [P, DT])
        bc = sb("bc", [P, 2 * DS, T])
        dA = sb("dA", [P, 2, SU, T])
        hb = sb("hb", [P, 2, SU, T])
        xs = sb("xs", [P, DT, T])
        sz = sb("sz", [P, DT, T])
        dt = sb("dt", [P, DT, T])
        u = sb("u", [P, DT, T])
        xT = sb("xT", [P, KC, T])
        xdbl = sb("xdbl", [2 * DS, T])
        stats = sb("stats", [P, QT, 6])
        mv = sb("mv", [P, QT, 2])
        rstd = sb("rstd", [P, QT])
        xn = hb[:, 0, 0:2, :].rearrange("p a (c d) -> p (a c) d", d=D)

        soft = hb[:, 1, 0:DT, :]
        load_block(core, [
            (w_in[:, :, :], w["L0_attn_W_in_T"].rearrange("(c p) e -> p c e", p=P)),
            (w_dt[:, :, :], w["L0_attn_W_dt_T"].rearrange("(c p) f -> p c f", p=P)),
            (w_x[:, :, :], w["L0_attn_W_x_T"].rearrange("(c p) s -> p c s", p=P)),
            (w_out[:, :, :], w["L0_attn_W_out_T"].rearrange("(c p) d -> p c d", p=P)),
            (conv_w[:, :, :], w["L0_attn_conv_w"].rearrange("(c p) o k -> p c (o k)", p=P)),
            (conv_b[:, :], w["L0_attn_conv_b_cols"]),
            (a_log[:, :, :], w["L0_attn_A_log"].rearrange("(c p) s -> p c s", p=P)),
            (d_par[:, :], w["L0_attn_D_param_cols"]),
            (b_dt[:, :], w["L0_attn_b_dt_cols"]),
        ])
        a_exp = core.sem("a_exp")
        with nc.Block() as block:
            @block.scalar
            def _(act):
                act.activation(a_neg[:, :, :], a_log[:, :, :], ACT.Exp).then_inc(a_exp, 1)

            @block.vector
            def _(dve):
                dve.wait_ge(a_exp, 1)
                dve.tensor_scalar(a_neg[:, :, :], a_neg[:, :, :], -1.0, None, ALU.mult)
                dve.memset(dA[:, :, :, 0:1], 0.0)
        core.fresh()

        sem = core.sem
        NU = DT * DS // SU
        with nc.Fori(0, B) as b:
            with nc.Block() as block:
                @block.tensor
                def _(pe):
                    norm_pe(core, pe, xn)
                    pe.wait_ge(sem("xT_ready"), KC)
                    for e in range(2 * DT):
                        bank = 4 + e if e < DT else e - DT
                        for c in range(KC):
                            last = pe.matmul(ps[:, bank, :], w_in[:, c, e * P:(e + 1) * P], xT[:, c, :],
                                             start=(c == 0), stop=(c == KC - 1))
                        last.then_inc(sem("xz_ready"), 1)
                    pe.wait_ge(sem("xs_ready"), 1)
                    pe.wait_ge(sem("sz_ready"), 1)
                    for c in range(DT):
                        last = pe.matmul(ps[0:2 * DS, 0, :], w_x[:, c, :], xs[:, c, :],
                                         start=(c == 0), stop=(c == DT - 1))
                    last.then_inc(sem("bc_ready"), 1)
                    for f in range(DT):
                        for c in range(DT):
                            last = pe.matmul(ps[:, 4 + f, :], w_dt[:, c, f * P:(f + 1) * P], xs[:, c, :],
                                             start=(c == 0), stop=(c == DT - 1))
                        last.then_inc(sem("dt_ready"), 1)
                    pe.wait_ge(sem("xdbl_out"), 1)
                    for n in range(NU):
                        d, half = divmod(n, DS // SU)
                        pe.wait_ge(sem("hc_ready"), n + 1)
                        if half == 0 and d >= 2:
                            pe.wait_ge(sem("y_done"), d - 1)
                        for s in range(SU):
                            last = pe.matmul(ps[:, d % 2, :], core.ident[:, :], hb[:, n % 2, s, :],
                                             start=(half == 0 and s == 0),
                                             stop=(half == DS // SU - 1 and s == SU - 1))
                        last.then_inc(sem("hc_summed"), 1)
                    pe.wait_ge(sem("y_done"), DT)
                    for q in range(QT):
                        for c in range(DT):
                            last = pe.matmul(ps[:, 2 + q // 2, (q % 2) * D:(q % 2 + 1) * D],
                                             xs[:, c, q * P:(q + 1) * P], w_out[:, c, :],
                                             start=(c == 0), stop=(c == DT - 1))
                    last.then_inc(sem("out_ready"), 1)

                @block.scalar
                def _(act):
                    norm_act(core, act, [xT[:, c, :] for c in range(KC)])
                    act.wait_ge(sem("conv_done"), 1)
                    act.activation(xs[:, :, :], u[:, :, :], ACT.Silu).then_inc(sem("xs_ready"), 1)
                    act.wait_ge(sem("xz_ready"), 2 * DT)
                    act.activation(sz[:, :, :], ps[:, 0:DT, :], ACT.Silu).then_inc(sem("sz_ready"), 1)
                    act.wait_ge(sem("bc_ready"), 1)
                    act.activation(xdbl[:, :], ps[0:2 * DS, 0, :], ACT.Copy).then_inc(sem("xdbl_out"), 1)
                    chain = Chain(act, sem("act_chain"))
                    act.wait_ge(sem("z_ready"), 1)
                    chain(act.activation(soft, dt[:, :, :], ACT.Abs))
                    chain(act.activation(soft, soft, ACT.Exp, scale=-1.0))
                    act.activation(soft, soft, ACT.Ln, bias=1.0).then_inc(sem("ln_ready"), 1)
                    act.wait_ge(sem("u_ready"), 1)
                    for n in range(NU):
                        d, half = divmod(n, DS // SU)
                        if n >= 2:
                            act.wait_ge(sem("scanned"), n - 1)
                        for s in range(SU):
                            i = half * SU + s
                            last = act.activation(dA[:, n % 2, s, 1:T], dt[:, d, 1:T], ACT.Exp,
                                                  scale=a_neg[:, d, i:i + 1])
                        last.then_inc(sem("dA_ready"), 1)

                @block.sync
                def _(sp):
                    sp.wait_ge(sem("xdbl_out"), 1)
                    sp.dma_start(scratch[:, :], xdbl[:, :]).then_inc(sem("xdbl_stored"), 16)
                    sp.wait_ge(sem("xdbl_stored"), 16)
                    for j in range(4):
                        k = 2 * DS // 4
                        sp.dma_start(bc[:, j * k:(j + 1) * k, :],
                                     scratch[j * k:(j + 1) * k, :].partition_broadcast(P))\
                          .then_inc(sem("bc_loaded"), 16)

                @block.gpsimd
                def _(pool):
                    norm_pool(core, pool, rstd)
                    pool.wait_ge(sem("u_ready"), 1)
                    pool.wait_ge(sem("bc_loaded"), 64)
                    for n in range(NU):
                        d, half = divmod(n, DS // SU)
                        if n >= 2:
                            pool.wait_ge(sem("hc_summed"), n - 1)
                        pool.tensor_tensor(hb[:, n % 2, :, :],
                                           u[:, d, :].unsqueeze(1).broadcast_to([P, SU, T]),
                                           bc[:, half * SU:(half + 1) * SU, :], ALU.mult)\
                            .then_inc(sem("dBx_ready"), 1)

                @block.vector
                def _(dve):
                    norm_dve(core, dve, b, xn, stats, mv, rstd, keep_sum=True)
                    chain = Chain(dve, sem("dve_chain"))
                    for e in range(DT):
                        dve.wait_ge(sem("xz_ready"), e + 1)
                        chain(dve.tensor_scalar(u[:, e, :], ps[:, 4 + e, :], conv_w[:, e, DCONV - 1:DCONV],
                                                conv_b[:, e:e + 1], ALU.mult, ALU.add))
                        for k in range(1, DCONV):
                            ins = dve.scalar_tensor_tensor(
                                out=u[:, e, k:T], in0=ps[:, 4 + e, 0:T - k],
                                scalar=conv_w[:, e, DCONV - 1 - k:DCONV - k], in1=u[:, e, k:T],
                                op0=ALU.mult, op1=ALU.add)
                            if k < DCONV - 1:
                                chain(ins)
                    ins.then_inc(sem("conv_done"), 1)
                    dve.wait_ge(sem("xs_ready"), 1)
                    for f in range(DT):
                        dve.wait_ge(sem("dt_ready"), f + 1)
                        ins = dve.tensor_scalar(dt[:, f, :], ps[:, 4 + f, :], b_dt[:, f:f + 1], None, ALU.add)
                    ins.then_inc(sem("z_ready"), 1)
                    dve.wait_ge(sem("z_ready"), 1)
                    dve.wait_ge(sem("ln_ready"), 1)
                    chain(dve.scalar_tensor_tensor(out=dt[:, :, :], in0=dt[:, :, :], scalar=0.0,
                                                   in1=soft, op0=ALU.max, op1=ALU.add))
                    dve.tensor_tensor(u[:, :, :], dt[:, :, :], xs[:, :, :], ALU.mult)\
                        .then_inc(sem("u_ready"), 1)

                    def finish(d):
                        dve.wait_ge(sem("hc_summed"), (d + 1) * DS // SU)
                        chain(dve.scalar_tensor_tensor(out=xs[:, d, :], in0=xs[:, d, :],
                                                       scalar=d_par[:, d:d + 1], in1=ps[:, d % 2, :],
                                                       op0=ALU.mult, op1=ALU.add))
                        dve.tensor_tensor(xs[:, d, :], xs[:, d, :], sz[:, d, :], ALU.mult)\
                            .then_inc(sem("y_done"), 1)

                    dve.wait_ge(sem("u_ready"), 1)
                    for n in range(NU):
                        d, half = divmod(n, DS // SU)
                        dve.wait_ge(sem("dA_ready"), n + 1)
                        dve.wait_ge(sem("dBx_ready"), n + 1)
                        h = hb[:, n % 2, :, :]
                        hf = h.rearrange("p s t -> p (s t)")
                        dve.tensor_tensor_scan(hf, dA[:, n % 2, :, :].rearrange("p s t -> p (s t)"), hf,
                                               0.0, ALU.mult, ALU.add).then_inc(sem("scanned"), 1)
                        dve.wait_ge(sem("scanned"), n + 1)
                        dve.tensor_tensor(h, h, bc[:, DS + half * SU:DS + (half + 1) * SU, :], ALU.mult)\
                            .then_inc(sem("hc_ready"), 1)
                        if half == 0 and d >= 1:
                            finish(d - 1)
                    finish(DT - 1)
                    dve.wait_ge(sem("out_ready"), 1)
                    dve.wait_ge(sem("x_plus_xn"), 1)
                    xb = x[:, ds(b * QT, QT), :]
                    dve.tensor_tensor(xb, xb, ps[:, 2:4, :].rearrange("p a (c d) -> p (a c) d", d=D), ALU.add)
            core.fresh()




def add_bias_rows(core, dve, b, bias):
    dve.wait_ge(core.sem("xn_ready"), QT)
    xb = core.x[:, ds(b * QT, QT), :]
    dve.tensor_tensor(xb, xb, bias[:, :].unsqueeze(1).broadcast_to([P, QT, D]), ALU.add)\
        .then_inc(core.sem("bias_added"), 1)


def turn_heads_pe(core, pe, q, heads_out):
    pe.wait_ge(core.sem("heads_normed"), q + 1)
    if q:
        pe.wait_ge(core.sem("x_added"), q)
    for c in range(KC):
        last = pe.transpose(core.ps[:, 7, c * P:(c + 1) * P], heads_out[:, q % 2, c * P:(c + 1) * P],
                            core.ident[:, :])
    last.then_inc(core.sem("heads_turned"), 1)


def turn_heads_act(core, act, q, heads_T):
    act.wait_ge(core.sem("heads_turned"), q + 1)
    act.activation(heads_T[:, :, :], core.ps[:, 7, 0:D].rearrange("p (c t) -> p c t", c=KC), ACT.Copy)\
        .then_inc(core.sem("heads_T_ready"), 1)


def project_pe(core, pe, q, heads_T, w_o):
    pe.wait_ge(core.sem("heads_T_ready"), q + 1)
    for c in range(KC):
        last = pe.matmul(core.ps[:, 7, D:2 * D], heads_T[:, c, :], w_o[:, c, :],
                         start=(c == 0), stop=(c == KC - 1))
    last.then_inc(core.sem("projected"), 1)


def project_dve(core, dve, b, q):
    dve.wait_ge(core.sem("projected"), q + 1)
    if q == 0:
        dve.wait_ge(core.sem("bias_added"), 1)
    xq = core.x[:, ds(b * QT + q, 1), :]
    dve.tensor_tensor(xq, xq, core.ps[:, 7:8, D:2 * D], ALU.add).then_inc(core.sem("x_added"), 1)


def normalise_dve(core, dve, q, summed, den, heads_out):
    dve.wait_ge(core.sem("values_summed"), summed)
    if q >= 2:
        dve.wait_ge(core.sem("heads_turned"), q - 1)
    pv = core.ps[:, 6, 0:H * (DH + 1)].rearrange("p (h e) -> p h e", e=DH + 1)
    dve.reciprocal(den[:, :], pv[:, :, DH]).then_inc(core.sem("den_ready"), 1)
    dve.wait_ge(core.sem("den_ready"), q + 1)
    dve.tensor_tensor(heads_out[:, q % 2, :].rearrange("p (h e) -> p h e", e=DH), pv[:, :, 0:DH],
                      den[:, :].unsqueeze(2).broadcast_to([P, H, DH]), ALU.mult)\
        .then_inc(core.sem("heads_normed"), 1)




def gather_attn_stage(core, w):
    nc = core.nc
    ps, sem = core.ps, core.sem
    with ExitStack() as ctx:
        def sb(name, shape, dt=F32):
            return ctx.enter_context(nc.sbuf_tensor("ga_" + name, shape, dt))

        w_q = sb("w_q", [P, KC, G * P])
        w_k = sb("w_k", [P, KC, G * P])
        w_v = sb("w_v", [P, KC, D])
        w_o = sb("w_o", [P, KC, D])
        b_q = sb("b_q", [P, G])
        b_k = sb("b_k", [P, G])
        b_v = sb("b_v", [P, D])
        b_o = sb("b_o", [P, D])
        cT = sb("cT", [P, KC, CTX])
        xn = sb("xn", [P, QT, D])
        xT = sb("xT", [P, KC, T])
        qT = sb("qT", [P, G, T])
        kT = sb("kT", [P, G, CK])
        v = sb("v", [P, H, DH + 1])
        probs = sb("probs", [P, 2, H, CK])
        pT = sb("pT", [P, 2, H, P])
        top = sb("top", [P, 2, H])
        den = sb("den", [P, H])
        heads_out = sb("heads_out", [P, 2, D])
        heads_T = sb("heads_T", [P, KC, P])
        stats = sb("stats", [P, QT, 6])
        mv = sb("mv", [P, QT, 2])
        rstd = sb("rstd", [P, QT])

        load_block(core, [
            (w_q[:, :, :], w["L0_xattn_Wq_strips"].rearrange("(c p) e -> p c e", p=P)),
            (w_k[:, :, :], w["L0_xattn_Wk_strips"].rearrange("(c p) e -> p c e", p=P)),
            (w_v[:, :, :], w["L0_xattn_Wv_T"].rearrange("(c p) e -> p c e", p=P)),
            (w_o[:, :, :], w["L0_xattn_Wo_T"].rearrange("(c p) e -> p c e", p=P)),
            (b_q[:, :], w["L0_xattn_bq_strips"]),
            (b_k[:, :], w["L0_xattn_bk_strips"]),
            (b_v[:, :], w["L0_xattn_bv"].partition_broadcast(P)),
            (b_o[:, :], w["L0_xattn_bo"].partition_broadcast(P)),
        ])
        with nc.Block() as block:
            @block.vector
            def _(dve):
                dve.memset(v[:, :, DH:DH + 1], 1.0)
        core.fresh()

        with nc.Fori(0, B) as b:
            with nc.Block() as block:
                @block.sync
                def _(sp):
                    sp.dma_start(cT[:, :, :], w["ctx_T"][ds(b, 1), :, :]
                                 .rearrange("o (c p) k -> p (o c) k", p=P)).then_inc(sem("ctx_loaded"), 16)

                @block.tensor
                def _(pe):
                    pe.wait_ge(sem("ctx_loaded"), 16)
                    for h in range(H):
                        g, j = divmod(h, G)
                        rows = slice(h, h + STRIDE * (CK - 1) + 1, STRIDE)
                        for c in range(KC):
                            pe.matmul(ps[STRIP * j:STRIP * (j + 1), 2, g * CK:(g + 1) * CK],
                                      w_k[:, c, g * P + STRIP * j:g * P + STRIP * (j + 1)], cT[:, c, rows],
                                      start=(c == 0), stop=(c == KC - 1))
                        for c in range(KC):
                            last = pe.matmul(ps[0:CK, 3, h * DH:(h + 1) * DH], cT[:, c, rows],
                                             w_v[:, c, h * DH:(h + 1) * DH],
                                             start=(c == 0), stop=(c == KC - 1))
                    last.then_inc(sem("kv_ready"), 1)
                    norm_pe(core, pe, xn)
                    pe.wait_ge(sem("xT_ready"), KC)
                    for g in range(G):
                        for c in range(KC):
                            last = pe.matmul(ps[:, 4 + g, :], w_q[:, c, g * P:(g + 1) * P], xT[:, c, :],
                                             start=(c == 0), stop=(c == KC - 1))
                        last.then_inc(sem("q_ready"), 1)

                    def scores(q):
                        if q == 0:
                            pe.wait_ge(sem("k_stored"), 1)
                            pe.wait_ge(sem("v_stored"), 1)
                            pe.wait_ge(sem("q_stored"), G)
                        else:
                            pe.wait_ge(sem("scores_read"), q)
                        for g in range(G):
                            for j in range(G):
                                s = slice(STRIP * j, STRIP * (j + 1))
                                last = pe.matmul(ps[:, j, g * CK:(g + 1) * CK], qT[s, g, q * P:(q + 1) * P],
                                                 kT[s, g, :], start=True, stop=True)
                        last.then_inc(sem("scores_ready"), 1)

                    scores(0)
                    for q in range(QT):
                        pe.wait_ge(sem("probs_ready"), q + 1)
                        for j in range(G):
                            out_read = sem("pT_act") if j % 2 == 0 else sem("pT_dve")
                            if 2 * q + j // 2:
                                pe.wait_ge(out_read, 2 * q + j // 2)
                            for g in range(G):
                                last = pe.transpose(ps[0:CK, 4 + j % 2, g * P:(g + 1) * P],
                                                    probs[:, q % 2, j * G + g, :], core.ident[:, :])
                            last.then_inc(sem("p_turned"), 1)
                        if q + 1 < QT:
                            scores(q + 1)
                        pe.wait_ge(sem("pT_act"), 2 * q + 2)
                        pe.wait_ge(sem("pT_dve"), 2 * q + 2)
                        if q:
                            pe.wait_ge(sem("heads_normed"), q)
                        for h in range(H):
                            g, j = divmod(h, G)
                            last = pe.matmul(ps[:, 6, h * (DH + 1):(h + 1) * (DH + 1)],
                                             pT[0:CK, q % 2, j * G + g, :], v[0:CK, h, :], start=True, stop=True)
                        last.then_inc(sem("values_summed"), 1)
                        turn_heads_pe(core, pe, q, heads_out)
                        project_pe(core, pe, q, heads_T, w_o)

                @block.scalar
                def _(act):
                    norm_act(core, act, [xT[:, c, :] for c in range(KC)])
                    for g in range(G):
                        act.wait_ge(sem("q_ready"), g + 1)
                        act.activation(qT[:, g, :], ps[:, 4 + g, :], ACT.Identity, bias=b_q[:, g:g + 1])\
                            .then_inc(sem("q_stored"), 1)
                    for q in range(QT):
                        act.wait_ge(sem("scores_read"), q + 1)
                        pq = probs[:, q % 2, :, :]
                        act.activation(pq, pq, ACT.Exp, scale=DH ** -0.5).then_inc(sem("probs_ready"), 1)
                        for j in (0, 2):
                            act.wait_ge(sem("p_turned"), G * q + j + 1)
                            if q >= 2:
                                act.wait_ge(sem("values_summed"), q - 1)
                            act.activation(pT[0:CK, q % 2, j * G:(j + 1) * G, :],
                                           ps[0:CK, 4, :].rearrange("k (g t) -> k g t", g=G), ACT.Copy)\
                                .then_inc(sem("pT_act"), 1)
                        turn_heads_act(core, act, q, heads_T)

                @block.gpsimd
                def _(pool):
                    norm_pool(core, pool, rstd)

                @block.vector
                def _(dve):
                    norm_dve(core, dve, b, xn, stats, mv, rstd)
                    add_bias_rows(core, dve, b, b_o)
                    dve.wait_ge(sem("kv_ready"), 1)
                    dve.tensor_tensor(kT[:, :, :], ps[:, 2, 0:G * CK].rearrange("p (g k) -> p g k", g=G),
                                      b_k[:, :].unsqueeze(2).broadcast_to([P, G, CK]), ALU.add)\
                        .then_inc(sem("k_stored"), 1)
                    dve.tensor_tensor(v[0:CK, :, 0:DH], ps[0:CK, 3, 0:D].rearrange("k (h e) -> k h e", e=DH),
                                      b_v[0:CK, :].rearrange("k (h e) -> k h e", e=DH), ALU.add)\
                        .then_inc(sem("v_stored"), 1)

                    def subtract_top(q):
                        dve.wait_ge(sem("scores_ready"), q + 1)
                        if q >= 2:
                            dve.wait_ge(sem("p_turned"), G * (q - 1))
                        s = ps[:, 0:G, 0:G * CK].rearrange("p j (g k) -> p j g k", g=G)
                        t = top[:, q % 2, :].rearrange("p (j g) -> p j g", g=G)
                        dve.tensor_reduce(t, s, AX.X, ALU.max).then_inc(sem("top_ready"), 1)
                        dve.wait_ge(sem("top_ready"), q + 1)
                        dve.tensor_tensor(probs[:, q % 2, :, :].rearrange("p (j g) k -> p j g k", g=G), s,
                                          t.unsqueeze(3).broadcast_to([P, G, G, CK]), ALU.subtract)\
                            .then_inc(sem("scores_read"), 1)

                    subtract_top(0)
                    for q in range(QT):
                        for j in (1, 3):
                            dve.wait_ge(sem("p_turned"), G * q + j + 1)
                            if q >= 2:
                                dve.wait_ge(sem("values_summed"), q - 1)
                            dve.tensor_copy(pT[0:CK, q % 2, j * G:(j + 1) * G, :],
                                            ps[0:CK, 5, :].rearrange("k (g t) -> k g t", g=G))\
                                .then_inc(sem("pT_dve"), 1)
                        if q + 1 < QT:
                            subtract_top(q + 1)
                        normalise_dve(core, dve, q, q + 1, den, heads_out)
                        project_dve(core, dve, b, q)
            core.fresh()



REL = 511
RELK = 256
SLAB = 640


def self_attn_stage(core, w, scratch):
    nc = core.nc
    ps, sem = core.ps, core.sem
    with ExitStack() as ctx:
        def sb(name, shape, dt=F32):
            return ctx.enter_context(nc.sbuf_tensor("sa_" + name, shape, dt))

        w_q = sb("w_q", [P, KC, G * P])
        w_k = sb("w_k", [P, KC, G * P])
        w_v = sb("w_v", [P, KC, D])
        w_o = sb("w_o", [P, KC, D])
        b_q = sb("b_q", [P, G])
        b_qn = sb("b_qn", [P, G])
        b_k = sb("b_k", [P, G])
        b_v = sb("b_v", [P, D])
        b_o = sb("b_o", [P, D])
        emb = sb("emb", [P, RELK // P, H, DH])
        tab = sb("tab", [P, RELK // P, H])
        rows = sb("rows", [H, SLAB])
        slab = sb("slab", [P, H, T])
        flipped = sb("flipped", [P, H, T])
        flip = sb("flip", [P, P])
        xn = sb("xn", [P, QT, D])
        xT = sb("xT", [P, KC, T])
        qT = sb("qT", [P, G, T])
        kT = sb("kT", [P, G, T])
        v = sb("v", [P, QT, H, DH + 1])
        probs = sb("probs", [P, 4, T])
        pT = sb("pT", [P, 4, T])
        top = sb("top", [P, 4])
        den = sb("den", [P, H])
        heads_out = sb("heads_out", [P, 2, D])
        heads_T = sb("heads_T", [P, KC, P])
        stats = sb("stats", [P, QT, 6])
        mv = sb("mv", [P, QT, 2])
        rstd = sb("rstd", [P, QT])

        load_block(core, [
            (emb[:, :, :, :], w["L1_attn_rel_back"].rearrange("(a p) (h e) -> p a h e", p=P, e=DH)),
            (flip[:, :], w["flip"]),
            (w_q[:, :, :], w["L1_attn_Wq_strips"].rearrange("(c p) e -> p c e", p=P)),
            (w_k[:, :, :], w["L1_attn_Wk_strips"].rearrange("(c p) e -> p c e", p=P)),
            (w_v[:, :, :], w["L1_attn_Wv_T"].rearrange("(c p) e -> p c e", p=P)),
            (w_o[:, :, :], w["L1_attn_proj_w_T"].rearrange("(c p) e -> p c e", p=P)),
            (b_q[:, :], w["L1_attn_bq_strips"]),
            (b_k[:, :], w["L1_attn_bk_strips"]),
            (b_v[:, :], w["L1_attn_bv"].partition_broadcast(P)),
            (b_o[:, :], w["L1_attn_proj_b"].partition_broadcast(P)),
        ])
        with nc.Block() as block:
            @block.vector
            def _(dve):
                dve.memset(v[:, :, :, DH:DH + 1], 1.0)
                dve.tensor_scalar(b_qn[:, :], b_q[:, :], -DH ** -0.5, None, ALU.mult)
                dve.tensor_reduce(tab[:, :, :], emb[:, :, :, :], AX.X, ALU.add).then_inc(sem("tab_ready"), 1)
                dve.memset(rows[:, T:SLAB], -NEG)
                dve.wait_ge(sem("tab_turned"), 1)
                dve.tensor_scalar(rows[:, T - RELK:T], ps[0:H, 0, 0:RELK], -1.0, None, ALU.mult)
                dve.tensor_scalar(rows[:, 0:T - RELK],
                                  ps[0:H, 0, 0:1].broadcast_to([H, T - RELK]), -1.0, None, ALU.mult)\
                    .then_inc(sem("rows_ready"), 1)

            @block.tensor
            def _(pe):
                pe.wait_ge(sem("tab_ready"), 1)
                for a in range(RELK // P):
                    last = pe.transpose(ps[0:H, 0, a * P:(a + 1) * P], tab[:, a, :], core.ident[:, :])
                last.then_inc(sem("tab_turned"), 1)
                pe.wait_ge(sem("slab_loaded"), 16)
                for h in range(H):
                    if h >= 6:
                        pe.wait_ge(sem("slab_ready"), h - 5)
                    pe.matmul(ps[:, 1 + h % 6, :], flip[:, :], flipped[:, h, :], start=True, stop=True)\
                      .then_inc(sem("slab_flipped"), 1)

            @block.scalar
            def _(act):
                for h in range(H):
                    act.wait_ge(sem("slab_flipped"), h + 1)
                    act.activation(slab[:, h, :], ps[:, 1 + h % 6, :], ACT.Copy).then_inc(sem("slab_ready"), 1)

            @block.sync
            def _(sp):
                sp.wait_ge(sem("rows_ready"), 1)
                sp.dma_start(scratch, rows[:, :]).then_inc(sem("rows_stored"), 16)
                sp.wait_ge(sem("rows_stored"), 16)
                sp.dma_start(flipped[:, :, :], bass.AP(scratch.tensor, scratch.offset,
                                                       [[1, P], [SLAB, H], [1, T]]))\
                  .then_inc(sem("slab_loaded"), 16)
                sp.wait_ge(sem("slab_loaded"), 16)
        core.fresh()

        NU = QT * H
        with nc.Fori(0, B) as b:
            with nc.Block() as block:
                @block.tensor
                def _(pe):
                    norm_pe(core, pe, xn)
                    pe.wait_ge(sem("xT_ready"), KC)
                    for g in range(G):
                        for c in range(KC):
                            last = pe.matmul(ps[:, 4 + g, :], w_q[:, c, g * P:(g + 1) * P], xT[:, c, :],
                                             start=(c == 0), stop=(c == KC - 1))
                        last.then_inc(sem("q_ready"), 1)
                    for g in range(G):
                        for c in range(KC):
                            last = pe.matmul(ps[:, g, :], w_k[:, c, g * P:(g + 1) * P], xT[:, c, :],
                                             start=(c == 0), stop=(c == KC - 1))
                        last.then_inc(sem("k_ready"), 1)
                    pe.wait_ge(sem("q_stored"), G)
                    for q in range(QT):
                        for c in range(KC):
                            last = pe.matmul(ps[:, 4 + q // 2, (q % 2) * D:(q % 2 + 1) * D],
                                             xT[:, c, q * P:(q + 1) * P], w_v[:, c, :],
                                             start=(c == 0), stop=(c == KC - 1))
                    last.then_inc(sem("v_ready"), 1)
                    pe.wait_ge(sem("k_stored"), G)

                    for n in range(NU + 8):
                        if n < NU:
                            q, h = divmod(n, H)
                            g, j = divmod(h, G)
                            if n >= 4:
                                pe.wait_ge(sem("scores_read"), n - 3)
                            s = slice(STRIP * j, STRIP * (j + 1))
                            pe.matmul(ps[:, j, 0:(q + 1) * P], qT[s, g, q * P:(q + 1) * P],
                                      kT[s, g, 0:(q + 1) * P], start=True, stop=True)\
                              .then_inc(sem("scores_ready"), 1)
                        if n == 0:
                            pe.wait_ge(sem("v_stored"), 1)
                        m = n - 2
                        if 0 <= m < NU:
                            pe.wait_ge(sem("probs_ready"), m + 1)
                            if m >= 2:
                                pe.wait_ge(sem("pT_act") if m % 2 == 0 else sem("pT_dve"), m // 2)
                            for k in range(m // H + 1):
                                last = pe.transpose(ps[:, 4 + m % 2, k * P:(k + 1) * P],
                                                    probs[:, m % 4, k * P:(k + 1) * P], core.ident[:, :])
                            last.then_inc(sem("p_turned"), 1)
                        m = n - 3
                        if 0 <= m < NU:
                            q, h = divmod(m, H)
                            pe.wait_ge(sem("pT_act") if m % 2 == 0 else sem("pT_dve"), m // 2 + 1)
                            if h == 0 and q:
                                pe.wait_ge(sem("heads_normed"), q)
                            for k in range(q + 1):
                                last = pe.matmul(ps[:, 6, h * (DH + 1):(h + 1) * (DH + 1)],
                                                 pT[:, m % 4, k * P:(k + 1) * P], v[:, k, h, :],
                                                 start=(k == 0), stop=(k == q))
                            last.then_inc(sem("values_summed"), 1)
                        if n - 5 >= 0 and (n - 5) % H == H - 1:
                            turn_heads_pe(core, pe, (n - 5) // H, heads_out)
                        if n - 7 >= 0 and (n - 7) % H == H - 1:
                            project_pe(core, pe, (n - 7) // H, heads_T, w_o)

                @block.scalar
                def _(act):
                    norm_act(core, act, [xT[:, c, :] for c in range(KC)])
                    for g in range(G):
                        act.wait_ge(sem("q_ready"), g + 1)
                        act.activation(qT[:, g, :], ps[:, 4 + g, :], ACT.Identity, bias=b_qn[:, g:g + 1],
                                       scale=-DH ** -0.5).then_inc(sem("q_stored"), 1)
                    for g in range(G):
                        act.wait_ge(sem("k_ready"), g + 1)
                        act.activation(kT[:, g, :], ps[:, g, :], ACT.Identity, bias=b_k[:, g:g + 1])\
                            .then_inc(sem("k_stored"), 1)
                    for n in range(NU + 7):
                        if n < NU:
                            nk = (n // H + 1) * P
                            act.wait_ge(sem("scores_read"), n + 1)
                            pn = probs[:, n % 4, 0:nk]
                            act.activation(pn, pn, ACT.Exp, bias=top[:, n % 4:n % 4 + 1], scale=-1.0)\
                                .then_inc(sem("probs_ready"), 1)
                        m = n - 2
                        if 0 <= m < NU and m % 2 == 0:
                            nk = (m // H + 1) * P
                            act.wait_ge(sem("p_turned"), m + 1)
                            if m >= 4:
                                act.wait_ge(sem("values_summed"), m - 3)
                            act.activation(pT[:, m % 4, 0:nk], ps[:, 4, 0:nk], ACT.Copy)\
                                .then_inc(sem("pT_act"), 1)
                        if n - 6 >= 0 and (n - 6) % H == H - 1:
                            turn_heads_act(core, act, (n - 6) // H, heads_T)

                @block.gpsimd
                def _(pool):
                    norm_pool(core, pool, rstd)

                @block.vector
                def _(dve):
                    norm_dve(core, dve, b, xn, stats, mv, rstd)
                    add_bias_rows(core, dve, b, b_o)
                    dve.wait_ge(sem("v_ready"), 1)
                    dve.tensor_tensor(v[:, :, :, 0:DH],
                                      ps[:, 4:6, :].rearrange("p a (c h e) -> p (a c) h e", c=2, e=DH),
                                      b_v[:, :].rearrange("p (h e) -> p h e", e=DH).unsqueeze(1)
                                      .broadcast_to([P, QT, H, DH]), ALU.add).then_inc(sem("v_stored"), 1)
                    for n in range(NU + 9):
                        if n < NU:
                            q, h = divmod(n, H)
                            nk = (q + 1) * P
                            dve.wait_ge(sem("scores_ready"), n + 1)
                            if n >= 4:
                                dve.wait_ge(sem("p_turned"), n - 3)
                            dve.tensor_tensor_reduce(probs[:, n % 4, 0:nk], ps[:, h % G, 0:nk],
                                                     slab[:, h, T - nk:T], 1.0, -NEG, ALU.add, ALU.min,
                                                     top[:, n % 4:n % 4 + 1]).then_inc(sem("scores_read"), 1)
                        m = n - 2
                        if 0 <= m < NU and m % 2 == 1:
                            nk = (m // H + 1) * P
                            dve.wait_ge(sem("p_turned"), m + 1)
                            if m >= 4:
                                dve.wait_ge(sem("values_summed"), m - 3)
                            dve.tensor_copy(pT[:, m % 4, 0:nk], ps[:, 5, 0:nk]).then_inc(sem("pT_dve"), 1)
                        if n - 4 >= 0 and (n - 4) % H == H - 1:
                            normalise_dve(core, dve, (n - 4) // H, n - 3, den, heads_out)
                        if n - 8 >= 0 and (n - 8) % H == H - 1:
                            project_dve(core, dve, b, (n - 8) // H)
            core.fresh()



CKT = (CTX + P - 1) // P
CLAST = CTX - (CKT - 1) * P


def key_rows(k):
    return P if k < CKT - 1 else CLAST


def cross_attn_stage(core, w):
    nc = core.nc
    ps, sem = core.ps, core.sem
    x = core.x
    with ExitStack() as ctx:
        def sb(name, shape, dt=F32):
            return ctx.enter_context(nc.sbuf_tensor("ca_" + name, shape, dt))

        w_q = sb("w_q", [P, KC, D])
        w_k = sb("w_k", [P, KC, D])
        w_v = sb("w_v", [P, KC, D])
        b_q = sb("b_q", [P, KC])
        b_k = sb("b_k", [P, KC])
        b_v = sb("b_v", [P, D])
        cT = sb("cT", [P, KC, CTX])
        kT = sb("kT", [P, KC, CTX])
        v = sb("v", [P, CKT, D])
        xn = sb("xn", [P, QT, D])
        xT = sb("xT", [P, KC, T])
        qT = sb("qT", [P, KC, T])
        probs = sb("probs", [P, 2, CTX])
        pT = sb("pT", [P, 2, CKT, P])
        top = sb("top", [P, 2])
        bar = sb("bar", [P, 2])
        den = sb("den", [P, 2])
        rden = sb("rden", [P, 2])
        stats = sb("stats", [P, QT, 6])
        mv = sb("mv", [P, QT, 2])
        rstd = sb("rstd", [P, QT])

        load_block(core, [
            (w_q[:, :, :], w["L1_xattn_Wq_T"].rearrange("(c p) e -> p c e", p=P)),
            (w_k[:, :, :], w["L1_xattn_Wk_T"].rearrange("(c p) e -> p c e", p=P)),
            (w_v[:, :, :], w["L1_xattn_Wv_T"].rearrange("(c p) e -> p c e", p=P)),
            (b_q[:, :], w["L1_xattn_bq_cols"]),
            (b_k[:, :], w["L1_xattn_bk_cols"]),
            (b_v[:, :], w["L1_xattn_bv"].partition_broadcast(P)),
        ])
        SCALE = D ** -0.5
        cuts = [(s, min(BANK, CTX - s)) for s in range(0, CTX, BANK)]
        NG = (CKT + 3) // 4
        with nc.Fori(0, B) as b:
            with nc.Block() as block:
                @block.sync
                def _(sp):
                    sp.dma_start(cT[:, :, :], w["ctx_T"][ds(b, 1), :, :]
                                 .rearrange("o (c p) k -> p (o c) k", p=P)).then_inc(sem("ctx_loaded"), 16)

                @block.tensor
                def _(pe):
                    pe.wait_ge(sem("ctx_loaded"), 16)
                    for n in range(KC * len(cuts)):
                        f, r = divmod(n, len(cuts))
                        s, k = cuts[r]
                        if n >= 4:
                            pe.wait_ge(sem("k_stored"), n - 3)
                        for c in range(KC):
                            last = pe.matmul(ps[:, 2 + n % 4, 0:k], w_k[:, c, f * P:(f + 1) * P],
                                             cT[:, c, s:s + k], start=(c == 0), stop=(c == KC - 1))
                        last.then_inc(sem("k_ready"), 1)
                    for k in range(CKT):
                        if k >= 2:
                            pe.wait_ge(sem("v_stored"), k - 1)
                        for c in range(KC):
                            last = pe.matmul(ps[0:key_rows(k), 6 + k % 2, 0:D],
                                             cT[:, c, k * P:k * P + key_rows(k)], w_v[:, c, :],
                                             start=(c == 0), stop=(c == KC - 1))
                        last.then_inc(sem("v_ready"), 1)
                    norm_pe(core, pe, xn)
                    pe.wait_ge(sem("xT_ready"), KC)
                    pe.wait_ge(sem("k_stored"), KC * len(cuts))
                    for f in range(KC):
                        for c in range(KC):
                            last = pe.matmul(ps[:, 4 + f, :], w_q[:, c, f * P:(f + 1) * P], xT[:, c, :],
                                             start=(c == 0), stop=(c == KC - 1))
                        last.then_inc(sem("q_ready"), 1)

                    def scores(q):
                        if q:
                            pe.wait_ge(sem("probs_ready"), q)
                        else:
                            pe.wait_ge(sem("q_stored"), KC)
                        for c in range(KC):
                            for r, (s, k) in enumerate(cuts):
                                last = pe.matmul(ps[:, r, 0:k], qT[:, c, q * P:(q + 1) * P],
                                                 kT[:, c, s:s + k], start=(c == 0), stop=(c == KC - 1))
                        last.then_inc(sem("scores_ready"), 1)

                    scores(0)
                    for q in range(QT):
                        pe.wait_ge(sem("probs_ready"), q + 1)
                        for g in range(NG):
                            if 2 * q + g // 2:
                                pe.wait_ge(sem("pT_act") if g % 2 == 0 else sem("pT_dve"), 2 * q + g // 2)
                            for k in range(4 * g, min(4 * g + 4, CKT)):
                                last = pe.transpose(ps[0:key_rows(k), 4 + g % 2, (k % 4) * P:(k % 4 + 1) * P],
                                                    probs[:, q % 2, k * P:k * P + key_rows(k)],
                                                    core.ident[:, :])
                            last.then_inc(sem("p_turned"), 1)
                        if q + 1 < QT:
                            scores(q + 1)
                        pe.wait_ge(sem("pT_act"), 2 * q + 2)
                        pe.wait_ge(sem("pT_dve"), 2 * q + 2)
                        if q == 0:
                            pe.wait_ge(sem("v_stored"), CKT)
                        else:
                            pe.wait_ge(sem("x_added"), q)
                        for k in range(CKT):
                            n = key_rows(k)
                            last = pe.matmul(ps[:, 6, 0:D], pT[0:n, q % 2, k, :], v[0:n, k, :],
                                             start=(k == 0), stop=(k == CKT - 1))
                        last.then_inc(sem("values_summed"), 1)

                @block.scalar
                def _(act):
                    for n in range(KC * len(cuts)):
                        f, r = divmod(n, len(cuts))
                        s, k = cuts[r]
                        act.wait_ge(sem("k_ready"), n + 1)
                        act.activation(kT[:, f, s:s + k], ps[:, 2 + n % 4, 0:k], ACT.Identity,
                                       bias=b_k[:, f:f + 1]).then_inc(sem("k_stored"), 1)
                    norm_act(core, act, [xT[:, c, :] for c in range(KC)])
                    for f in range(KC):
                        act.wait_ge(sem("q_ready"), f + 1)
                        act.activation(qT[:, f, :], ps[:, 4 + f, :], ACT.Identity, bias=b_q[:, f:f + 1])\
                            .then_inc(sem("q_stored"), 1)
                    for q in range(QT):
                        act.wait_ge(sem("top_ready"), q + 1)
                        if q >= 2:
                            act.wait_ge(sem("p_turned"), NG * (q - 1))
                        act.activation(probs[:, q % 2, :], ps[:, 0:4, :].rearrange("p r k -> p (r k)")[:, 0:CTX],
                                       ACT.Exp, bias=bar[:, q % 2:q % 2 + 1], scale=SCALE,
                                       accum_out=den[:, q % 2:q % 2 + 1]).then_inc(sem("probs_ready"), 1)
                        for g in (0, 2):
                            act.wait_ge(sem("p_turned"), NG * q + g + 1)
                            if q >= 2:
                                act.wait_ge(sem("values_summed"), q - 1)
                            act.activation(pT[:, q % 2, 4 * g:4 * g + 4, :],
                                           ps[:, 4, :].rearrange("k (g t) -> k g t", t=P), ACT.Copy)\
                                .then_inc(sem("pT_act"), 1)

                @block.gpsimd
                def _(pool):
                    norm_pool(core, pool, rstd)

                @block.vector
                def _(dve):
                    norm_dve(core, dve, b, xn, stats, mv, rstd)
                    for k in range(CKT):
                        n = key_rows(k)
                        dve.wait_ge(sem("v_ready"), k + 1)
                        dve.tensor_tensor(v[0:n, k, :], ps[0:n, 6 + k % 2, 0:D], b_v[0:n, :], ALU.add)\
                            .then_inc(sem("v_stored"), 1)

                    def largest(q):
                        dve.wait_ge(sem("scores_ready"), q + 1)
                        dve.tensor_reduce(top[:, q % 2:q % 2 + 1],
                                          ps[:, 0:4, :].rearrange("p r k -> p (r k)")[:, 0:CTX],
                                          AX.X, ALU.max).then_inc(sem("max_found"), 1)
                        dve.wait_ge(sem("max_found"), q + 1)
                        dve.tensor_scalar(bar[:, q % 2:q % 2 + 1], top[:, q % 2:q % 2 + 1], -SCALE, None,
                                          ALU.mult).then_inc(sem("top_ready"), 1)

                    largest(0)
                    for q in range(QT):
                        for g in (1, 3):
                            kt = 4 * g
                            dve.wait_ge(sem("p_turned"), NG * q + g + 1)
                            if q >= 2:
                                dve.wait_ge(sem("values_summed"), q - 1)
                            if kt + 4 <= CKT:
                                ins = dve.tensor_copy(pT[:, q % 2, kt:kt + 4, :],
                                                      ps[:, 5, :].rearrange("k (g t) -> k g t", t=P))
                            else:
                                ins = dve.tensor_copy(pT[0:CLAST, q % 2, kt, :], ps[0:CLAST, 5, 0:P])
                            ins.then_inc(sem("pT_dve"), 1)
                        if q + 1 < QT:
                            largest(q + 1)
                        dve.wait_ge(sem("probs_ready"), q + 1)
                        dve.reciprocal(rden[:, q % 2:q % 2 + 1], den[:, q % 2:q % 2 + 1])\
                            .then_inc(sem("den_ready"), 1)
                        dve.wait_ge(sem("den_ready"), q + 1)
                        dve.wait_ge(sem("values_summed"), q + 1)
                        xq = x[:, ds(b * QT + q, 1), :]
                        dve.scalar_tensor_tensor(out=xq, in0=ps[:, 6:7, 0:D], scalar=rden[:, q % 2:q % 2 + 1],
                                                 in1=xq, op0=ALU.mult, op1=ALU.add)\
                            .then_inc(sem("x_added"), 1)
            core.fresh()



NE = 64
FF = 128
NSH = 2
EG, EPG = 8, 8
TOPG, TOPE = 4, 8
ROUTE_SCALE = 2.5
EL = 8
HALF = B * T // 2
EW = 2 * KC * FF + D


def moe_stage(core, w, coef_rows):
    nc = core.nc
    ps, sem = core.ps, core.sem
    with ExitStack() as ctx:
        def sb(name, shape, dt=F32):
            return ctx.enter_context(nc.sbuf_tensor("moe_" + name, shape, dt))

        router = sb("router", [P, KC, NE])
        e_bias = sb("e_bias", [P, NE])
        earlier = sb("earlier", [P, EG, EG])
        slots = sb("slots", [P, EL, EW])
        coef = sb("coef", [P, EL, HALF])
        xT_all = sb("xT_all", [P, KC, B * T])
        xTh = sb("xTh", [P, KC, HALF])
        ones = sb("ones", [NSH, B * T])

        load_block(core, [
            (router[:, :, :], w["L0_ffn_router_T"].rearrange("(c p) e -> p c e", p=P)),
            (e_bias[:, :], w["L0_ffn_e_bias"].partition_broadcast(P)),
            (earlier[:, :, :], w["earlier"].partition_broadcast(P)),
        ])

        with ExitStack() as inner:
            def sb2(name, shape, dt=F32):
                return inner.enter_context(nc.sbuf_tensor("rt_" + name, shape, dt))

            xn = sb2("xn", [P, QT, D])
            xT = sb2("xT", [P, KC, T])
            score = sb2("score", [P, QT, NE])
            biased = sb2("biased", [P, QT, NE])
            best = sb2("best", [P, QT, EG, 8])
            gsum = sb2("gsum", [P, QT, EG])
            above = sb2("above", [P, QT, EG, EG])
            equal = sb2("equal", [P, QT, EG, EG])
            rank = sb2("rank", [P, QT, EG])
            top = sb2("top", [P, QT, 8])
            marked = sb2("marked", [P, QT, NE])
            total = sb2("total", [P, QT])
            coef_T = sb2("coef_T", [NE, T])
            stats = sb2("stats", [P, QT, 6])
            mv = sb2("mv", [P, QT, 2])
            rstd = sb2("rstd", [P, QT])
            with nc.Fori(0, B) as b:
                with nc.Block() as block:
                    @block.tensor
                    def _(pe):
                        norm_pe(core, pe, xn)
                        pe.wait_ge(sem("xT_ready"), KC)
                        for q in range(QT):
                            for c in range(KC):
                                last = pe.matmul(ps[:, 2, q * NE:(q + 1) * NE], xT[:, c, q * P:(q + 1) * P],
                                                 router[:, c, :], start=(c == 0), stop=(c == KC - 1))
                        last.then_inc(sem("logits_ready"), 1)
                        pe.wait_ge(sem("coef_ready"), 1)
                        for q in range(QT):
                            last = pe.transpose(ps[0:NE, 3, q * P:(q + 1) * P], marked[:, q, :],
                                                core.ident[:, :])
                        last.then_inc(sem("coef_turned"), 1)

                    @block.scalar
                    def _(act):
                        norm_act(core, act, [xT[:, c, :] for c in range(KC)])
                        act.wait_ge(sem("logits_ready"), 1)
                        act.activation(score[:, :, :], ps[:, 2, 0:QT * NE].rearrange("p (q e) -> p q e", e=NE),
                                       ACT.Sigmoid).then_inc(sem("score_ready"), 1)
                        act.wait_ge(sem("coef_turned"), 1)
                        act.activation(coef_T[:, :], ps[0:NE, 3, :], ACT.Copy).then_inc(sem("coef_T_ready"), 1)

                    @block.gpsimd
                    def _(pool):
                        norm_pool(core, pool, rstd)
                        pool.wait_ge(sem("xT_ready"), KC)
                        pool.tensor_copy(xT_all[:, :, ds(b * T, T)], xT[:, :, :])

                    @block.sync
                    def _(sp):
                        sp.wait_ge(sem("coef_T_ready"), 1)
                        sp.dma_start(coef_rows[0:NE, ds(b * T, T)], coef_T[:, :]).then_inc(sem("coef_stored"), 16)
                        sp.wait_ge(sem("coef_stored"), 16)

                    @block.vector
                    def _(dve):
                        norm_dve(core, dve, b, xn, stats, mv, rstd)
                        chain = Chain(dve, sem("dve_chain"))
                        dve.wait_ge(sem("score_ready"), 1)
                        chain(dve.tensor_tensor(biased[:, :, :], score[:, :, :],
                                                e_bias[:, :].unsqueeze(1).broadcast_to([P, QT, NE]), ALU.add))
                        for q in range(QT):
                            for g in range(EG):
                                last = dve.max(best[:, q, g, :], biased[:, q, g * EPG:(g + 1) * EPG])
                        chain(last)
                        chain(dve.tensor_tensor(gsum[:, :, :], best[:, :, :, 0], best[:, :, :, 1], ALU.add))
                        mine = gsum[:, :, :].unsqueeze(3).broadcast_to([P, QT, EG, EG])
                        theirs = gsum[:, :, :].unsqueeze(2).broadcast_to([P, QT, EG, EG])
                        dve.tensor_tensor(above[:, :, :, :], theirs, mine, ALU.is_gt)
                        chain(dve.tensor_tensor(equal[:, :, :, :], theirs, mine, ALU.is_equal))
                        chain(dve.tensor_tensor(equal[:, :, :, :], equal[:, :, :, :],
                                                earlier[:, :, :].unsqueeze(1).broadcast_to([P, QT, EG, EG]),
                                                ALU.mult))
                        chain(dve.tensor_tensor(above[:, :, :, :], above[:, :, :, :], equal[:, :, :, :], ALU.add))
                        chain(dve.tensor_reduce(rank[:, :, :], above[:, :, :, :], AX.X, ALU.add))
                        chain(dve.tensor_scalar(rank[:, :, :], rank[:, :, :], TOPG - 0.5, None, ALU.is_lt))
                        chain(dve.tensor_tensor(biased[:, :, :].rearrange("p q (g e) -> p q g e", e=EPG),
                                                biased[:, :, :].rearrange("p q (g e) -> p q g e", e=EPG),
                                                rank[:, :, :].unsqueeze(3).broadcast_to([P, QT, EG, EPG]),
                                                ALU.mult))
                        for q in range(QT):
                            last = dve.max(top[:, q, :], biased[:, q, :])
                        chain(last)
                        for q in range(QT):
                            last = dve.match_replace(marked[:, q, :], top[:, q, :], biased[:, q, :], NEG)
                        chain(last)
                        chain(dve.tensor_tensor(marked[:, :, :], marked[:, :, :], biased[:, :, :], ALU.not_equal))
                        chain(dve.tensor_tensor(marked[:, :, :], marked[:, :, :], score[:, :, :], ALU.mult))
                        chain(dve.tensor_reduce(total[:, :], marked[:, :, :], AX.X, ALU.add))
                        chain(dve.tensor_scalar(total[:, :], total[:, :], 1e-20, None, ALU.add))
                        chain(dve.reciprocal(total[:, :], total[:, :]))
                        chain(dve.tensor_tensor(marked[:, :, :], marked[:, :, :],
                                                total[:, :].unsqueeze(2).broadcast_to([P, QT, NE]), ALU.mult))
                        dve.tensor_scalar(marked[:, :, :], marked[:, :, :], ROUTE_SCALE, None, ALU.mult)\
                            .then_inc(sem("coef_ready"), 1)
                core.fresh()

        gate = sb("gate", [P, 2, T])
        prod = sb("prod", [P, 2, T])
        hid = sb("hid", [P, 2, T])
        experts = w["L0_ffn_experts"]
        KEEP = EL - 2

        def load_slot(sp, half, e, slot, loaded):
            sp.dma_start(slots[:, slot:slot + 1, :], experts[ds(e, 1), :, :].rearrange("o p n -> p o n"))\
              .then_inc(loaded, 16)
            row = bass.AP(coef_rows.tensor, coef_rows.offset, [[0, P], [B * T, NE + EL], [1, B * T]])
            sp.dma_start(coef[:, slot:slot + 1, :], row[:, ds(e, 1), ds(half * HALF, HALF)])\
              .then_inc(loaded, 16)

        def expert_block(half, step, n_experts, shared, x_half):
            units = [(e, t) for e in range(n_experts) for t in range(HALF // T)]
            with nc.Block() as block:
                @block.sync
                def _(sp):
                    if shared:
                        return
                    for e in range(KEEP, EL):
                        load_slot(sp, half, step * EL + e, e, sem("late_loaded"))
                    for e in range(KEEP):
                        sp.wait_ge(sem("unit_done"), (e + 1) * (HALF // T))
                        load_slot(sp, half, step * EL + (EL + e), e, sem("next_loaded"))
                    sp.wait_ge(sem("next_loaded"), 32 * KEEP)

                @block.tensor
                def _(pe):
                    def down(m):
                        e, t = units[m]
                        pe.wait_ge(sem("hid_ready"), m + 1)
                        for q in range(QT):
                            i = t * QT + q
                            last = pe.matmul(ps[:, i // 2, (i % 2) * D:(i % 2 + 1) * D],
                                             hid[:, m % 2, q * P:(q + 1) * P], slots[:, e, 2 * KC * FF:EW],
                                             start=False, stop=False, skip_group_check=True)
                        last.then_inc(sem("unit_done"), 1)

                    for m, (e, t) in enumerate(units):
                        if e >= KEEP and t == 0:
                            pe.wait_ge(sem("late_loaded"), 32 * (EL - KEEP))
                        for i in range(2):
                            if m >= 2:
                                pe.wait_ge(sem("gate_ready") if i == 0 else sem("prod_ready"), m - 1)
                            for c in range(KC):
                                last = pe.matmul(ps[:, 4 + 2 * (m % 2) + i, :],
                                                 slots[:, e, (i * KC + c) * FF:(i * KC + c + 1) * FF],
                                                 x_half[:, c, t * T:(t + 1) * T],
                                                 start=(c == 0), stop=(c == KC - 1))
                            last.then_inc(sem("g_ready") if i == 0 else sem("u_ready"), 1)
                        if m:
                            down(m - 1)
                    down(len(units) - 1)

                @block.scalar
                def _(act):
                    for m in range(len(units)):
                        act.wait_ge(sem("g_ready"), m + 1)
                        if m >= 2:
                            act.wait_ge(sem("prod_ready"), m - 1)
                        act.activation(gate[:, m % 2, :], ps[:, 4 + 2 * (m % 2), :], ACT.Silu)\
                            .then_inc(sem("gate_ready"), 1)

                @block.vector
                def _(dve):
                    for m in range(len(units)):
                        dve.wait_ge(sem("u_ready"), m + 1)
                        dve.wait_ge(sem("gate_ready"), m + 1)
                        out = hid if shared else prod
                        if m >= 2:
                            dve.wait_ge(sem("unit_done") if shared else sem("hid_ready"), m - 1)
                        ins = dve.tensor_tensor(out[:, m % 2, :], gate[:, m % 2, :],
                                                ps[:, 5 + 2 * (m % 2), :], ALU.mult)
                        ins.then_inc(sem("prod_ready"), 1)
                        if shared:
                            dve.wait_ge(sem("prod_ready"), m + 1)
                            dve.sem_inc(sem("hid_ready"), 1)

                @block.gpsimd
                def _(pool):
                    if shared:
                        return
                    for m, (e, t) in enumerate(units):
                        if e >= KEEP and t == 0:
                            pool.wait_ge(sem("late_loaded"), 32 * (EL - KEEP))
                        pool.wait_ge(sem("prod_ready"), m + 1)
                        if m >= 2:
                            pool.wait_ge(sem("unit_done"), m - 1)
                        pool.tensor_tensor(hid[:, m % 2, :], prod[:, m % 2, :],
                                           coef[:, e, t * T:(t + 1) * T], ALU.mult)\
                            .then_inc(sem("hid_ready"), 1)
            core.fresh()

        with nc.Block() as block:
            @block.vector
            def _(dve):
                dve.memset(ones[:, :], 1.0).then_inc(sem("ones_set"), 1)

            @block.sync
            def _(sp):
                sp.wait_ge(sem("ones_set"), 1)
                for e in range(NE, NE + EL, NSH):
                    sp.dma_start(coef_rows[e:e + NSH, :], ones[:, :]).then_inc(sem("ones_stored"), 16)
                sp.wait_ge(sem("ones_stored"), 16 * EL // NSH)
        core.fresh()

        with nc.Fori(0, 2) as half:
            with nc.Block() as block:
                @block.sync
                def _(sp):
                    for e in range(KEEP):
                        load_slot(sp, half, e, e, sem("next_loaded"))
                    sp.wait_ge(sem("next_loaded"), 32 * KEEP)

                @block.vector
                def _(dve):
                    dve.memset(ps[:, 0:4, :], 0.0)
                    dve.tensor_copy(xTh[:, :, :], xT_all[:, :, ds(half * HALF, HALF)])
            core.fresh()
            with nc.Fori(0, NE // EL) as step:
                expert_block(half, step, EL, False, xTh)
            expert_block(half, None, NSH, True, xTh)
            with nc.Block() as block:
                @block.vector
                def _(dve):
                    xh = core.x[:, ds(half * (NT // 2), NT // 2), :]
                    dve.tensor_tensor(xh, xh, ps[:, 0:4, :].rearrange("p a (c d) -> p (a c) d", d=D), ALU.add)
            core.fresh()



PH = 8
NK = 64
DK = 128
PK = 8
NSLOT = PH * PK
ET = NK * NK // P
RMS_EPS = 1e-6
HT = T // 2
CG = 16


def peer_stage(core, w):
    nc = core.nc
    ps, sem = core.ps, core.sem
    with ExitStack() as ctx:
        def sb(name, shape, dt=F32):
            return ctx.enter_context(nc.sbuf_tensor("pr_" + name, shape, dt))

        w_q = sb("w_q", [P, KC, 2 * PH * DK])
        keys = sb("keys", [P, 2 * PH, NK])
        down = sb("down", [P, KC, ET, P])
        up = sb("up", [P, ET, D])
        norm_w = sb("norm_w", [P, D])
        iota = sb("iota", [P, P])
        act_h = sb("act_h", [P, ET, HT])
        hot = sb("hot", [P, NK * (P + ET)])
        hot_part = hot[:, 0:NK * P].rearrange("p (t k) -> p t k", k=P)
        hot_tile = hot[:, NK * P:].rearrange("p (t k) -> p t k", k=ET)
        xT = sb("xT", [P, KC, T])
        turned = sb("turned", [P, 3, QT, NK])
        key1 = sb("key1", [P, NSLOT])
        key2 = sb("key2", [P, NSLOT])
        upper = sb("upper", [P, NSLOT])
        lists = sb("lists", [P, 3, NSLOT])
        twice = sb("twice", [P, 3, 2, NSLOT])
        s8 = sb("s8", [P, PH, 2, PK])
        i8 = sb("i8", [P, PH, 2, PK], U32)
        i8f = sb("i8f", [P, PH, 2, PK])
        sums = sb("sums", [P, PH, PK * PK])
        f8 = sb("f8", [P, PH, PK])
        pk = sb("pk", [P, PH, PK], U32)
        ab = sb("ab", [P, 2, NSLOT], U32)
        abf = sb("abf", [P, 2, NSLOT])
        pick = sb("pick", [P, NSLOT, PK])
        stats = sb("stats", [P, QT, 6])
        mv = sb("mv", [P, QT, 2])
        rstd = sb("rstd", [P, QT])
        ssq = sb("ssq", [P, QT])
        xn = act_h[:, 0:4, :].rearrange("p a t -> p (a t)").rearrange("p (q d) -> p q d", d=D)
        sims = act_h[:, 8:16, :].rearrange("p a t -> p (a t)").rearrange("p (s k) -> p s k", s=2)
        qT = hot[:, 0:2 * PH * T].rearrange("p (s t) -> p s t", t=T)

        load_block(core, [
            (w_q[:, :, :], w["L1_ffn_w_q_T"].rearrange("(c p) e -> p c e", p=P)),
            (keys[:, :, :], w["L1_ffn_keys_T"]),
            (down[:, :, :, :], w["L1_ffn_down_T"].rearrange("(c p) (i e) -> p c i e", p=P, e=P)),
            (up[:, :, :], w["L1_ffn_up"]),
            (norm_w[:, :], w["L1_ffn_norm_w"].partition_broadcast(P)),
            (iota[:, :], w["iota"].partition_broadcast(P)),
        ])

        def rms(dve, chain):
            for q in range(QT):
                last = dve.tensor_tensor_reduce(xT[:, 0, 0:D], xn[:, q, :], xn[:, q, :], 1.0, 0.0,
                                                ALU.mult, ALU.add, ssq[:, q:q + 1])
                chain(last)
            dve.tensor_scalar(ssq[:, :], ssq[:, :], 1.0 / D, RMS_EPS, ALU.mult, ALU.add)\
                .then_inc(sem("ssq_ready"), 1)
            dve.wait_ge(sem("rms_ready"), 1)
            for q in range(QT):
                dve.scalar_tensor_tensor(out=xn[:, q, :], in0=xn[:, q, :], scalar=ssq[:, q:q + 1],
                                         in1=norm_w[:, :], op0=ALU.mult, op1=ALU.mult)\
                    .then_inc(sem("xn_ready"), 1)

        NQ = 2 * PH
        NG = HT // CG
        with nc.Fori(0, B) as b:
            with nc.Block() as block:
                @block.tensor
                def _(pe):
                    norm_pe(core, pe, xn)
                    pe.wait_ge(sem("xT_ready"), KC)
                    for s in range(NQ):
                        if s >= 4:
                            pe.wait_ge(sem("q_stored"), s - 3)
                        for c in range(KC):
                            last = pe.matmul(ps[:, s % 4, :], w_q[:, c, s * DK:(s + 1) * DK], xT[:, c, :],
                                             start=(c == 0), stop=(c == KC - 1))
                        last.then_inc(sem("q_ready"), 1)
                    pe.wait_ge(sem("q_stored"), NQ)
                    for q in range(QT):
                        if q >= 2:
                            pe.wait_ge(sem("sims_stored"), q - 1)
                        for s in range(NQ):
                            last = pe.matmul(ps[:, 4 + 2 * (q % 2) + s // 8, (s % 8) * NK:(s % 8 + 1) * NK],
                                             qT[:, s, q * P:(q + 1) * P], keys[:, s, :],
                                             start=True, stop=True)
                        last.then_inc(sem("sims_ready"), 1)
                    for q in range(QT):
                        pe.wait_ge(sem("lists_ready"), q + 1)
                        if q:
                            pe.wait_ge(sem("turned_stored"), 2 * q)
                        for i in range(3):
                            last = pe.transpose(ps[:, 0, i * P:(i + 1) * P],
                                                twice[:, i, :, :].rearrange("p a s -> p (a s)"),
                                                core.ident[:, :])
                        last.then_inc(sem("lists_turned"), 1)
                    for hf in range(2):
                        if hf:
                            pe.wait_ge(sem("x_added"), hf)
                        for n in range(ET // 2):
                            m = hf * (ET // 2) + n
                            if m >= 2:
                                pe.wait_ge(sem("gelu_done"), m - 1)
                            for i in range(2):
                                for c in range(KC):
                                    last = pe.matmul(ps[:, 1 + 6 * (n % 2), i * HT:(i + 1) * HT],
                                                     down[:, c, 2 * n + i, :], xT[:, c, hf * HT:(hf + 1) * HT],
                                                     start=(c == 0), stop=(c == KC - 1))
                            last.then_inc(sem("down_ready"), 1)
                        for g in range(NG):
                            m = hf * NG + g
                            if g % (NG // 2) == 0:
                                pe.wait_ge(sem("hot_part_ready"), 2 * hf + g // (NG // 2) + 1)
                                pe.wait_ge(sem("hot_tile_ready"), 2 * hf + g // (NG // 2) + 1)
                            if m >= 2:
                                pe.wait_ge(sem("weighted"), m - 1)
                            for t in range(CG):
                                tok = (g * CG + t) % P
                                s = slice(NK * (tok // NK), NK * (tok // NK + 1))
                                last = pe.matmul(ps[:, 2 + m % 2, t * ET:(t + 1) * ET],
                                                 hot_part[s, tok % NK, :], hot_tile[s, tok % NK, :],
                                                 start=True, stop=True)
                            last.then_inc(sem("outer_ready"), 1)
                        pe.wait_ge(sem("weighted"), (hf + 1) * NG)
                        for q in range(2):
                            for i in range(ET):
                                last = pe.matmul(ps[:, 6, q * D:(q + 1) * D], act_h[:, i, q * P:(q + 1) * P],
                                                 up[:, i, :], start=(i == 0), stop=(i == ET - 1))
                        last.then_inc(sem("up_ready"), 1)

                @block.scalar
                def _(act):
                    norm_act(core, act, [xT[:, c, :] for c in range(KC)])
                    for s in range(NQ):
                        act.wait_ge(sem("q_ready"), s + 1)
                        act.activation(qT[:, s, :], ps[:, s % 4, :], ACT.Copy).then_inc(sem("q_stored"), 1)
                    for q in range(QT):
                        act.wait_ge(sem("sims_ready"), q + 1)
                        if q >= 2:
                            act.wait_ge(sem("sims_used"), q - 1)
                        act.activation(sims[:, q % 2, :].rearrange("p (a k) -> p a k", a=2),
                                       ps[:, 4 + 2 * (q % 2):6 + 2 * (q % 2), :], ACT.Copy)\
                            .then_inc(sem("sims_stored"), 1)
                    for q in range(QT):
                        act.wait_ge(sem("lists_turned"), q + 1)
                        for a in range(2):
                            s = slice(NK * a, NK * (a + 1))
                            act.activation(turned[s, :, q, :],
                                           ps[s, 0, 0:3 * P].rearrange("p (i t) -> p i t", i=3)[:, :, s],
                                           ACT.Copy).then_inc(sem("turned_stored"), 1)
                    for hf in range(2):
                        for n in range(ET // 2):
                            if n == 0:
                                act.wait_ge(sem("sims_used"), QT)
                                if hf:
                                    act.wait_ge(sem("up_ready"), hf)
                            act.wait_ge(sem("down_ready"), hf * (ET // 2) + n + 1)
                            act.activation(act_h[:, 2 * n:2 * n + 2, :],
                                           ps[:, 1 + 6 * (n % 2), :].rearrange("p (i t) -> p i t", i=2), ACT.Gelu)\
                                .then_inc(sem("gelu_done"), 1)

                @block.gpsimd
                def _(pool):
                    norm_pool(core, pool, rstd)
                    pool.wait_ge(sem("ssq_ready"), 1)
                    pool.tensor_tensor(ssq[:, :], ssq[:, :], core.neg_half[:, :], ALU.pow)\
                        .then_inc(sem("rms_ready"), 1)
                    for q in range(QT):
                        pool.wait_ge(sem("hot_tiles"), q + 1)
                        pool.tensor_tensor(hot_tile, hot_tile,
                                           turned[:, 2, q, :].unsqueeze(2).broadcast_to([P, NK, ET]),
                                           ALU.mult).then_inc(sem("hot_tile_ready"), 1)

                @block.vector
                def _(dve):
                    norm_dve(core, dve, b, xn, stats, mv, rstd, extra=lambda chain: rms(dve, chain))
                    chain = Chain(dve, sem("dve_chain"))
                    for q in range(QT):
                        dve.wait_ge(sem("sims_stored"), q + 1)
                        sim = sims[:, q % 2, :].rearrange("p (h a k) -> p h a k", h=PH, a=2)
                        for h in range(PH):
                            for a in range(2):
                                last = dve.max(s8[:, h, a, :], sim[:, h, a, :])
                        chain(last)
                        for h in range(PH):
                            for a in range(2):
                                last = dve.max_index(i8[:, h, a, :], s8[:, h, a, :], sim[:, h, a, :])
                        last.then_inc(sem("sims_used"), 1)
                        dve.wait_ge(sem("sims_used"), q + 1)
                        dve.tensor_copy(i8f[:, :, :, :], i8[:, :, :, :])
                        chain(dve.tensor_tensor(
                            sums[:, :, :].rearrange("p h (a b) -> p h a b", a=PK),
                            s8[:, :, 0, :].unsqueeze(3).broadcast_to([P, PH, PK, PK]),
                            s8[:, :, 1, :].unsqueeze(2).broadcast_to([P, PH, PK, PK]), ALU.add))
                        for h in range(PH):
                            last = dve.max(f8[:, h, :], sums[:, h, :])
                        chain(last)
                        for h in range(PH):
                            last = dve.max_index(pk[:, h, :], f8[:, h, :], sums[:, h, :])
                        chain(last)
                        pkf = pk[:, :, :].rearrange("p h k -> p (h k)")
                        dve.tensor_scalar(ab[:, 0, :], pkf, 3, None, ALU.logical_shift_right)
                        chain(dve.tensor_scalar(ab[:, 1, :], pkf, PK - 1, None, ALU.bitwise_and))
                        chain(dve.tensor_copy(abf[:, :, :], ab[:, :, :]))
                        for a in range(2):
                            chain(dve.tensor_tensor(pick[:, :, :],
                                                    abf[:, a, :].unsqueeze(2).broadcast_to([P, NSLOT, PK]),
                                                    iota[:, 0:PK].unsqueeze(1).broadcast_to([P, NSLOT, PK]),
                                                    ALU.is_equal))
                            p4 = pick[:, :, :].rearrange("p (h k) a -> p h k a", h=PH)
                            chain(dve.tensor_tensor(p4, p4, i8f[:, :, a, :].unsqueeze(2)
                                                    .broadcast_to([P, PH, PK, PK]), ALU.mult))
                            chain(dve.tensor_reduce((key1, key2)[a][:, :], pick[:, :, :], AX.X, ALU.add))
                        chain(dve.tensor_scalar(upper[:, :], key1[:, :], ET - 0.5, None, ALU.is_ge))
                        dve.scalar_tensor_tensor(out=lists[:, 0, :], in0=upper[:, :], scalar=float(NK),
                                                 in1=key2[:, :], op0=ALU.mult, op1=ALU.add)
                        chain(dve.scalar_tensor_tensor(out=lists[:, 1, :], in0=upper[:, :], scalar=-float(ET),
                                                       in1=key1[:, :], op0=ALU.mult, op1=ALU.add))
                        chain(dve.tensor_scalar(lists[:, 2, :], f8[:, :, :].rearrange("p h k -> p (h k)"),
                                                0.0, None, ALU.max))
                        if q:
                            dve.wait_ge(sem("lists_turned"), q)
                        dve.tensor_copy(twice[:, :, :, :],
                                        lists[:, :, :].unsqueeze(2).broadcast_to([P, 3, 2, NSLOT]))\
                            .then_inc(sem("lists_ready"), 1)
                    for hf in range(2):
                        for g in range(NG):
                            m = hf * NG + g
                            if g % (NG // 2) == 0:
                                q = 2 * hf + g // (NG // 2)
                                dve.wait_ge(sem("turned_stored"), 2 * q + 2)
                                if q:
                                    dve.wait_ge(sem("outer_ready"), m)
                                else:
                                    dve.wait_ge(sem("sims_ready"), QT)
                                dve.tensor_tensor(hot_tile, iota[:, 0:ET].unsqueeze(1).broadcast_to([P, NK, ET]),
                                                  turned[:, 1, q, :].unsqueeze(2).broadcast_to([P, NK, ET]),
                                                  ALU.is_equal).then_inc(sem("hot_tiles"), 1)
                                dve.tensor_tensor(hot_part, iota[:, :].unsqueeze(1).broadcast_to([P, NK, P]),
                                                  turned[:, 0, q, :].unsqueeze(2).broadcast_to([P, NK, P]),
                                                  ALU.is_equal).then_inc(sem("hot_part_ready"), 1)
                            dve.wait_ge(sem("outer_ready"), m + 1)
                            if g == 0:
                                dve.wait_ge(sem("gelu_done"), (hf + 1) * (ET // 2))
                            hs = act_h[:, :, g * CG:(g + 1) * CG].rearrange("p i t -> p t i")
                            last = dve.tensor_tensor(hs, hs, ps[:, 2 + m % 2, :]
                                                     .rearrange("p (t i) -> p t i", i=ET), ALU.mult)
                            last.then_inc(sem("weighted"), 1)
                        dve.wait_ge(sem("up_ready"), hf + 1)
                        xq = core.x[:, ds(b * QT + 2 * hf, 2), :]
                        dve.tensor_tensor(xq, xq, ps[:, 6, :].rearrange("p (q d) -> p q d", q=2), ALU.add)\
                            .then_inc(sem("x_added"), 1)
            core.fresh()




def build(nc, w, out, stages):
    with ExitStack() as ctx:
        core = Core(nc, ctx)
        scratch = {
            "xdbl": nc.dram_tensor("xdbl_scratch", (2 * DS, T), F32, kind="Internal").ap(),
            "coef": nc.dram_tensor("coef_scratch", (NE + EL, B * T), F32, kind="Internal").ap(),
            "rel_rows": nc.dram_tensor("rel_rows_scratch", (H, SLAB), F32, kind="Internal").ap(),
        }
        load_block(core, [
            (core.x[:, :, :], w["x"].rearrange("b (q p) d -> p (b q) d", p=P)),
            (core.ident[:, :], w["ident"]),
        ])
        with nc.Block() as block:
            @block.vector
            def _(dve):
                dve.memset(core.neg_half[:, :], -0.5)
        for s in stages:
            if s == "ssm":
                ssm_stage(core, w, scratch["xdbl"])
            if s == "gather_attn":
                gather_attn_stage(core, w)
            if s == "moe":
                moe_stage(core, w, scratch["coef"])
            if s == "peer":
                peer_stage(core, w)
            if s == "self_attn":
                self_attn_stage(core, w, scratch["rel_rows"])
            if s == "cross_attn":
                cross_attn_stage(core, w)
        stored = core.sem("out_stored")
        with nc.Block() as block:
            @block.sync
            def _(sp):
                sp.dma_start(out.rearrange("b (q p) d -> p (b q) d", p=P), core.x[:, :, :]).then_inc(stored, 16)
                sp.wait_ge(stored, 16)


def layouts(inputs):
    import numpy as np

    w = {k: np.ascontiguousarray(v) for k, v in inputs.items()}
    out = {"ident": np.eye(P, dtype=np.float32), "x": w["x"]}
    def columns(v):
        return np.ascontiguousarray(v.reshape(-1, P).T)

    for k in ("conv_w", "A_log"):
        out["L0_attn_" + k] = w["L0_attn_" + k]
    for k in ("conv_b", "D_param", "b_dt"):
        out["L0_attn_" + k + "_cols"] = columns(w["L0_attn_" + k])
    for k in ("W_in", "W_dt", "W_x", "W_out"):
        out["L0_attn_" + k + "_T"] = np.ascontiguousarray(w["L0_attn_" + k].T)
    def strips(wt):
        return np.pad(wt.reshape(wt.shape[0], H, DH), ((0, 0), (0, 0), (0, STRIP - DH))).reshape(wt.shape[0], -1)

    def strip_columns(v):
        return np.ascontiguousarray(strips(v.reshape(1, -1)).reshape(G, P).T)

    out["ctx_T"] = np.ascontiguousarray(w["ctx_1024"].transpose(0, 2, 1))
    for k in ("q", "k"):
        out[f"L0_xattn_W{k}_strips"] = strips(w[f"L0_xattn_W{k}"].T)
        out[f"L0_xattn_b{k}_strips"] = strip_columns(w[f"L0_xattn_b{k}"])
    for k in ("v", "o"):
        out[f"L0_xattn_W{k}_T"] = np.ascontiguousarray(w[f"L0_xattn_W{k}"].T)
        out[f"L0_xattn_b{k}"] = w[f"L0_xattn_b{k}"]
    wq, wk, wv = (w["L1_attn_qkv_w"][i * D:(i + 1) * D] for i in range(3))
    bq, bk, bv = (w["L1_attn_qkv_b"][i * D:(i + 1) * D] for i in range(3))
    out["L1_attn_Wq_strips"], out["L1_attn_Wk_strips"] = strips(wq.T), strips(wk.T)
    out["L1_attn_bq_strips"], out["L1_attn_bk_strips"] = strip_columns(bq), strip_columns(bk)
    out["L1_attn_Wv_T"], out["L1_attn_bv"] = np.ascontiguousarray(wv.T), np.ascontiguousarray(bv)
    out["L1_attn_proj_w_T"] = np.ascontiguousarray(w["L1_attn_proj_w"].T)
    out["L1_attn_proj_b"] = w["L1_attn_proj_b"]
    out["L1_attn_rel_back"] = np.ascontiguousarray(w["L1_attn_rel_pos_emb"][::-1][:RELK])
    for k in ("q", "k", "v"):
        out[f"L1_xattn_W{k}_T"] = np.ascontiguousarray(w[f"L1_xattn_W{k}"].T)
    for k in ("q", "k"):
        out[f"L1_xattn_b{k}_cols"] = columns(w[f"L1_xattn_b{k}"])
    out["L1_xattn_bv"] = w["L1_xattn_bv"]

    def expert_parts(wg, wu, wd):
        n = wg.shape[0]
        halves = [m.reshape(n, KC, P, FF).transpose(0, 2, 1, 3).reshape(n, P, KC * FF) for m in (wg, wu)]
        return np.concatenate(halves + [wd], axis=2)

    routed = expert_parts(w["L0_ffn_Wg"], w["L0_ffn_Wu"], w["L0_ffn_Wd"])
    shared = expert_parts(w["L0_ffn_SWg"].reshape(D, NSH, FF).transpose(1, 0, 2),
                          w["L0_ffn_SWu"].reshape(D, NSH, FF).transpose(1, 0, 2),
                          w["L0_ffn_SWd"].reshape(NSH, FF, D))
    out["L0_ffn_experts"] = np.pad(np.concatenate([routed, shared]), ((0, EL - NSH), (0, 0), (0, 0)))
    out["L0_ffn_router_T"] = np.ascontiguousarray(w["L0_ffn_router_w"].T)
    out["L0_ffn_e_bias"] = w["L0_ffn_e_bias"]
    out["earlier"] = np.tril(np.ones((EG, EG), np.float32), -1)

    out["flip"] = np.ascontiguousarray(np.eye(P, dtype=np.float32)[::-1])
    out["iota"] = np.arange(P, dtype=np.float32)
    out["L1_ffn_norm_w"] = w["L1_ffn_norm_w"]
    out["L1_ffn_w_q_T"] = np.ascontiguousarray(w["L1_ffn_w_q"].T)
    out["L1_ffn_keys_T"] = np.ascontiguousarray(w["L1_ffn_keys"].transpose(3, 0, 2, 1).reshape(DK, 2 * PH, NK))
    tiles = (2, ET, NK, D)
    out["L1_ffn_down_T"] = np.ascontiguousarray(
        w["L1_ffn_expert_down"].reshape(tiles).transpose(3, 1, 0, 2).reshape(D, NK * NK))
    out["L1_ffn_up"] = np.ascontiguousarray(
        w["L1_ffn_expert_up"].reshape(tiles).transpose(0, 2, 1, 3).reshape(P, ET, D))
    return out


def kernel(**inputs):
    import numpy as _np
    import concourse.bacc as _bacc
    from concourse import mybir as _mybir
    from concourse.bass_utils import run_bass_kernel_spmd as _run

    nc = _bacc.Bacc("TRN2", target_bir_lowering=False, num_devices=1)
    arrays, aps = {}, {}
    for name, a in layouts({k: _np.asarray(v) for k, v in inputs.items()}).items():
        arrays[name + "_dram"] = a
        aps[name] = nc.dram_tensor(name + "_dram", a.shape, _mybir.dt.from_np(a.dtype), kind="ExternalInput").ap()
    out = nc.dram_tensor("out_dram", (B, T, D), F32, kind="ExternalOutput").ap()
    build(nc, aps, out, STAGES)
    r = _run(nc, [arrays], core_ids=[0])
    return r.results[0]["out_dram"]
```

```python
from contextlib import ExitStack

import concourse.bass as bass
from concourse import mybir

F32 = mybir.dt.float32
F32R = mybir.dt.float32r
U32 = mybir.dt.uint32
BF16 = mybir.dt.bfloat16
ALU = mybir.AluOpType
ACT = mybir.ActivationFunctionType
AX = mybir.AxisListType
ds = bass.ds

P = 128
B, T, D = 4, 512, 256
QT = T // P
NT = B * QT
KC = D // P
BANK = 512
LN_EPS = 1e-5
DI, DS, DCONV = 512, 16, 4
DT = DI // P
SU = 4
UR = 4
H, DH = 16, 16
G = 4
STRIP = 32
CTX = 1601
STRIDE = 16
CK = CTX // STRIDE
NEG = -1.0e30

STAGES = ("ssm", "gather_attn", "moe", "self_attn", "cross_attn", "peer")


class Chain:

    def __init__(self, engine, sem):
        self.engine, self.sem, self.n = engine, sem, 0

    def __call__(self, instruction):
        self.n += 1
        instruction.then_inc(self.sem, 1)
        self.engine.wait_ge(self.sem, self.n)


class Core:

    def __init__(self, nc, ctx):
        self.nc, self.ctx = nc, ctx
        self.sems = {}
        self.x = ctx.enter_context(nc.sbuf_tensor("x_res", [P, NT, D], F32))
        self.ident = ctx.enter_context(nc.sbuf_tensor("ident", [P, P], F32))
        self.neg_half = ctx.enter_context(nc.sbuf_tensor("neg_half", [P, QT], F32))
        self.ps = ctx.enter_context(nc.psum_tensor("ps", [P, 8, BANK], F32))

    def sem(self, name):
        if name not in self.sems:
            self.sems[name] = self.ctx.enter_context(self.nc.semaphore(name))
        return self.sems[name]

    def fresh(self):
        nums = sorted(s.num for s in self.sems.values())
        lo, hi = nums[0], nums[-1] + 1
        assert nums == list(range(lo, hi))
        self.nc.vector.sem_clear(range(lo, hi))
        self.nc.all_engine_barrier()


def load_block(core, pairs):
    nc = core.nc
    loaded = core.sem("weights_loaded")
    loaded2 = core.sem("weights_loaded_act")
    with nc.Block() as block:
        @block.sync
        def _(sp):
            for out, in_ in pairs[0::2]:
                sp.dma_start(out, in_).then_inc(loaded, 16)
            sp.wait_ge(loaded, 16 * len(pairs[0::2]))

        @block.scalar
        def _(act):
            for out, in_ in pairs[1::2]:
                act.dma_start(out, in_).then_inc(loaded2, 16)
            if pairs[1::2]:
                act.wait_ge(loaded2, 16 * len(pairs[1::2]))
    core.fresh()


def norm_dve(core, dve, b, xn, stats, mv, rstd, keep_sum=False, extra=None):
    x = core.x
    chain = Chain(dve, core.sem("norm_chain"))
    for q in range(QT):
        last = dve.bn_stats(stats[:, q, :], x[:, ds(b * QT + q, 1), :])
    chain(last)
    for q in range(QT):
        last = dve.bn_aggr(mv[:, q, :], stats[:, q, :])
    chain(last)
    dve.tensor_scalar(rstd[:, :], mv[:, :, 1], LN_EPS, None, ALU.add).then_inc(core.sem("var_ready"), 1)
    dve.wait_ge(core.sem("rstd_ready"), 1)
    for q in range(QT):
        ins = dve.tensor_scalar(xn[:, q, :], x[:, ds(b * QT + q, 1), :], mv[:, q, 0:1], rstd[:, q:q + 1],
                                ALU.subtract, ALU.mult)
        if extra is None:
            ins.then_inc(core.sem("xn_ready"), 1)
    if extra is not None:
        chain(ins)
        extra(chain)
    elif keep_sum:
        dve.wait_ge(core.sem("xn_ready"), QT)
        xb = x[:, ds(b * QT, QT), :]
        dve.tensor_tensor(xb, xb, xn[:, :, :], ALU.add).then_inc(core.sem("x_plus_xn"), 1)


def norm_pool(core, pool, rstd):
    pool.wait_ge(core.sem("var_ready"), 1)
    pool.tensor_tensor(rstd[:, :], rstd[:, :], core.neg_half[:, :], ALU.pow)\
        .then_inc(core.sem("rstd_ready"), 1)


def norm_pe(core, pe, xn, banks=(0, 1)):
    for q in range(QT):
        pe.wait_ge(core.sem("xn_ready"), q + 1)
        for c in range(KC):
            last = pe.transpose(core.ps[:, banks[c], q * P:(q + 1) * P], xn[:, q, c * P:(c + 1) * P],
                                core.ident[:, :])
    last.then_inc(core.sem("xn_turned"), 1)


def norm_act(core, act, xT, banks=(0, 1)):
    act.wait_ge(core.sem("xn_turned"), 1)
    for c in range(KC):
        act.activation(xT[c], core.ps[:, banks[c], :], ACT.Copy).then_inc(core.sem("xT_ready"), 1)




def ssm_stage(core, w, scratch):
    nc = core.nc
    x, ps = core.x, core.ps
    with ExitStack() as ctx:
        def sb(name, shape, dt=F32):
            return ctx.enter_context(nc.sbuf_tensor("ssm_" + name, shape, dt))

        w_in = sb("w_in", [P, KC, 2 * DI])
        w_dt = sb("w_dt", [P, DT, DI])
        w_x = sb("w_x", [P, DT, 2 * DS])
        w_out = sb("w_out", [P, DT, D])
        conv_w = sb("conv_w", [P, DT, DCONV])
        conv_b = sb("conv_b", [P, DT])
        a_log = sb("a_log", [P, DT, DS])
        a_neg = sb("a_neg", [P, DT, DS])
        d_par = sb("d_par", [P, DT])
        b_dt = sb("b_dt", [P, DT])
        bc = sb("bc", [P, 2 * DS, T])
        dA = sb("dA", [P, UR, SU, T])
        hb = sb("hb", [P, UR, SU, T])
        xs = sb("xs", [P, DT, T])
        sz = sb("sz", [P, DT, T])
        dt = sb("dt", [P, DT, T])
        u = sb("u", [P, DT, T])
        soft = sb("soft", [P, DT, T])
        xdbl = sb("xdbl", [2 * DS, T])
        stats = sb("stats", [P, QT, 6])
        mv = sb("mv", [P, QT, 2])
        rstd = sb("rstd", [P, QT])
        xn = hb[:, 0, 0:2, :].rearrange("p a (c d) -> p (a c) d", d=D)

        xT = soft[:, 0:KC, :]
        load_block(core, [
            (w_in[:, :, :], w["L0_attn_W_in_T"].rearrange("(c p) e -> p c e", p=P)),
            (w_dt[:, :, :], w["L0_attn_W_dt_T"].rearrange("(c p) f -> p c f", p=P)),
            (w_x[:, :, :], w["L0_attn_W_x_T"].rearrange("(c p) s -> p c s", p=P)),
            (w_out[:, :, :], w["L0_attn_W_out_T"].rearrange("(c p) d -> p c d", p=P)),
            (conv_w[:, :, :], w["L0_attn_conv_w"].rearrange("(c p) o k -> p c (o k)", p=P)),
            (conv_b[:, :], w["L0_attn_conv_b_cols"]),
            (a_log[:, :, :], w["L0_attn_A_log"].rearrange("(c p) s -> p c s", p=P)),
            (d_par[:, :], w["L0_attn_D_param_cols"]),
            (b_dt[:, :], w["L0_attn_b_dt_cols"]),
        ])
        a_exp = core.sem("a_exp")
        with nc.Block() as block:
            @block.scalar
            def _(act):
                act.activation(a_neg[:, :, :], a_log[:, :, :], ACT.Exp).then_inc(a_exp, 1)

            @block.vector
            def _(dve):
                dve.wait_ge(a_exp, 1)
                dve.tensor_scalar(a_neg[:, :, :], a_neg[:, :, :], -1.0, None, ALU.mult)
                dve.memset(dA[:, :, :, 0:1], 0.0)
        core.fresh()

        sem = core.sem
        bc_loaded = [sem(f"bc_{part}_loaded") for part in range(DS // SU)]
        NU = DT * DS // SU
        with nc.Fori(0, B) as b:
            with nc.Block() as block:
                @block.tensor
                def _(pe):
                    norm_pe(core, pe, xn)
                    pe.wait_ge(sem("xT_ready"), KC)
                    for e in range(2 * DT):
                        bank = 4 + e if e < DT else e - DT
                        for c in range(KC):
                            last = pe.matmul(ps[:, bank, :], w_in[:, c, e * P:(e + 1) * P], xT[:, c, :],
                                             start=(c == 0), stop=(c == KC - 1))
                        last.then_inc(sem("xz_ready"), 1)
                    pe.wait_ge(sem("xs_ready"), 1)
                    pe.wait_ge(sem("sz_ready"), 1)
                    for c in range(DT):
                        last = pe.matmul(ps[0:2 * DS, 0, :], w_x[:, c, :], xs[:, c, :],
                                         start=(c == 0), stop=(c == DT - 1))
                    last.then_inc(sem("bc_ready"), 1)
                    for f in range(DT):
                        for c in range(DT):
                            last = pe.matmul(ps[:, 4 + f, :], w_dt[:, c, f * P:(f + 1) * P], xs[:, c, :],
                                             start=(c == 0), stop=(c == DT - 1))
                        last.then_inc(sem("dt_ready"), 1)
                    pe.wait_ge(sem("xdbl_out"), 1)
                    for n in range(NU):
                        d, part = divmod(n, DS // SU)
                        pe.wait_ge(sem("hc_ready"), n + 1)
                        if part == 0 and d >= 2:
                            pe.wait_ge(sem("y_done"), d - 1)
                        for s in range(SU):
                            last = pe.matmul(ps[:, d % 2, :], core.ident[:, :], hb[:, n % UR, s, :],
                                             start=(part == 0 and s == 0),
                                             stop=(part == DS // SU - 1 and s == SU - 1))
                        last.then_inc(sem("hc_summed"), 1)
                    pe.wait_ge(sem("y_done"), DT)
                    for q in range(QT):
                        for c in range(DT):
                            last = pe.matmul(ps[:, 2 + q // 2, (q % 2) * D:(q % 2 + 1) * D],
                                             xs[:, c, q * P:(q + 1) * P], w_out[:, c, :],
                                             start=(c == 0), stop=(c == DT - 1))
                    last.then_inc(sem("out_ready"), 1)

                @block.scalar
                def _(act):
                    norm_act(core, act, [xT[:, c, :] for c in range(KC)])
                    act.wait_ge(sem("conv_done"), 1)
                    act.activation(xs[:, :, :], u[:, :, :], ACT.Silu).then_inc(sem("xs_ready"), 1)
                    act.wait_ge(sem("xz_ready"), 2 * DT)
                    act.activation(sz[:, :, :], ps[:, 0:DT, :], ACT.Silu).then_inc(sem("sz_ready"), 1)
                    act.wait_ge(sem("bc_ready"), 1)
                    act.activation(xdbl[:, :], ps[0:2 * DS, 0, :], ACT.Copy).then_inc(sem("xdbl_out"), 1)
                    chain = Chain(act, sem("act_chain"))

                    def logarithms(tiles):
                        act.wait_ge(sem("z_ready"), tiles.stop)
                        chain(act.activation(soft[:, tiles, :], dt[:, tiles, :], ACT.Abs))
                        chain(act.activation(soft[:, tiles, :], soft[:, tiles, :], ACT.Exp, scale=-1.0))
                        act.activation(soft[:, tiles, :], soft[:, tiles, :], ACT.Ln, bias=1.0)\
                            .then_inc(sem("ln_ready"), 1)

                    logarithms(slice(0, 1))
                    for n in range(NU):
                        if n == 2:
                            logarithms(slice(1, DT))
                        if n % (DS // SU) == 0 and n // (DS // SU) < 2:
                            act.wait_ge(sem("u_ready"), n // (DS // SU) + 1)
                        d, part = divmod(n, DS // SU)
                        if n >= UR:
                            act.wait_ge(sem("scanned"), n - UR + 1)
                        for s in range(SU):
                            i = part * SU + s
                            last = act.activation(dA[:, n % UR, s, 1:T], dt[:, d, 1:T], ACT.Exp,
                                                  scale=a_neg[:, d, i:i + 1])
                        last.then_inc(sem("dA_ready"), 1)

                @block.sync
                def _(sp):
                    sp.wait_ge(sem("xdbl_out"), 1)
                    sp.dma_start(scratch[:, :], xdbl[:, :]).then_inc(sem("xdbl_stored"), 16)
                    sp.wait_ge(sem("xdbl_stored"), 16)
                    for part in range(DS // SU):
                        for rows in (slice(part * SU, (part + 1) * SU),
                                     slice(DS + part * SU, DS + (part + 1) * SU)):
                            sp.dma_start(bc[:, rows, :], scratch[rows, :].partition_broadcast(P))\
                              .then_inc(bc_loaded[part], 16)

                @block.gpsimd
                def _(pool):
                    norm_pool(core, pool, rstd)
                    for n in range(NU):
                        d, part = divmod(n, DS // SU)
                        if d == 0:
                            pool.wait_ge(bc_loaded[part], 32)
                        if part == 0 and d < 2:
                            pool.wait_ge(sem("u_ready"), d + 1)
                        if n >= UR:
                            pool.wait_ge(sem("hc_summed"), n - UR + 1)
                        pool.tensor_tensor(hb[:, n % UR, :, :],
                                           u[:, d, :].unsqueeze(1).broadcast_to([P, SU, T]),
                                           bc[:, part * SU:(part + 1) * SU, :], ALU.mult)\
                            .then_inc(sem("dBx_ready"), 1)

                @block.vector
                def _(dve):
                    norm_dve(core, dve, b, xn, stats, mv, rstd, keep_sum=True)
                    chain = Chain(dve, sem("dve_chain"))
                    for e in range(DT):
                        dve.wait_ge(sem("xz_ready"), e + 1)
                        chain(dve.tensor_scalar(u[:, e, :], ps[:, 4 + e, :], conv_w[:, e, DCONV - 1:DCONV],
                                                conv_b[:, e:e + 1], ALU.mult, ALU.add))
                        for k in range(1, DCONV):
                            ins = dve.scalar_tensor_tensor(
                                out=u[:, e, k:T], in0=ps[:, 4 + e, 0:T - k],
                                scalar=conv_w[:, e, DCONV - 1 - k:DCONV - k], in1=u[:, e, k:T],
                                op0=ALU.mult, op1=ALU.add)
                            if k < DCONV - 1:
                                chain(ins)
                    ins.then_inc(sem("conv_done"), 1)
                    dve.wait_ge(sem("xs_ready"), 1)
                    for f in range(DT):
                        dve.wait_ge(sem("dt_ready"), f + 1)
                        dve.tensor_scalar(dt[:, f, :], ps[:, 4 + f, :], b_dt[:, f:f + 1], None, ALU.add)\
                            .then_inc(sem("z_ready"), 1)

                    def step_sizes(tiles, order):
                        dve.wait_ge(sem("z_ready"), DT)
                        dve.wait_ge(sem("ln_ready"), order)
                        chain(dve.scalar_tensor_tensor(out=dt[:, tiles, :], in0=dt[:, tiles, :], scalar=0.0,
                                                       in1=soft[:, tiles, :], op0=ALU.max, op1=ALU.add))
                        dve.tensor_tensor(u[:, tiles, :], dt[:, tiles, :], xs[:, tiles, :], ALU.mult)\
                            .then_inc(sem("u_ready"), 1)

                    step_sizes(slice(0, 1), 1)

                    def finish(d):
                        dve.wait_ge(sem("hc_summed"), (d + 1) * DS // SU)
                        chain(dve.scalar_tensor_tensor(out=xs[:, d, :], in0=xs[:, d, :],
                                                       scalar=d_par[:, d:d + 1], in1=ps[:, d % 2, :],
                                                       op0=ALU.mult, op1=ALU.add))
                        dve.tensor_tensor(xs[:, d, :], xs[:, d, :], sz[:, d, :], ALU.mult)\
                            .then_inc(sem("y_done"), 1)

                    for n in range(NU):
                        if n == 2:
                            step_sizes(slice(1, DT), 2)
                        d, part = divmod(n, DS // SU)
                        dve.wait_ge(sem("dA_ready"), n + 1)
                        dve.wait_ge(sem("dBx_ready"), n + 1)
                        h = hb[:, n % UR, :, :]
                        hf = h.rearrange("p s t -> p (s t)")
                        dve.tensor_tensor_scan(hf, dA[:, n % UR, :, :].rearrange("p s t -> p (s t)"), hf,
                                               0.0, ALU.mult, ALU.add).then_inc(sem("scanned"), 1)
                        dve.wait_ge(sem("scanned"), n + 1)
                        dve.tensor_tensor(h, h, bc[:, DS + part * SU:DS + (part + 1) * SU, :], ALU.mult)\
                            .then_inc(sem("hc_ready"), 1)
                        if part == 0 and d >= 1:
                            finish(d - 1)
                    finish(DT - 1)
                    dve.wait_ge(sem("out_ready"), 1)
                    dve.wait_ge(sem("x_plus_xn"), 1)
                    xb = x[:, ds(b * QT, QT), :]
                    dve.tensor_tensor(xb, xb, ps[:, 2:4, :].rearrange("p a (c d) -> p (a c) d", d=D), ALU.add)
            core.fresh()




def add_bias_rows(core, dve, b, bias):
    dve.wait_ge(core.sem("xn_ready"), QT)
    xb = core.x[:, ds(b * QT, QT), :]
    dve.tensor_tensor(xb, xb, bias[:, :].unsqueeze(1).broadcast_to([P, QT, D]), ALU.add)\
        .then_inc(core.sem("bias_added"), 1)


def copy_sums_act(core, act, q, summed, sums_T):
    act.wait_ge(core.sem("values_summed"), summed)
    if q:
        act.wait_ge(core.sem("heads_T_ready"), q)
    act.activation(sums_T[:, :, :], core.ps[:, 6, :].rearrange("p (g t) -> p g t", g=G), ACT.Copy)\
        .then_inc(core.sem("sums_copied"), 1)


def spread_pe(core, pe, q, sums_T, spread):
    pe.wait_ge(core.sem("sums_copied"), q + 1)
    if q:
        pe.wait_ge(core.sem("x_added"), q)
    pe.matmul(core.ps[:, 7, :], spread[:, :], sums_T[:, :, :].rearrange("p g t -> p (g t)"), start=True, stop=True)\
      .then_inc(core.sem("den_spread"), 1)


def invert_den_dve(core, dve, q, g, inv_den):
    if g == 0:
        dve.wait_ge(core.sem("den_spread"), q + 1)
        if q:
            dve.wait_ge(core.sem("heads_T_ready"), q)
    dve.reciprocal(inv_den[:, g, :], core.ps[:, 7, g * P:(g + 1) * P]).then_inc(core.sem("den_ready"), 1)


def normalise_pool(core, pool, sums_T, inv_den, heads_T):
    for q in range(QT):
        if q:
            pool.wait_ge(core.sem("projected"), q)
        pool.wait_ge(core.sem("den_ready"), G * (q + 1))
        pool.tensor_tensor(heads_T[:, :, :], sums_T[:, :, :], inv_den[:, :, :], ALU.mult)\
            .then_inc(core.sem("heads_T_ready"), 1)


def project_strips_pe(core, pe, q, heads_T, w_o):
    pe.wait_ge(core.sem("heads_T_ready"), q + 1)
    for g in range(G):
        last = pe.matmul(core.ps[:, 7, 0:D], heads_T[:, g, :], w_o[:, g, :], start=(g == 0), stop=(g == G - 1))
    last.then_inc(core.sem("projected"), 1)


def project_strips_dve(core, dve, b, q):
    dve.wait_ge(core.sem("projected"), q + 1)
    if q == 0:
        dve.wait_ge(core.sem("bias_added"), 1)
    xq = core.x[:, ds(b * QT + q, 1), :]
    dve.tensor_tensor(xq, xq, core.ps[:, 7:8, 0:D], ALU.add).then_inc(core.sem("x_added"), 1)




def gather_attn_stage(core, w):
    nc = core.nc
    ps, sem = core.ps, core.sem
    with ExitStack() as ctx:
        def sb(name, shape, dt=F32):
            return ctx.enter_context(nc.sbuf_tensor("ga_" + name, shape, dt))

        w_q = sb("w_q", [P, KC, G * P])
        w_k = sb("w_k", [P, KC, G * P])
        w_v = sb("w_v", [P, KC, G * P])
        w_o = sb("w_o", [P, G, D])
        b_q = sb("b_q", [P, G])
        b_k = sb("b_k", [P, G])
        b_v = sb("b_v", [P, G])
        b_o = sb("b_o", [P, D])
        spread = sb("spread", [P, P])
        cT = sb("cT", [P, KC, STRIDE * P])
        xn = sb("xn", [P, QT, D])
        xT = sb("xT", [P, KC, T])
        qT = sb("qT", [P, G, T])
        kT = sb("kT", [P, G, P])
        vT = sb("vT", [P, G, P])
        v = sb("v", [P, H, STRIP])
        probs = sb("probs", [P, 2, H, CK])
        pT = sb("pT", [P, 2, H, P])
        top = sb("top", [P, 2, H])
        sums_T = sb("sums_T", [P, G, P])
        inv_den = sb("inv_den", [P, G, P])
        heads_T = sb("heads_T", [P, G, P])
        stats = sb("stats", [P, QT, 6])
        mv = sb("mv", [P, QT, 2])
        rstd = sb("rstd", [P, QT])

        load_block(core, [
            (cT[:, :, 0:CTX], w["ctx_T"][0, :, :].rearrange("(c p) k -> p c k", p=P)),
            (w_k[:, :, :], w["L0_xattn_Wk_strips"].rearrange("(c p) e -> p c e", p=P)),
            (w_q[:, :, :], w["L0_xattn_Wq_strips"].rearrange("(c p) e -> p c e", p=P)),
            (w_v[:, :, :], w["L0_xattn_Wv_strips"].rearrange("(c p) e -> p c e", p=P)),
            (w_o[:, :, :], w["L0_xattn_Wo_strips"].rearrange("(g p) e -> p g e", p=P)),
            (spread[:, :], w["spread"]),
            (b_q[:, :], w["L0_xattn_bq_strips"]),
            (b_k[:, :], w["L0_xattn_bk_strips"]),
            (b_v[:, :], w["L0_xattn_bv_one_strips"]),
            (b_o[:, :], w["L0_xattn_bo"].partition_broadcast(P)),
        ])
        with nc.Block() as block:
            @block.vector
            def _(dve):
                dve.memset(cT[:, :, CTX:STRIDE * P], 0.0)
        core.fresh()

        def gather_block(b, last_batch):
            with nc.Block() as block:
                @block.sync
                def _(sp):
                    if not last_batch:
                        sp.wait_ge(sem("kv_ready"), 2)
                        sp.dma_start(cT[:, :, 0:CTX], w["ctx_T"][ds(b + 1, 1), :, :]
                                     .rearrange("o (c p) k -> p (o c) k", p=P)).then_inc(sem("ctx_loaded"), 16)
                        sp.wait_ge(sem("ctx_loaded"), 16)

                @block.tensor
                def _(pe):
                    for bank, wt in ((2, w_k), (3, w_v)):
                        for h in range(H):
                            g, j = divmod(h, G)
                            for c in range(KC):
                                last = pe.matmul(ps[STRIP * j:STRIP * (j + 1), bank, g * P:(g + 1) * P],
                                                 wt[:, c, g * P + STRIP * j:g * P + STRIP * (j + 1)],
                                                 cT[:, c, h:h + STRIDE * (P - 1) + 1:STRIDE],
                                                 start=(c == 0), stop=(c == KC - 1))
                        last.then_inc(sem("kv_ready"), 1)
                    norm_pe(core, pe, xn)
                    pe.wait_ge(sem("vT_stored"), 1)
                    for g in range(G):
                        last = pe.transpose(ps[:, 3, g * P:(g + 1) * P], vT[:, g, :], core.ident[:, :])
                    last.then_inc(sem("v_turned"), 1)
                    pe.wait_ge(sem("xT_ready"), KC)
                    for g in range(G):
                        for c in range(KC):
                            last = pe.matmul(ps[:, 4 + g, :], w_q[:, c, g * P:(g + 1) * P], xT[:, c, :],
                                             start=(c == 0), stop=(c == KC - 1))
                        last.then_inc(sem("q_ready"), 1)

                    def scores(q):
                        if q == 0:
                            pe.wait_ge(sem("k_stored"), 1)
                            pe.wait_ge(sem("v_stored"), 1)
                            pe.wait_ge(sem("q_stored"), G)
                        else:
                            pe.wait_ge(sem("scores_read"), q)
                        for j in range(G):
                            for g in range(G):
                                s = slice(STRIP * j, STRIP * (j + 1))
                                last = pe.matmul(ps[:, j, g * P:(g + 1) * P], qT[s, g, q * P:(q + 1) * P],
                                                 kT[s, g, :], start=True, stop=True)
                        last.then_inc(sem("scores_ready"), 1)

                    def turn_weights(q):
                        pe.wait_ge(sem("probs_ready"), q + 1)
                        for j in range(G):
                            if G * q + j >= 2:
                                pe.wait_ge(sem("pT_stored"), G * q + j - 1)
                            for g in range(G):
                                last = pe.transpose(ps[0:CK, 4 + j % 2, g * P:(g + 1) * P],
                                                    probs[:, q % 2, j * G + g, :], core.ident[:, :])
                            last.then_inc(sem("p_turned"), 1)

                    def sum_values(q):
                        pe.wait_ge(sem("pT_stored"), G * (q + 1))
                        if q:
                            pe.wait_ge(sem("sums_copied"), q)
                        for h in range(H):
                            g, j = divmod(h, G)
                            last = pe.matmul(ps[STRIP * j:STRIP * (j + 1), 6, g * P:(g + 1) * P],
                                             v[0:CK, h, :], pT[0:CK, q % 2, j * G + g, :], start=True, stop=True)
                        last.then_inc(sem("values_summed"), 1)

                    scores(0)
                    for q in range(QT + 2):
                        if q + 1 < QT:
                            scores(q + 1)
                        if q < QT:
                            turn_weights(q)
                        if 0 <= q - 2 < QT:
                            project_strips_pe(core, pe, q - 2, heads_T, w_o)
                        if 0 <= q - 1 < QT:
                            spread_pe(core, pe, q - 1, sums_T, spread)
                        if q < QT:
                            sum_values(q)

                @block.scalar
                def _(act):
                    act.wait_ge(sem("kv_ready"), 2)
                    for g in range(G):
                        last = act.activation(vT[:, g, :], ps[:, 3, g * P:(g + 1) * P], ACT.Identity,
                                              bias=b_v[:, g:g + 1])
                    last.then_inc(sem("vT_stored"), 1)
                    norm_act(core, act, [xT[:, c, :] for c in range(KC)])
                    act.wait_ge(sem("v_turned"), 1)
                    act.activation(v[:, :, :], ps[:, 3, :].rearrange("k (h e) -> k h e", e=STRIP), ACT.Copy)\
                        .then_inc(sem("v_stored"), 1)
                    for g in range(G):
                        act.wait_ge(sem("q_ready"), g + 1)
                        act.activation(qT[:, g, :], ps[:, 4 + g, :], ACT.Identity, bias=b_q[:, g:g + 1])\
                            .then_inc(sem("q_stored"), 1)

                    def weights(q):
                        act.wait_ge(sem("scores_read"), q + 1)
                        pq = probs[:, q % 2, :, :]
                        act.activation(pq, pq, ACT.Exp, scale=DH ** -0.5).then_inc(sem("probs_ready"), 1)

                    weights(0)
                    for q in range(QT):
                        for j in range(G):
                            act.wait_ge(sem("p_turned"), G * q + j + 1)
                            if q >= 2:
                                act.wait_ge(sem("values_summed"), q - 1)
                            act.activation(pT[0:CK, q % 2, j * G:(j + 1) * G, :],
                                           ps[0:CK, 4 + j % 2, :].rearrange("k (g t) -> k g t", g=G), ACT.Copy)\
                                .then_inc(sem("pT_stored"), 1)
                        if q + 1 < QT:
                            weights(q + 1)
                        copy_sums_act(core, act, q, q + 1, sums_T)

                @block.gpsimd
                def _(pool):
                    norm_pool(core, pool, rstd)
                    normalise_pool(core, pool, sums_T, inv_den, heads_T)

                @block.vector
                def _(dve):
                    norm_dve(core, dve, b, xn, stats, mv, rstd)
                    add_bias_rows(core, dve, b, b_o)
                    dve.wait_ge(sem("kv_ready"), 1)
                    dve.tensor_tensor(kT[:, :, :], ps[:, 2, :].rearrange("p (g k) -> p g k", g=G),
                                      b_k[:, :].unsqueeze(2).broadcast_to([P, G, P]), ALU.add)\
                        .then_inc(sem("k_stored"), 1)

                    def subtract_top(q):
                        dve.wait_ge(sem("scores_ready"), q + 1)
                        if q >= 2:
                            dve.wait_ge(sem("p_turned"), G * (q - 1))
                        s = ps[:, 0:G, :].rearrange("p j (g k) -> p j g k", g=G)[:, :, :, 0:CK]
                        t = top[:, q % 2, :].rearrange("p (j g) -> p j g", g=G)
                        dve.tensor_reduce(t, s, AX.X, ALU.max).then_inc(sem("top_ready"), 1)
                        dve.wait_ge(sem("top_ready"), q + 1)
                        dve.tensor_tensor(probs[:, q % 2, :, :].rearrange("p (j g) k -> p j g k", g=G), s,
                                          t.unsqueeze(3).broadcast_to([P, G, G, CK]), ALU.subtract)\
                            .then_inc(sem("scores_read"), 1)

                    subtract_top(0)
                    for q in range(QT + 2):
                        if q + 1 < QT:
                            subtract_top(q + 1)
                        if 0 <= q - 2 < QT:
                            project_strips_dve(core, dve, b, q - 2)
                        if 0 <= q - 1 < QT:
                            for g in range(G):
                                invert_den_dve(core, dve, q - 1, g, inv_den)
            core.fresh()

        with nc.Fori(0, B - 1) as b:
            gather_block(b, False)
        gather_block(B - 1, True)



REL = 511
RELK = 256
PR = 6
SLAB = 640


def self_attn_stage(core, w, scratch):
    nc = core.nc
    ps, sem = core.ps, core.sem
    with ExitStack() as ctx:
        def sb(name, shape, dt=F32):
            return ctx.enter_context(nc.sbuf_tensor("sa_" + name, shape, dt))

        w_q = sb("w_q", [P, KC, G * P])
        w_k = sb("w_k", [P, KC, G * P])
        w_v = sb("w_v", [P, KC, D])
        w_o = sb("w_o", [P, G, D])
        b_q = sb("b_q", [P, G])
        b_qn = sb("b_qn", [P, G])
        b_k = sb("b_k", [P, G])
        b_v = sb("b_v", [P, D])
        b_o = sb("b_o", [P, D])
        emb = sb("emb", [P, RELK // P, H, DH])
        tab = sb("tab", [P, RELK // P, H])
        rows = sb("rows", [H, SLAB])
        slab = sb("slab", [P, H, T])
        flipped = sb("flipped", [P, H, T])
        flip = sb("flip", [P, P])
        xn = sb("xn", [P, QT, D])
        xT = sb("xT", [P, KC, T])
        qT = sb("qT", [P, G, T])
        kT = sb("kT", [P, G, T])
        v = sb("v", [P, QT, H, STRIP])
        probs = sb("probs", [P, PR, T])
        pT = sb("pT", [P, 4, T])
        top = sb("top", [P, PR])
        spread = sb("spread", [P, P])
        sums_T = sb("sums_T", [P, G, P])
        inv_den = sb("inv_den", [P, G, P])
        heads_T = sb("heads_T", [P, G, P])
        stats = sb("stats", [P, QT, 6])
        mv = sb("mv", [P, QT, 2])
        rstd = sb("rstd", [P, QT])

        load_block(core, [
            (emb[:, :, :, :], w["L1_attn_rel_back"].rearrange("(a p) (h e) -> p a h e", p=P, e=DH)),
            (flip[:, :], w["flip"]),
            (w_q[:, :, :], w["L1_attn_Wq_strips"].rearrange("(c p) e -> p c e", p=P)),
            (w_k[:, :, :], w["L1_attn_Wk_strips"].rearrange("(c p) e -> p c e", p=P)),
            (w_v[:, :, :], w["L1_attn_Wv_T"].rearrange("(c p) e -> p c e", p=P)),
            (w_o[:, :, :], w["L1_attn_proj_w_strips"].rearrange("(g p) e -> p g e", p=P)),
            (spread[:, :], w["spread"]),
            (b_q[:, :], w["L1_attn_bq_strips"]),
            (b_k[:, :], w["L1_attn_bk_strips"]),
            (b_v[:, :], w["L1_attn_bv"].partition_broadcast(P)),
            (b_o[:, :], w["L1_attn_proj_b"].partition_broadcast(P)),
        ])
        with nc.Block() as block:
            @block.vector
            def _(dve):
                dve.memset(v[:, :, :, DH:DH + 1], 1.0)
                dve.memset(v[:, :, :, DH + 1:STRIP], 0.0)
                dve.tensor_scalar(b_qn[:, :], b_q[:, :], -DH ** -0.5, None, ALU.mult)
                dve.tensor_reduce(tab[:, :, :], emb[:, :, :, :], AX.X, ALU.add).then_inc(sem("tab_ready"), 1)
                dve.memset(rows[:, T:SLAB], -NEG)
                dve.wait_ge(sem("tab_turned"), 1)
                dve.tensor_scalar(rows[:, T - RELK:T], ps[0:H, 0, 0:RELK], -1.0, None, ALU.mult)
                dve.tensor_scalar(rows[:, 0:T - RELK],
                                  ps[0:H, 0, 0:1].broadcast_to([H, T - RELK]), -1.0, None, ALU.mult)\
                    .then_inc(sem("rows_ready"), 1)

            @block.tensor
            def _(pe):
                pe.wait_ge(sem("tab_ready"), 1)
                for a in range(RELK // P):
                    last = pe.transpose(ps[0:H, 0, a * P:(a + 1) * P], tab[:, a, :], core.ident[:, :])
                last.then_inc(sem("tab_turned"), 1)
                pe.wait_ge(sem("slab_loaded"), 16)
                for h in range(H):
                    if h >= 6:
                        pe.wait_ge(sem("slab_ready"), h - 5)
                    pe.matmul(ps[:, 1 + h % 6, :], flip[:, :], flipped[:, h, :], start=True, stop=True)\
                      .then_inc(sem("slab_flipped"), 1)

            @block.scalar
            def _(act):
                for h in range(H):
                    act.wait_ge(sem("slab_flipped"), h + 1)
                    act.activation(slab[:, h, :], ps[:, 1 + h % 6, :], ACT.Copy).then_inc(sem("slab_ready"), 1)

            @block.sync
            def _(sp):
                sp.wait_ge(sem("rows_ready"), 1)
                sp.dma_start(scratch, rows[:, :]).then_inc(sem("rows_stored"), 16)
                sp.wait_ge(sem("rows_stored"), 16)
                sp.dma_start(flipped[:, :, :], bass.AP(scratch.tensor, scratch.offset,
                                                       [[1, P], [SLAB, H], [1, T]]))\
                  .then_inc(sem("slab_loaded"), 16)
                sp.wait_ge(sem("slab_loaded"), 16)
        core.fresh()

        NU = QT * H
        with nc.Fori(0, B) as b:
            with nc.Block() as block:
                @block.tensor
                def _(pe):
                    norm_pe(core, pe, xn)
                    pe.wait_ge(sem("xT_ready"), KC)
                    for g in range(G):
                        for c in range(KC):
                            last = pe.matmul(ps[:, 4 + g, :], w_q[:, c, g * P:(g + 1) * P], xT[:, c, :],
                                             start=(c == 0), stop=(c == KC - 1))
                        last.then_inc(sem("q_ready"), 1)
                    for g in range(G):
                        for c in range(KC):
                            last = pe.matmul(ps[:, g, :], w_k[:, c, g * P:(g + 1) * P], xT[:, c, :],
                                             start=(c == 0), stop=(c == KC - 1))
                        last.then_inc(sem("k_ready"), 1)
                    pe.wait_ge(sem("q_stored"), G)
                    for q in range(QT):
                        for c in range(KC):
                            last = pe.matmul(ps[:, 4 + q // 2, (q % 2) * D:(q % 2 + 1) * D],
                                             xT[:, c, q * P:(q + 1) * P], w_v[:, c, :],
                                             start=(c == 0), stop=(c == KC - 1))
                    last.then_inc(sem("v_ready"), 1)
                    pe.wait_ge(sem("k_stored"), G)

                    for n in range(NU + 12):
                        if n < NU:
                            q, h = divmod(n, H)
                            g, j = divmod(h, G)
                            if n >= 4:
                                pe.wait_ge(sem("scores_read"), n - 3)
                            s = slice(STRIP * j, STRIP * (j + 1))
                            pe.matmul(ps[:, j, 0:(q + 1) * P], qT[s, g, q * P:(q + 1) * P],
                                      kT[s, g, 0:(q + 1) * P], start=True, stop=True)\
                              .then_inc(sem("scores_ready"), 1)
                        if n == 0:
                            pe.wait_ge(sem("v_stored"), 1)
                        m = n - 3
                        if 0 <= m < NU:
                            pe.wait_ge(sem("probs_ready"), m + 1)
                            if m >= 2:
                                pe.wait_ge(sem("pT_act") if m % 2 == 0 else sem("pT_dve"), m // 2)
                            for k in range(m // H + 1):
                                last = pe.matmul(ps[:, 4 + m % 2, k * P:(k + 1) * P],
                                                 probs[:, m % PR, k * P:(k + 1) * P], core.ident[:, :],
                                                 start=True, stop=True)
                            last.then_inc(sem("p_turned"), 1)
                        m = n - 5
                        if 0 <= m < NU:
                            q, h = divmod(m, H)
                            g, j = divmod(h, G)
                            pe.wait_ge(sem("pT_act") if m % 2 == 0 else sem("pT_dve"), m // 2 + 1)
                            if h == 0 and q:
                                pe.wait_ge(sem("sums_copied"), q)
                            for k in range(q + 1):
                                last = pe.matmul(ps[STRIP * j:STRIP * (j + 1), 6, g * P:(g + 1) * P],
                                                 v[:, k, h, :], pT[:, m % 4, k * P:(k + 1) * P],
                                                 start=(k == 0), stop=(k == q))
                            last.then_inc(sem("values_summed"), 1)
                        if n - 6 >= 0 and (n - 6) % H == H - 1:
                            spread_pe(core, pe, (n - 6) // H, sums_T, spread)
                        if n - 11 >= 0 and (n - 11) % H == H - 1:
                            project_strips_pe(core, pe, (n - 11) // H, heads_T, w_o)

                @block.scalar
                def _(act):
                    norm_act(core, act, [xT[:, c, :] for c in range(KC)])
                    for g in range(G):
                        act.wait_ge(sem("q_ready"), g + 1)
                        act.activation(qT[:, g, :], ps[:, 4 + g, :], ACT.Identity, bias=b_qn[:, g:g + 1],
                                       scale=-DH ** -0.5).then_inc(sem("q_stored"), 1)
                    for g in range(G):
                        act.wait_ge(sem("k_ready"), g + 1)
                        act.activation(kT[:, g, :], ps[:, g, :], ACT.Identity, bias=b_k[:, g:g + 1])\
                            .then_inc(sem("k_stored"), 1)
                    for n in range(NU + 7):
                        if n < NU:
                            nk = (n // H + 1) * P
                            act.wait_ge(sem("scores_read"), n + 1)
                            pn = probs[:, n % PR, 0:nk]
                            act.activation(pn, pn, ACT.Exp, bias=top[:, n % PR:n % PR + 1], scale=-1.0)\
                                .then_inc(sem("probs_ready"), 1)
                        m = n - 3
                        if 0 <= m < NU and m % 2 == 0:
                            nk = (m // H + 1) * P
                            act.wait_ge(sem("p_turned"), m + 1)
                            if m >= 4:
                                act.wait_ge(sem("values_summed"), m - 3)
                            act.activation(pT[:, m % 4, 0:nk], ps[:, 4, 0:nk], ACT.Copy)\
                                .then_inc(sem("pT_act"), 1)
                        if n - 5 >= 0 and (n - 5) % H == H - 1:
                            copy_sums_act(core, act, (n - 5) // H, n - 4, sums_T)

                @block.gpsimd
                def _(pool):
                    norm_pool(core, pool, rstd)
                    normalise_pool(core, pool, sums_T, inv_den, heads_T)

                @block.vector
                def _(dve):
                    norm_dve(core, dve, b, xn, stats, mv, rstd)
                    add_bias_rows(core, dve, b, b_o)
                    dve.wait_ge(sem("v_ready"), 1)
                    dve.tensor_tensor(v[:, :, :, 0:DH],
                                      ps[:, 4:6, :].rearrange("p a (c h e) -> p (a c) h e", c=2, e=DH),
                                      b_v[:, :].rearrange("p (h e) -> p h e", e=DH).unsqueeze(1)
                                      .broadcast_to([P, QT, H, DH]), ALU.add).then_inc(sem("v_stored"), 1)
                    for n in range(NU + 12):
                        if n < NU:
                            q, h = divmod(n, H)
                            nk = (q + 1) * P
                            dve.wait_ge(sem("scores_ready"), n + 1)
                            if n >= PR:
                                dve.wait_ge(sem("p_turned"), n - PR + 1)
                            dve.tensor_tensor_reduce(probs[:, n % PR, 0:nk], ps[:, h % G, 0:nk],
                                                     slab[:, h, T - nk:T], 1.0, -NEG, ALU.add, ALU.min,
                                                     top[:, n % PR:n % PR + 1]).then_inc(sem("scores_read"), 1)
                        m = n - 3
                        if 0 <= m < NU and m % 2 == 1:
                            nk = (m // H + 1) * P
                            dve.wait_ge(sem("p_turned"), m + 1)
                            if m >= 4:
                                dve.wait_ge(sem("values_summed"), m - 3)
                            dve.tensor_copy(pT[:, m % 4, 0:nk], ps[:, 5, 0:nk]).then_inc(sem("pT_dve"), 1)
                        for g in range(G):
                            m = n - 6 - g
                            if m >= 0 and m % H == H - 1:
                                invert_den_dve(core, dve, m // H, g, inv_den)
                        if n - 11 >= 0 and (n - 11) % H == H - 1:
                            project_strips_dve(core, dve, b, (n - 11) // H)
            core.fresh()



CKT = (CTX + P - 1) // P
CLAST = CTX - (CKT - 1) * P


def key_rows(k):
    return P if k < CKT - 1 else CLAST


def cross_attn_stage(core, w):
    nc = core.nc
    ps, sem = core.ps, core.sem
    x = core.x
    with ExitStack() as ctx:
        def sb(name, shape, dt=F32):
            return ctx.enter_context(nc.sbuf_tensor("ca_" + name, shape, dt))

        w_q = sb("w_q", [P, KC, D])
        w_k = sb("w_k", [P, KC, D])
        w_v = sb("w_v", [P, KC, D])
        b_q = sb("b_q", [P, KC])
        b_k = sb("b_k", [P, KC])
        b_v = sb("b_v", [P, D])
        cT = sb("cT", [P, KC, CTX])
        kT = sb("kT", [P, KC, CTX])
        v = sb("v", [P, CKT, D])
        xn = sb("xn", [P, QT, D])
        xT = sb("xT", [P, KC, T])
        qT = sb("qT", [P, KC, T])
        probs = sb("probs", [P, 2, CTX])
        pT = sb("pT", [P, 2, CKT, P])
        top = sb("top", [P, 2])
        bar = sb("bar", [P, 2])
        den = sb("den", [P, 2])
        rden = sb("rden", [P, 2])
        stats = sb("stats", [P, QT, 6])
        mv = sb("mv", [P, QT, 2])
        rstd = sb("rstd", [P, QT])

        load_block(core, [
            (w_q[:, :, :], w["L1_xattn_Wq_T"].rearrange("(c p) e -> p c e", p=P)),
            (w_k[:, :, :], w["L1_xattn_Wk_T"].rearrange("(c p) e -> p c e", p=P)),
            (w_v[:, :, :], w["L1_xattn_Wv_T"].rearrange("(c p) e -> p c e", p=P)),
            (b_q[:, :], w["L1_xattn_bq_cols"]),
            (b_k[:, :], w["L1_xattn_bk_cols"]),
            (b_v[:, :], w["L1_xattn_bv"].partition_broadcast(P)),
        ])
        SCALE = D ** -0.5
        cuts = [(s, min(BANK, CTX - s)) for s in range(0, CTX, BANK)]
        NG = (CKT + 3) // 4
        with nc.Fori(0, B) as b:
            with nc.Block() as block:
                @block.sync
                def _(sp):
                    sp.dma_start(cT[:, :, :], w["ctx_T"][ds(b, 1), :, :]
                                 .rearrange("o (c p) k -> p (o c) k", p=P)).then_inc(sem("ctx_loaded"), 16)

                @block.tensor
                def _(pe):
                    pe.wait_ge(sem("ctx_loaded"), 16)
                    for n in range(KC * len(cuts)):
                        f, r = divmod(n, len(cuts))
                        s, k = cuts[r]
                        if n >= 4:
                            pe.wait_ge(sem("k_stored"), n - 3)
                        for c in range(KC):
                            last = pe.matmul(ps[:, 2 + n % 4, 0:k], w_k[:, c, f * P:(f + 1) * P],
                                             cT[:, c, s:s + k], start=(c == 0), stop=(c == KC - 1))
                        last.then_inc(sem("k_ready"), 1)
                    for k in range(CKT):
                        if k >= 2:
                            pe.wait_ge(sem("v_stored"), k - 1)
                        for c in range(KC):
                            last = pe.matmul(ps[0:key_rows(k), 6 + k % 2, 0:D],
                                             cT[:, c, k * P:k * P + key_rows(k)], w_v[:, c, :],
                                             start=(c == 0), stop=(c == KC - 1))
                        last.then_inc(sem("v_ready"), 1)
                    norm_pe(core, pe, xn)
                    pe.wait_ge(sem("xT_ready"), KC)
                    pe.wait_ge(sem("k_stored"), KC * len(cuts))
                    for f in range(KC):
                        for c in range(KC):
                            last = pe.matmul(ps[:, 4 + f, :], w_q[:, c, f * P:(f + 1) * P], xT[:, c, :],
                                             start=(c == 0), stop=(c == KC - 1))
                        last.then_inc(sem("q_ready"), 1)

                    def scores(q):
                        if q:
                            pe.wait_ge(sem("probs_ready"), q)
                        else:
                            pe.wait_ge(sem("q_stored"), KC)
                        for c in range(KC):
                            for r, (s, k) in enumerate(cuts):
                                last = pe.matmul(ps[:, r, 0:k], qT[:, c, q * P:(q + 1) * P],
                                                 kT[:, c, s:s + k], start=(c == 0), stop=(c == KC - 1))
                        last.then_inc(sem("scores_ready"), 1)

                    scores(0)
                    for q in range(QT):
                        pe.wait_ge(sem("probs_ready"), q + 1)
                        for g in range(NG):
                            if 2 * q + g // 2:
                                pe.wait_ge(sem("pT_act") if g % 2 == 0 else sem("pT_dve"), 2 * q + g // 2)
                            for k in range(4 * g, min(4 * g + 4, CKT)):
                                last = pe.transpose(ps[0:key_rows(k), 4 + g % 2, (k % 4) * P:(k % 4 + 1) * P],
                                                    probs[:, q % 2, k * P:k * P + key_rows(k)],
                                                    core.ident[:, :])
                            last.then_inc(sem("p_turned"), 1)
                        if q + 1 < QT:
                            scores(q + 1)
                        pe.wait_ge(sem("pT_act"), 2 * q + 2)
                        pe.wait_ge(sem("pT_dve"), 2 * q + 2)
                        if q == 0:
                            pe.wait_ge(sem("v_stored"), CKT)
                        else:
                            pe.wait_ge(sem("x_added"), q)
                        for k in range(CKT):
                            n = key_rows(k)
                            last = pe.matmul(ps[:, 6, 0:D], pT[0:n, q % 2, k, :], v[0:n, k, :],
                                             start=(k == 0), stop=(k == CKT - 1))
                        last.then_inc(sem("values_summed"), 1)

                @block.scalar
                def _(act):
                    for n in range(KC * len(cuts)):
                        f, r = divmod(n, len(cuts))
                        s, k = cuts[r]
                        act.wait_ge(sem("k_ready"), n + 1)
                        act.activation(kT[:, f, s:s + k], ps[:, 2 + n % 4, 0:k], ACT.Identity,
                                       bias=b_k[:, f:f + 1]).then_inc(sem("k_stored"), 1)
                    norm_act(core, act, [xT[:, c, :] for c in range(KC)])
                    for f in range(KC):
                        act.wait_ge(sem("q_ready"), f + 1)
                        act.activation(qT[:, f, :], ps[:, 4 + f, :], ACT.Identity, bias=b_q[:, f:f + 1])\
                            .then_inc(sem("q_stored"), 1)
                    for q in range(QT):
                        act.wait_ge(sem("top_ready"), q + 1)
                        if q >= 2:
                            act.wait_ge(sem("p_turned"), NG * (q - 1))
                        act.activation(probs[:, q % 2, :], ps[:, 0:4, :].rearrange("p r k -> p (r k)")[:, 0:CTX],
                                       ACT.Exp, bias=bar[:, q % 2:q % 2 + 1], scale=SCALE,
                                       accum_out=den[:, q % 2:q % 2 + 1]).then_inc(sem("probs_ready"), 1)
                        for g in (0, 2):
                            act.wait_ge(sem("p_turned"), NG * q + g + 1)
                            if q >= 2:
                                act.wait_ge(sem("values_summed"), q - 1)
                            act.activation(pT[:, q % 2, 4 * g:4 * g + 4, :],
                                           ps[:, 4, :].rearrange("k (g t) -> k g t", t=P), ACT.Copy)\
                                .then_inc(sem("pT_act"), 1)

                @block.gpsimd
                def _(pool):
                    norm_pool(core, pool, rstd)

                @block.vector
                def _(dve):
                    norm_dve(core, dve, b, xn, stats, mv, rstd)
                    for k in range(CKT):
                        n = key_rows(k)
                        dve.wait_ge(sem("v_ready"), k + 1)
                        dve.tensor_tensor(v[0:n, k, :], ps[0:n, 6 + k % 2, 0:D], b_v[0:n, :], ALU.add)\
                            .then_inc(sem("v_stored"), 1)

                    def largest(q):
                        dve.wait_ge(sem("scores_ready"), q + 1)
                        dve.tensor_reduce(top[:, q % 2:q % 2 + 1],
                                          ps[:, 0:4, :].rearrange("p r k -> p (r k)")[:, 0:CTX],
                                          AX.X, ALU.max).then_inc(sem("max_found"), 1)
                        dve.wait_ge(sem("max_found"), q + 1)
                        dve.tensor_scalar(bar[:, q % 2:q % 2 + 1], top[:, q % 2:q % 2 + 1], -SCALE, None,
                                          ALU.mult).then_inc(sem("top_ready"), 1)

                    largest(0)
                    for q in range(QT):
                        for g in (1, 3):
                            kt = 4 * g
                            dve.wait_ge(sem("p_turned"), NG * q + g + 1)
                            if q >= 2:
                                dve.wait_ge(sem("values_summed"), q - 1)
                            if kt + 4 <= CKT:
                                ins = dve.tensor_copy(pT[:, q % 2, kt:kt + 4, :],
                                                      ps[:, 5, :].rearrange("k (g t) -> k g t", t=P))
                            else:
                                ins = dve.tensor_copy(pT[0:CLAST, q % 2, kt, :], ps[0:CLAST, 5, 0:P])
                            ins.then_inc(sem("pT_dve"), 1)
                        if q + 1 < QT:
                            largest(q + 1)
                        dve.wait_ge(sem("probs_ready"), q + 1)
                        dve.reciprocal(rden[:, q % 2:q % 2 + 1], den[:, q % 2:q % 2 + 1])\
                            .then_inc(sem("den_ready"), 1)
                        dve.wait_ge(sem("den_ready"), q + 1)
                        dve.wait_ge(sem("values_summed"), q + 1)
                        xq = x[:, ds(b * QT + q, 1), :]
                        dve.scalar_tensor_tensor(out=xq, in0=ps[:, 6:7, 0:D], scalar=rden[:, q % 2:q % 2 + 1],
                                                 in1=xq, op0=ALU.mult, op1=ALU.add)\
                            .then_inc(sem("x_added"), 1)
            core.fresh()



NE = 64
FF = 128
NSH = 2
EG, EPG = 8, 8
TOPG, TOPE = 4, 8
ROUTE_SCALE = 2.5
EL = 8
EB = 16
HALF = B * T // 2
EW = 2 * KC * FF + D


def moe_stage(core, w, coef_rows):
    nc = core.nc
    ps, sem = core.ps, core.sem
    with ExitStack() as ctx:
        def sb(name, shape, dt=F32):
            return ctx.enter_context(nc.sbuf_tensor("moe_" + name, shape, dt))

        router = sb("router", [P, KC, NE])
        e_bias = sb("e_bias", [P, NE])
        earlier = sb("earlier", [P, EG, EG])
        slots = sb("slots", [P, EL, EW])
        coef = sb("coef", [P, EL, HALF])
        xT_all = sb("xT_all", [P, KC, B * T])
        WR = 3
        x_hi = sb("x_hi", [P, KC, HALF], F32R)
        x_lo = sb("x_lo", [P, KC, HALF], F32R)
        w_hi = sb("w_hi", [P, WR, EW], F32R)
        w_lo = sb("w_lo", [P, WR, EW], F32R)
        ones = sb("ones", [NSH, B * T])

        load_block(core, [
            (router[:, :, :], w["L0_ffn_router_T"].rearrange("(c p) e -> p c e", p=P)),
            (e_bias[:, :], w["L0_ffn_e_bias"].partition_broadcast(P)),
            (earlier[:, :, :], w["earlier"].partition_broadcast(P)),
        ])

        with ExitStack() as inner:
            def sb2(name, shape, dt=F32):
                return inner.enter_context(nc.sbuf_tensor("rt_" + name, shape, dt))

            xn = sb2("xn", [P, QT, D])
            xT = sb2("xT", [P, KC, T])
            score = sb2("score", [P, QT, NE])
            biased = sb2("biased", [P, QT, NE])
            best = sb2("best", [P, QT, EG, 8])
            gsum = sb2("gsum", [P, QT, EG])
            above = sb2("above", [P, QT, EG, EG])
            equal = sb2("equal", [P, QT, EG, EG])
            rank = sb2("rank", [P, QT, EG])
            top = sb2("top", [P, QT, 8])
            marked = sb2("marked", [P, QT, NE])
            total = sb2("total", [P, QT])
            coef_T = sb2("coef_T", [NE, T])
            stats = sb2("stats", [P, QT, 6])
            mv = sb2("mv", [P, QT, 2])
            rstd = sb2("rstd", [P, QT])
            with nc.Fori(0, B) as b:
                with nc.Block() as block:
                    @block.tensor
                    def _(pe):
                        norm_pe(core, pe, xn)
                        pe.wait_ge(sem("xT_ready"), KC)
                        for q in range(QT):
                            for c in range(KC):
                                last = pe.matmul(ps[:, 2, q * NE:(q + 1) * NE], xT[:, c, q * P:(q + 1) * P],
                                                 router[:, c, :], start=(c == 0), stop=(c == KC - 1))
                        last.then_inc(sem("logits_ready"), 1)
                        pe.wait_ge(sem("coef_ready"), 1)
                        for q in range(QT):
                            last = pe.transpose(ps[0:NE, 3, q * P:(q + 1) * P], marked[:, q, :],
                                                core.ident[:, :])
                        last.then_inc(sem("coef_turned"), 1)

                    @block.scalar
                    def _(act):
                        norm_act(core, act, [xT[:, c, :] for c in range(KC)])
                        act.wait_ge(sem("logits_ready"), 1)
                        act.activation(score[:, :, :], ps[:, 2, 0:QT * NE].rearrange("p (q e) -> p q e", e=NE),
                                       ACT.Sigmoid).then_inc(sem("score_ready"), 1)
                        act.wait_ge(sem("coef_turned"), 1)
                        act.activation(coef_T[:, :], ps[0:NE, 3, :], ACT.Copy).then_inc(sem("coef_T_ready"), 1)

                    @block.gpsimd
                    def _(pool):
                        norm_pool(core, pool, rstd)
                        pool.wait_ge(sem("xT_ready"), KC)
                        pool.tensor_copy(xT_all[:, :, ds(b * T, T)], xT[:, :, :])

                    @block.sync
                    def _(sp):
                        sp.wait_ge(sem("coef_T_ready"), 1)
                        sp.dma_start(coef_rows[0:NE, ds(b * T, T)], coef_T[:, :]).then_inc(sem("coef_stored"), 16)
                        sp.wait_ge(sem("coef_stored"), 16)

                    @block.vector
                    def _(dve):
                        norm_dve(core, dve, b, xn, stats, mv, rstd)
                        chain = Chain(dve, sem("dve_chain"))
                        dve.wait_ge(sem("score_ready"), 1)
                        chain(dve.tensor_tensor(biased[:, :, :], score[:, :, :],
                                                e_bias[:, :].unsqueeze(1).broadcast_to([P, QT, NE]), ALU.add))
                        for q in range(QT):
                            for g in range(EG):
                                last = dve.max(best[:, q, g, :], biased[:, q, g * EPG:(g + 1) * EPG])
                        chain(last)
                        chain(dve.tensor_tensor(gsum[:, :, :], best[:, :, :, 0], best[:, :, :, 1], ALU.add))
                        mine = gsum[:, :, :].unsqueeze(3).broadcast_to([P, QT, EG, EG])
                        theirs = gsum[:, :, :].unsqueeze(2).broadcast_to([P, QT, EG, EG])
                        dve.tensor_tensor(above[:, :, :, :], theirs, mine, ALU.is_gt)
                        chain(dve.tensor_tensor(equal[:, :, :, :], theirs, mine, ALU.is_equal))
                        chain(dve.tensor_tensor(equal[:, :, :, :], equal[:, :, :, :],
                                                earlier[:, :, :].unsqueeze(1).broadcast_to([P, QT, EG, EG]),
                                                ALU.mult))
                        chain(dve.tensor_tensor(above[:, :, :, :], above[:, :, :, :], equal[:, :, :, :], ALU.add))
                        chain(dve.tensor_reduce(rank[:, :, :], above[:, :, :, :], AX.X, ALU.add))
                        chain(dve.tensor_scalar(rank[:, :, :], rank[:, :, :], TOPG - 0.5, None, ALU.is_lt))
                        chain(dve.tensor_tensor(biased[:, :, :].rearrange("p q (g e) -> p q g e", e=EPG),
                                                biased[:, :, :].rearrange("p q (g e) -> p q g e", e=EPG),
                                                rank[:, :, :].unsqueeze(3).broadcast_to([P, QT, EG, EPG]),
                                                ALU.mult))
                        for q in range(QT):
                            last = dve.max(top[:, q, :], biased[:, q, :])
                        chain(last)
                        for q in range(QT):
                            last = dve.match_replace(marked[:, q, :], top[:, q, :], biased[:, q, :], NEG)
                        chain(last)
                        chain(dve.tensor_tensor(marked[:, :, :], marked[:, :, :], biased[:, :, :], ALU.not_equal))
                        chain(dve.tensor_tensor(marked[:, :, :], marked[:, :, :], score[:, :, :], ALU.mult))
                        chain(dve.tensor_reduce(total[:, :], marked[:, :, :], AX.X, ALU.add))
                        chain(dve.tensor_scalar(total[:, :], total[:, :], 1e-20, None, ALU.add))
                        chain(dve.reciprocal(total[:, :], total[:, :]))
                        chain(dve.tensor_tensor(marked[:, :, :], marked[:, :, :],
                                                total[:, :].unsqueeze(2).broadcast_to([P, QT, NE]), ALU.mult))
                        dve.tensor_scalar(marked[:, :, :], marked[:, :, :], ROUTE_SCALE, None, ALU.mult)\
                            .then_inc(sem("coef_ready"), 1)
                core.fresh()

        gate = sb("gate", [P, 2, T])
        prod = sb("prod", [P, 2, T])
        hid = sb("hid", [P, 2, T])
        HR = 3
        hid_hi = sb("hid_hi", [P, HR, T], F32R)
        hid_lo = sb("hid_lo", [P, HR, T], F32R)
        experts = w["L0_ffn_experts"]
        KEEP = EL - 2
        slot_loaded = [sem(f"slot_{i}_loaded") for i in range(EL)]

        def load_slot(sp, half, e, slot):
            loaded = slot_loaded[slot]
            sp.dma_start(slots[:, slot:slot + 1, :], experts[ds(e, 1), :, :].rearrange("o p n -> p o n"))\
              .then_inc(loaded, 16)
            row = bass.AP(coef_rows.tensor, coef_rows.offset, [[0, P], [B * T, NE + EL], [1, B * T]])
            sp.dma_start(coef[:, slot:slot + 1, :], row[:, ds(e, 1), ds(half * HALF, HALF)])\
              .then_inc(loaded, 16)

        def expert_block(half, step, n_experts, shared):
            units = [(e, t) for e in range(n_experts) for t in range(HALF // T)]
            with nc.Block() as block:
                @block.sync
                def _(sp):
                    if shared:
                        return
                    for e in range(KEEP, EL):
                        load_slot(sp, half, step * EB + e, e)
                    for e in range(EL, EB + KEEP):
                        sp.wait_ge(sem("w_lo_ready"), e - EL + 1)
                        sp.wait_ge(sem("hid_ready"), (e - EL + 1) * (HALF // T))
                        load_slot(sp, half, step * EB + e, e % EL)
                    for i in range(KEEP):
                        sp.wait_ge(slot_loaded[i], 32 * (EB // EL))

                TB = HALF // T

                @block.tensor
                def _(pe):
                    def down(m):
                        e, t = units[m]
                        pe.wait_ge(sem("hid_lo_ready"), m + 1)
                        wd = slice(2 * KC * FF, EW)
                        for q in range(QT):
                            i = t * QT + q
                            hs = slice(q * P, (q + 1) * P)
                            for h, v in ((hid_hi, w_hi), (hid_hi, w_lo), (hid_lo, w_hi)):
                                last = pe.matmul(ps[:, i // 2, (i % 2) * D:(i % 2 + 1) * D],
                                                 h[:, m % HR, hs], v[:, e % WR, wd],
                                                 start=False, stop=False, skip_group_check=True)
                        last.then_inc(sem("unit_done"), 1)

                    for m, (e, t) in enumerate(units):
                        if t == 0:
                            pe.wait_ge(sem("w_lo_ready"), e + 1)
                        for i in range(2):
                            if m >= 2:
                                pe.wait_ge(sem("gate_ready") if i == 0 else sem("prod_ready"), m - 1)
                            n = 0
                            for c in range(KC):
                                ws = slice((i * KC + c) * FF, (i * KC + c + 1) * FF)
                                xs = slice(t * T, (t + 1) * T)
                                for v, y in ((w_hi, x_hi), (w_hi, x_lo), (w_lo, x_hi)):
                                    last = pe.matmul(ps[:, 4 + 2 * (m % 2) + i, :], v[:, e % WR, ws], y[:, c, xs],
                                                     start=(n == 0), stop=(n == 3 * KC - 1))
                                    n += 1
                            last.then_inc(sem("g_ready") if i == 0 else sem("u_ready"), 1)
                        if m >= 2:
                            down(m - 2)
                    down(len(units) - 2)
                    down(len(units) - 1)

                @block.scalar
                def _(act):
                    def split(e):
                        loads = e // EL + (e % EL >= KEEP)
                        if loads:
                            act.wait_ge(slot_loaded[e % EL], 32 * loads)
                        if e >= WR:
                            act.wait_ge(sem("unit_done"), (e - WR + 1) * TB)
                        act.activation(w_hi[:, e % WR, :], slots[:, e % EL, :], ACT.Copy).then_inc(sem("w_hi_ready"), 1)

                    def high(m):
                        act.wait_ge(sem("hid_ready"), m + 1)
                        if m >= HR:
                            act.wait_ge(sem("unit_done"), m - HR + 1)
                        act.activation(hid_hi[:, m % HR, :], hid[:, m % 2, :], ACT.Copy)\
                            .then_inc(sem("hid_hi_ready"), 1)

                    split(0)
                    for m, (e, t) in enumerate(units):
                        act.wait_ge(sem("g_ready"), m + 1)
                        if m >= 2:
                            act.wait_ge(sem("prod_ready"), m - 1)
                        act.activation(gate[:, m % 2, :], ps[:, 4 + 2 * (m % 2), :], ACT.Silu)\
                            .then_inc(sem("gate_ready"), 1)
                        if m:
                            high(m - 1)
                        if t == 0 and e < n_experts - 1:
                            split(e + 1)
                    high(len(units) - 1)

                @block.vector
                def _(dve):
                    def split(e):
                        dve.wait_ge(sem("w_hi_ready"), e + 1)
                        dve.tensor_tensor(w_lo[:, e % WR, :], slots[:, e % EL, :], w_hi[:, e % WR, :].bitcast(F32),
                                          ALU.subtract).then_inc(sem("w_lo_ready"), 1)

                    def low(m):
                        dve.wait_ge(sem("hid_hi_ready"), m + 1)
                        dve.tensor_tensor(hid_lo[:, m % HR, :], hid[:, m % 2, :],
                                          hid_hi[:, m % HR, :].bitcast(F32), ALU.subtract)\
                            .then_inc(sem("hid_lo_ready"), 1)

                    split(0)
                    for m, (e, t) in enumerate(units):
                        dve.wait_ge(sem("u_ready"), m + 1)
                        dve.wait_ge(sem("gate_ready"), m + 1)
                        if m >= 2:
                            dve.wait_ge(sem("hid_ready"), m - 1)
                        dve.tensor_tensor(prod[:, m % 2, :], gate[:, m % 2, :], ps[:, 5 + 2 * (m % 2), :],
                                          ALU.mult).then_inc(sem("prod_ready"), 1)
                        if m:
                            low(m - 1)
                        if t == 0 and e < n_experts - 1:
                            split(e + 1)
                    low(len(units) - 1)

                @block.gpsimd
                def _(pool):
                    for m, (e, t) in enumerate(units):
                        pool.wait_ge(sem("prod_ready"), m + 1)
                        if m >= 2:
                            pool.wait_ge(sem("hid_lo_ready"), m - 1)
                        if shared:
                            ins = pool.tensor_copy(hid[:, m % 2, :], prod[:, m % 2, :])
                        else:
                            ins = pool.tensor_tensor(hid[:, m % 2, :], prod[:, m % 2, :],
                                                     coef[:, e % EL, t * T:(t + 1) * T], ALU.mult)
                        ins.then_inc(sem("hid_ready"), 1)
            core.fresh()

        with nc.Block() as block:
            @block.vector
            def _(dve):
                dve.memset(ones[:, :], 1.0).then_inc(sem("ones_set"), 1)

            @block.sync
            def _(sp):
                sp.wait_ge(sem("ones_set"), 1)
                for e in range(NE, NE + EL, NSH):
                    sp.dma_start(coef_rows[e:e + NSH, :], ones[:, :]).then_inc(sem("ones_stored"), 16)
                sp.wait_ge(sem("ones_stored"), 16 * EL // NSH)
        core.fresh()

        with nc.Fori(0, 2) as half:
            with nc.Block() as block:
                @block.sync
                def _(sp):
                    for e in range(KEEP):
                        load_slot(sp, half, e, e)
                    for i in range(KEEP):
                        sp.wait_ge(slot_loaded[i], 32)

                @block.scalar
                def _(act):
                    act.activation(x_hi[:, :, :], xT_all[:, :, ds(half * HALF, HALF)], ACT.Copy)\
                        .then_inc(sem("x_hi_ready"), 1)

                @block.vector
                def _(dve):
                    dve.memset(ps[:, 0:4, :], 0.0)
                    dve.wait_ge(sem("x_hi_ready"), 1)
                    dve.tensor_tensor(x_lo[:, :, :], xT_all[:, :, ds(half * HALF, HALF)],
                                      x_hi[:, :, :].bitcast(F32), ALU.subtract)
            core.fresh()
            with nc.Fori(0, NE // EB) as step:
                expert_block(half, step, EB, False)
            expert_block(half, None, NSH, True)
            with nc.Block() as block:
                @block.vector
                def _(dve):
                    xh = core.x[:, ds(half * (NT // 2), NT // 2), :]
                    dve.tensor_tensor(xh, xh, ps[:, 0:4, :].rearrange("p a (c d) -> p (a c) d", d=D), ALU.add)
            core.fresh()



PH = 8
NK = 64
DK = 128
PK = 8
NSLOT = PH * PK
ET = NK * NK // P
RMS_EPS = 1e-6
HT = T // 2
CG = 16
RN = HT // (2 * CG)
ROWS = 3
PARTS = 3


def peer_stage(core, w):
    nc = core.nc
    ps, sem = core.ps, core.sem
    with ExitStack() as ctx:
        def sb(name, shape, dt=F32):
            return ctx.enter_context(nc.sbuf_tensor("pr_" + name, shape, dt))

        w_sim = sb("w_sim", [P, KC, 2 * PH * NK])
        down = sb("down", [P, KC, ET, P])
        up = sb("up", [P, ET, D])
        norm_w = sb("norm_w", [P, D])
        iota = sb("iota", [P, P])
        act_h = sb("act_h", [P, ET, HT])
        hot_part = sb("hot_part", [P, 2, CG, P], BF16)
        hot_tile = sb("hot_tile", [P, 2, CG, ET], BF16)
        hot_w = sb("hot_w", [P, 2, PARTS, CG, ET], BF16)
        w_parts = sb("w_parts", [P, PARTS, QT, NK], BF16)
        w_rest = sb("w_rest", [P, QT, NK])
        xT = sb("xT", [P, KC, T])
        xT_old = sb("xT_old", [P, KC, T])
        turned = sb("turned", [P, ROWS, QT, NK])
        turned_old = sb("turned_old", [P, 2, QT, NK])
        sims = sb("sims", [P, QT, PH, 2, NK])
        key1 = sb("key1", [P, NSLOT])
        key2 = sb("key2", [P, NSLOT])
        upper = sb("upper", [P, NSLOT])
        lists = sb("lists", [P, ROWS, NSLOT])
        twice = sb("twice", [P, ROWS, 2, NSLOT])
        s8 = sb("s8", [P, PH, 2, PK])
        i8 = sb("i8", [P, PH, 2, PK], U32)
        i8f = sb("i8f", [P, PH, 2, PK])
        sums = sb("sums", [P, PH, PK * PK])
        f8 = sb("f8", [P, PH, PK])
        pk = sb("pk", [P, PH, PK], U32)
        ab = sb("ab", [P, 2, NSLOT], U32)
        abf = sb("abf", [P, 2, NSLOT])
        pick = sums[:, :, :].rearrange("p h (k a) -> p (h k) a", a=PK)
        stats = sb("stats", [P, QT, 6])
        mv = sb("mv", [P, QT, 2])
        rstd = sb("rstd", [P, QT])
        ssq = sb("ssq", [P, QT])
        xn = sims[:, 0, :, :, :].rearrange("p h a k -> p (h a k)").rearrange("p (q d) -> p q d", d=D)
        square = sims[:, 1, 0:2, :, :].rearrange("p h a k -> p (h a k)")

        load_block(core, [
            (down[:, :, :, :], w["L1_ffn_down_T"].rearrange("(c p) (i e) -> p c i e", p=P, e=P)),
            (up[:, :, :], w["L1_ffn_up"]),
            (norm_w[:, :], w["L1_ffn_norm_w"].partition_broadcast(P)),
            (iota[:, :], w["iota"].partition_broadcast(P)),
        ])

        with ExitStack() as once:
            w_q = once.enter_context(nc.sbuf_tensor("pr_w_q", [P, 2 * PH, D], F32))
            keys = once.enter_context(nc.sbuf_tensor("pr_keys", [P, 2 * PH, NK], F32))
            load_block(core, [
                (w_q[:, :, :], w["L1_ffn_w_q"].rearrange("(s p) d -> p s d", p=P)),
                (keys[:, :, :], w["L1_ffn_keys_T"]),
            ])
            with nc.Block() as block:
                @block.tensor
                def _(pe):
                    for c in range(KC):
                        for s in range(2 * PH):
                            last = pe.matmul(ps[:, 2 * c + s // PH, (s % PH) * NK:(s % PH + 1) * NK],
                                             w_q[:, s, c * P:(c + 1) * P], keys[:, s, :], start=True, stop=True)
                            if s % PH == PH - 1:
                                last.then_inc(sem("w_sim_ready"), 1)

                @block.scalar
                def _(act):
                    for i in range(2 * KC):
                        act.wait_ge(sem("w_sim_ready"), i + 1)
                        act.activation(w_sim[:, i // 2, (i % 2) * BANK:(i % 2 + 1) * BANK], ps[:, i, :], ACT.Copy)
            core.fresh()

        def rms(dve, chain):
            for q in range(QT):
                chain(dve.tensor_tensor_reduce(square, xn[:, q, :], xn[:, q, :], 1.0, 0.0,
                                               ALU.mult, ALU.add, ssq[:, q:q + 1]))
            dve.tensor_scalar(ssq[:, :], ssq[:, :], 1.0 / D, RMS_EPS, ALU.mult, ALU.add)\
                .then_inc(sem("ssq_ready"), 1)
            dve.wait_ge(sem("rms_ready"), 1)
            for q in range(QT):
                dve.scalar_tensor_tensor(out=xn[:, q, :], in0=xn[:, q, :], scalar=ssq[:, q:q + 1],
                                         in1=norm_w[:, :], op0=ALU.mult, op1=ALU.mult)\
                    .then_inc(sem("xn_ready"), 1)

        NDOWN = ET // 2
        EARLY = QT - 1

        def weight_bank(r, a):
            return (6, 4)[r % 2] + a

        def peer_block(new, old):
            with nc.Block() as block:
                @block.tensor
                def _(pe):
                    def down_products(hf):
                        for n in range(NDOWN):
                            m = hf * NDOWN + n
                            if m >= 2:
                                pe.wait_ge(sem("gelu_done"), m - 1)
                            for i in range(2):
                                for c in range(KC):
                                    last = pe.matmul(ps[:, 4 + n % 2, i * HT:(i + 1) * HT],
                                                     down[:, c, 2 * n + i, :], xT_old[:, c, hf * HT:(hf + 1) * HT],
                                                     start=(c == 0), stop=(c == KC - 1))
                            last.then_inc(sem("down_ready"), 1)

                    def outer(r):
                        if r % RN == 1:
                            pe.wait_ge(sem("gelu_done"), (r // RN + 1) * NDOWN)
                        pe.wait_ge(sem("hot_part_ready"), r + 1)
                        pe.wait_ge(sem("hot_w_ready"), r + 1)
                        if r >= 2:
                            pe.wait_ge(sem("weighted"), 2 * (r - 1))
                        for t in range(CG):
                            for part in range(PARTS):
                                for a in range(2):
                                    s = slice(NK * a, NK * (a + 1))
                                    last = pe.matmul(ps[:, weight_bank(r, a), t * ET:(t + 1) * ET],
                                                     hot_part[s, r % 2, t, :], hot_w[s, r % 2, part, t, :],
                                                     start=(part == 0), stop=(part == PARTS - 1))
                        last.then_inc(sem("outer_ready"), 1)

                    def up_products(hf):
                        pe.wait_ge(sem("weighted"), 2 * RN * (hf + 1))
                        if hf:
                            pe.wait_ge(sem("x_added"), 1)
                        for q in range(2):
                            for i in range(ET):
                                last = pe.matmul(ps[:, 3, q * D:(q + 1) * D], act_h[:, i, q * P:(q + 1) * P],
                                                 up[:, i, :], start=(i == 0), stop=(i == ET - 1))
                        last.then_inc(sem("up_ready"), 1)

                    def similarities(q):
                        if q:
                            pe.wait_ge(sem("sims_stored"), 2 * q)
                        for a in range(2):
                            for c in range(KC):
                                last = pe.matmul(ps[:, a, :], xT[:, c, q * P:(q + 1) * P],
                                                 w_sim[:, c, a * BANK:(a + 1) * BANK],
                                                 start=(c == 0), stop=(c == KC - 1))
                            last.then_inc(sem("sims_ready"), 1)

                    def turn_lists(q):
                        pe.wait_ge(sem("lists_ready"), q + 1)
                        if q:
                            pe.wait_ge(sem("turned_stored"), 2 * q)
                        for i in range(ROWS):
                            last = pe.transpose(ps[:, 2, i * P:(i + 1) * P],
                                                twice[:, i, :, :].rearrange("p a s -> p (a s)"),
                                                core.ident[:, :])
                        last.then_inc(sem("lists_turned"), 1)

                    if old is not None:
                        down_products(0)
                    if new is not None:
                        norm_pe(core, pe, xn)
                        pe.wait_ge(sem("xT_ready"), KC)
                    if old is not None:
                        outer(0)
                    if new is not None:
                        for q in range(QT):
                            similarities(q)
                    if old is not None:
                        for r in range(1, RN):
                            outer(r)
                        up_products(0)
                        down_products(1)
                    if new is not None:
                        for q in range(EARLY):
                            turn_lists(q)
                    if old is not None:
                        for r in range(RN, 2 * RN):
                            outer(r)
                        up_products(1)
                    if new is not None:
                        for q in range(EARLY, QT):
                            turn_lists(q)

                @block.scalar
                def _(act):
                    def gelu(hf):
                        if hf:
                            act.wait_ge(sem("up_ready"), 1)
                        for n in range(NDOWN):
                            act.wait_ge(sem("down_ready"), hf * NDOWN + n + 1)
                            act.activation(act_h[:, 2 * n:2 * n + 2, :],
                                           ps[:, 4 + n % 2, :].rearrange("p (i t) -> p i t", i=2), ACT.Gelu)\
                                .then_inc(sem("gelu_done"), 1)

                    def store_turned(q):
                        act.wait_ge(sem("lists_turned"), q + 1)
                        for a in range(2):
                            s = slice(NK * a, NK * (a + 1))
                            act.activation(turned[s, :, q, :],
                                           ps[s, 2, 0:ROWS * P].rearrange("p (i t) -> p i t", i=ROWS)[:, :, s],
                                           ACT.Copy).then_inc(sem("turned_stored"), 1)

                    if old is not None:
                        gelu(0)
                    if new is not None:
                        norm_act(core, act, [xT[:, c, :] for c in range(KC)])
                        for q in range(QT):
                            for a in range(2):
                                act.wait_ge(sem("sims_ready"), 2 * q + a + 1)
                                act.activation(sims[:, q, a * PH // 2:(a + 1) * PH // 2, :, :],
                                               ps[:, a, :].rearrange("p (h a k) -> p h a k", a=2, k=NK),
                                               ACT.Copy).then_inc(sem("sims_stored"), 1)
                    if old is not None:
                        gelu(1)
                    if new is not None:
                        for q in range(QT):
                            store_turned(q)

                @block.gpsimd
                def _(pool):
                    if new is not None:
                        norm_pool(core, pool, rstd)
                        pool.wait_ge(sem("ssq_ready"), 1)
                        pool.tensor_tensor(ssq[:, :], ssq[:, :], core.neg_half[:, :], ALU.pow)\
                            .then_inc(sem("rms_ready"), 1)
                    if old is not None:
                        for r in range(2 * RN):
                            q, c = divmod(r, RN // 2)
                            pool.wait_ge(sem("hot_tile_ready"), r + 1)
                            if r >= 2:
                                pool.wait_ge(sem("outer_ready"), r - 1)
                            for part in range(PARTS):
                                last = pool.tensor_tensor(
                                    hot_w[:, r % 2, part, :, :], hot_tile[:, r % 2, :, :],
                                    w_parts[:, part, q, c * CG:(c + 1) * CG].unsqueeze(2)
                                    .broadcast_to([P, CG, ET]), ALU.mult)
                            last.then_inc(sem("hot_w_ready"), 1)
                    if new is not None:
                        if old is not None:
                            pool.wait_ge(sem("down_ready"), 2 * NDOWN)
                        pool.wait_ge(sem("xT_ready"), KC)
                        pool.tensor_copy(xT_old[:, :, :], xT[:, :, :])
                        pool.wait_ge(sem("turned_stored"), 2 * QT)
                        if old is not None:
                            pool.wait_ge(sem("hot_w_ready"), 2 * RN)
                            pool.wait_ge(sem("hot_part_ready"), 2 * RN)
                        pool.tensor_copy(turned_old[:, :, :, :], turned[:, 0:2, :, :])
                        chain = Chain(pool, sem("parts_chain"))
                        chain(pool.tensor_copy(w_parts[:, 0, :, :], turned[:, 2, :, :]))
                        chain(pool.tensor_tensor(w_rest[:, :, :], turned[:, 2, :, :], w_parts[:, 0, :, :],
                                                 ALU.subtract))
                        chain(pool.tensor_copy(w_parts[:, 1, :, :], w_rest[:, :, :]))
                        pool.tensor_tensor(w_parts[:, 2, :, :], w_rest[:, :, :], w_parts[:, 1, :, :], ALU.subtract)

                @block.vector
                def _(dve):
                    chain = Chain(dve, sem("dve_chain"))

                    def make_lists(q):
                        dve.wait_ge(sem("sims_stored"), 2 * (q + 1))
                        for h in range(PH):
                            for a in range(2):
                                last = dve.max(s8[:, h, a, :], sims[:, q, h, a, :])
                        chain(last)
                        for h in range(PH):
                            for a in range(2):
                                last = dve.max_index(i8[:, h, a, :], s8[:, h, a, :], sims[:, q, h, a, :])
                        chain(last)
                        dve.tensor_copy(i8f[:, :, :, :], i8[:, :, :, :])
                        chain(dve.tensor_tensor(
                            sums[:, :, :].rearrange("p h (a b) -> p h a b", a=PK),
                            s8[:, :, 0, :].unsqueeze(3).broadcast_to([P, PH, PK, PK]),
                            s8[:, :, 1, :].unsqueeze(2).broadcast_to([P, PH, PK, PK]), ALU.add))
                        for h in range(PH):
                            last = dve.max(f8[:, h, :], sums[:, h, :])
                        chain(last)
                        for h in range(PH):
                            last = dve.max_index(pk[:, h, :], f8[:, h, :], sums[:, h, :])
                        chain(last)
                        pkf = pk[:, :, :].rearrange("p h k -> p (h k)")
                        dve.tensor_scalar(ab[:, 0, :], pkf, 3, None, ALU.logical_shift_right)
                        chain(dve.tensor_scalar(ab[:, 1, :], pkf, PK - 1, None, ALU.bitwise_and))
                        chain(dve.tensor_copy(abf[:, :, :], ab[:, :, :]))
                        for a in range(2):
                            chain(dve.tensor_tensor(pick,
                                                    abf[:, a, :].unsqueeze(2).broadcast_to([P, NSLOT, PK]),
                                                    iota[:, 0:PK].unsqueeze(1).broadcast_to([P, NSLOT, PK]),
                                                    ALU.is_equal))
                            p4 = pick.rearrange("p (h k) a -> p h k a", h=PH)
                            chain(dve.tensor_tensor(p4, p4, i8f[:, :, a, :].unsqueeze(2)
                                                    .broadcast_to([P, PH, PK, PK]), ALU.mult))
                            chain(dve.tensor_reduce((key1, key2)[a][:, :], pick, AX.X, ALU.add))
                        dve.tensor_scalar(lists[:, 2, :], f8[:, :, :].rearrange("p h k -> p (h k)"),
                                          0.0, None, ALU.max)
                        chain(dve.tensor_scalar(upper[:, :], key1[:, :], ET - 0.5, None, ALU.is_ge))
                        dve.scalar_tensor_tensor(out=lists[:, 0, :], in0=upper[:, :], scalar=float(NK),
                                                 in1=key2[:, :], op0=ALU.mult, op1=ALU.add)
                        chain(dve.scalar_tensor_tensor(out=lists[:, 1, :], in0=upper[:, :], scalar=-float(ET),
                                                       in1=key1[:, :], op0=ALU.mult, op1=ALU.add))
                        if q:
                            dve.wait_ge(sem("lists_turned"), q)
                        dve.tensor_copy(twice[:, :, :, :],
                                        lists[:, :, :].unsqueeze(2).broadcast_to([P, ROWS, 2, NSLOT]))\
                            .then_inc(sem("lists_ready"), 1)

                    def one_hot(r):
                        q, c = divmod(r, RN // 2)
                        cols = slice(c * CG, (c + 1) * CG)
                        if r >= 2:
                            dve.wait_ge(sem("hot_w_ready"), r - 1)
                            dve.wait_ge(sem("outer_ready"), r - 1)
                        dve.tensor_tensor(hot_tile[:, r % 2, :, :], iota[:, 0:ET].unsqueeze(1).broadcast_to([P, CG, ET]),
                                          turned_old[:, 1, q, cols].unsqueeze(2).broadcast_to([P, CG, ET]),
                                          ALU.is_equal).then_inc(sem("hot_tile_ready"), 1)
                        dve.tensor_tensor(hot_part[:, r % 2, :, :], iota[:, :].unsqueeze(1).broadcast_to([P, CG, P]),
                                          turned_old[:, 0, q, cols].unsqueeze(2).broadcast_to([P, CG, P]),
                                          ALU.is_equal).then_inc(sem("hot_part_ready"), 1)

                    def weigh(hf):
                        one_hot(hf * RN)
                        for n in range(RN):
                            r = hf * RN + n
                            if n < RN - 1:
                                one_hot(r + 1)
                            if n == 0:
                                dve.wait_ge(sem("gelu_done"), (hf + 1) * NDOWN)
                            dve.wait_ge(sem("outer_ready"), r + 1)
                            for a in range(2):
                                t0 = (n // (RN // 2)) * P + a * NK + (n % (RN // 2)) * CG
                                hs = act_h[:, :, t0:t0 + CG].rearrange("p i t -> p t i")
                                dve.tensor_tensor(hs, hs, ps[:, weight_bank(r, a), :].rearrange("p (t i) -> p t i", i=ET),
                                                  ALU.mult).then_inc(sem("weighted"), 1)

                    def add_x(hf):
                        dve.wait_ge(sem("up_ready"), hf + 1)
                        xq = core.x[:, ds(old * QT + 2 * hf, 2), :]
                        dve.tensor_tensor(xq, xq, ps[:, 3, :].rearrange("p (q d) -> p q d", q=2), ALU.add)\
                            .then_inc(sem("x_added"), 1)

                    if new is not None:
                        norm_dve(core, dve, new, xn, stats, mv, rstd, extra=lambda c: rms(dve, c))
                    if old is not None:
                        weigh(0)
                    if new is not None:
                        make_lists(0)
                    if old is not None:
                        add_x(0)
                    if new is not None:
                        for q in range(1, EARLY):
                            make_lists(q)
                    if old is not None:
                        weigh(1)
                    if new is not None:
                        for q in range(EARLY, QT):
                            make_lists(q)
                    if old is not None:
                        add_x(1)
            core.fresh()

        peer_block(0, None)
        with nc.Fori(1, B) as b:
            peer_block(b, b - 1)
        peer_block(None, B - 1)




def build(nc, w, out, stages):
    with ExitStack() as ctx:
        core = Core(nc, ctx)
        scratch = {
            "xdbl": nc.dram_tensor("xdbl_scratch", (2 * DS, T), F32, kind="Internal").ap(),
            "coef": nc.dram_tensor("coef_scratch", (NE + EL, B * T), F32, kind="Internal").ap(),
            "rel_rows": nc.dram_tensor("rel_rows_scratch", (H, SLAB), F32, kind="Internal").ap(),
        }
        load_block(core, [
            (core.x[:, :, :], w["x"].rearrange("b (q p) d -> p (b q) d", p=P)),
            (core.ident[:, :], w["ident"]),
        ])
        with nc.Block() as block:
            @block.vector
            def _(dve):
                dve.memset(core.neg_half[:, :], -0.5)
        for s in stages:
            if s == "ssm":
                ssm_stage(core, w, scratch["xdbl"])
            if s == "gather_attn":
                gather_attn_stage(core, w)
            if s == "moe":
                moe_stage(core, w, scratch["coef"])
            if s == "peer":
                peer_stage(core, w)
            if s == "self_attn":
                self_attn_stage(core, w, scratch["rel_rows"])
            if s == "cross_attn":
                cross_attn_stage(core, w)
        stored = core.sem("out_stored")
        with nc.Block() as block:
            @block.sync
            def _(sp):
                sp.dma_start(out.rearrange("b (q p) d -> p (b q) d", p=P), core.x[:, :, :]).then_inc(stored, 16)
                sp.wait_ge(stored, 16)


def layouts(inputs):
    import numpy as np

    w = {k: np.ascontiguousarray(v) for k, v in inputs.items()}
    out = {"ident": np.eye(P, dtype=np.float32), "x": w["x"]}
    def columns(v):
        return np.ascontiguousarray(v.reshape(-1, P).T)

    for k in ("conv_w", "A_log"):
        out["L0_attn_" + k] = w["L0_attn_" + k]
    for k in ("conv_b", "D_param", "b_dt"):
        out["L0_attn_" + k + "_cols"] = columns(w["L0_attn_" + k])
    for k in ("W_in", "W_dt", "W_x", "W_out"):
        out["L0_attn_" + k + "_T"] = np.ascontiguousarray(w["L0_attn_" + k].T)
    def strips(wt):
        return np.pad(wt.reshape(wt.shape[0], H, DH), ((0, 0), (0, 0), (0, STRIP - DH))).reshape(wt.shape[0], -1)

    def strip_columns(v):
        return np.ascontiguousarray(strips(v.reshape(1, -1)).reshape(G, P).T)

    def strip_rows(wt):
        return np.pad(wt.reshape(H, DH, D), ((0, 0), (0, STRIP - DH), (0, 0))).reshape(-1, D)

    out["spread"] = np.repeat(np.eye(P, dtype=np.float32)[:, DH::STRIP], STRIP, axis=1)
    out["ctx_T"] = np.ascontiguousarray(w["ctx_1024"].transpose(0, 2, 1))
    for k in ("q", "k"):
        out[f"L0_xattn_W{k}_strips"] = strips(w[f"L0_xattn_W{k}"].T)
        out[f"L0_xattn_b{k}_strips"] = strip_columns(w[f"L0_xattn_b{k}"])
    out["L0_xattn_Wv_strips"] = strips(w["L0_xattn_Wv"].T)
    bv_one = np.pad(w["L0_xattn_bv"].reshape(H, DH), ((0, 0), (0, 1)), constant_values=1)
    out["L0_xattn_bv_one_strips"] = np.ascontiguousarray(
        np.pad(bv_one, ((0, 0), (0, STRIP - DH - 1))).reshape(G, P).T)
    out["L0_xattn_Wo_strips"] = strip_rows(w["L0_xattn_Wo"].T)
    out["L0_xattn_bo"] = w["L0_xattn_bo"]
    wq, wk, wv = (w["L1_attn_qkv_w"][i * D:(i + 1) * D] for i in range(3))
    bq, bk, bv = (w["L1_attn_qkv_b"][i * D:(i + 1) * D] for i in range(3))
    out["L1_attn_Wq_strips"], out["L1_attn_Wk_strips"] = strips(wq.T), strips(wk.T)
    out["L1_attn_bq_strips"], out["L1_attn_bk_strips"] = strip_columns(bq), strip_columns(bk)
    out["L1_attn_Wv_T"], out["L1_attn_bv"] = np.ascontiguousarray(wv.T), np.ascontiguousarray(bv)
    out["L1_attn_proj_w_strips"] = strip_rows(w["L1_attn_proj_w"].T)
    out["L1_attn_proj_b"] = w["L1_attn_proj_b"]
    out["L1_attn_rel_back"] = np.ascontiguousarray(w["L1_attn_rel_pos_emb"][::-1][:RELK])
    for k in ("q", "k", "v"):
        out[f"L1_xattn_W{k}_T"] = np.ascontiguousarray(w[f"L1_xattn_W{k}"].T)
    for k in ("q", "k"):
        out[f"L1_xattn_b{k}_cols"] = columns(w[f"L1_xattn_b{k}"])
    out["L1_xattn_bv"] = w["L1_xattn_bv"]

    def expert_parts(wg, wu, wd):
        n = wg.shape[0]
        halves = [m.reshape(n, KC, P, FF).transpose(0, 2, 1, 3).reshape(n, P, KC * FF) for m in (wg, wu)]
        return np.concatenate(halves + [wd], axis=2)

    routed = expert_parts(w["L0_ffn_Wg"], w["L0_ffn_Wu"], w["L0_ffn_Wd"])
    shared = expert_parts(w["L0_ffn_SWg"].reshape(D, NSH, FF).transpose(1, 0, 2),
                          w["L0_ffn_SWu"].reshape(D, NSH, FF).transpose(1, 0, 2),
                          w["L0_ffn_SWd"].reshape(NSH, FF, D))
    out["L0_ffn_experts"] = np.pad(np.concatenate([routed, shared]), ((0, EL - NSH), (0, 0), (0, 0)))
    out["L0_ffn_router_T"] = np.ascontiguousarray(w["L0_ffn_router_w"].T)
    out["L0_ffn_e_bias"] = w["L0_ffn_e_bias"]
    out["earlier"] = np.tril(np.ones((EG, EG), np.float32), -1)

    out["flip"] = np.ascontiguousarray(np.eye(P, dtype=np.float32)[::-1])
    out["iota"] = np.arange(P, dtype=np.float32)
    out["L1_ffn_norm_w"] = w["L1_ffn_norm_w"]
    out["L1_ffn_w_q"] = w["L1_ffn_w_q"]
    out["L1_ffn_keys_T"] = np.ascontiguousarray(w["L1_ffn_keys"].transpose(3, 0, 2, 1).reshape(DK, 2 * PH, NK))
    tiles = (2, ET, NK, D)
    out["L1_ffn_down_T"] = np.ascontiguousarray(
        w["L1_ffn_expert_down"].reshape(tiles).transpose(3, 1, 0, 2).reshape(D, NK * NK))
    out["L1_ffn_up"] = np.ascontiguousarray(
        w["L1_ffn_expert_up"].reshape(tiles).transpose(0, 2, 1, 3).reshape(P, ET, D))
    return out


def kernel(**inputs):
    import numpy as _np
    import concourse.bacc as _bacc
    from concourse import mybir as _mybir
    from concourse.bass_utils import run_bass_kernel_spmd as _run

    nc = _bacc.Bacc("TRN2", target_bir_lowering=False, num_devices=1)
    arrays, aps = {}, {}
    for name, a in layouts({k: _np.asarray(v) for k, v in inputs.items()}).items():
        arrays[name + "_dram"] = a
        aps[name] = nc.dram_tensor(name + "_dram", a.shape, _mybir.dt.from_np(a.dtype), kind="ExternalInput").ap()
    out = nc.dram_tensor("out_dram", (B, T, D), F32, kind="ExternalOutput").ap()
    build(nc, aps, out, STAGES)
    r = _run(nc, [arrays], core_ids=[0])
    return r.results[0]["out_dram"]
```

```python
from contextlib import ExitStack

import concourse.bass as bass
from concourse import mybir

F32 = mybir.dt.float32
F32R = mybir.dt.float32r
U32 = mybir.dt.uint32
BF16 = mybir.dt.bfloat16
ALU = mybir.AluOpType
ACT = mybir.ActivationFunctionType
AX = mybir.AxisListType
ds = bass.ds

P = 128
B, T, D = 4, 512, 256
QT = T // P
NT = B * QT
KC = D // P
BANK = 512
LN_EPS = 1e-5
DI, DS, DCONV = 512, 16, 4
DT = DI // P
SU = 4
UR = 3
H, DH = 16, 16
G = 4
STRIP = 32
CTX = 1601
STRIDE = 16
CK = CTX // STRIDE
NEG = -1.0e30

STAGES = ("ssm", "gather_attn", "moe", "self_attn", "cross_attn", "peer")


class Chain:

    def __init__(self, engine, sem):
        self.engine, self.sem, self.n = engine, sem, 0

    def __call__(self, instruction):
        self.n += 1
        instruction.then_inc(self.sem, 1)
        self.engine.wait_ge(self.sem, self.n)


class Core:

    def __init__(self, nc, ctx):
        self.nc, self.ctx = nc, ctx
        self.sems = {}
        self.ahead_loaded = ctx.enter_context(nc.semaphore("ahead_loaded"))
        self.x = ctx.enter_context(nc.sbuf_tensor("x_res", [P, NT, D], F32))
        self.ident = ctx.enter_context(nc.sbuf_tensor("ident", [P, P], F32))
        self.neg_half = ctx.enter_context(nc.sbuf_tensor("neg_half", [P, NT], F32))
        self.ps = ctx.enter_context(nc.psum_tensor("ps", [P, 8, BANK], F32))

    def sem(self, name):
        if name not in self.sems:
            self.sems[name] = self.ctx.enter_context(self.nc.semaphore(name))
        return self.sems[name]

    def fresh(self):
        nums = sorted(s.num for s in self.sems.values())
        lo, hi = nums[0], nums[-1] + 1
        assert nums == list(range(lo, hi))
        self.nc.vector.sem_clear(range(lo, hi))
        self.nc.all_engine_barrier()


def load_block(core, pairs):
    nc = core.nc
    loaded = core.sem("weights_loaded")
    loaded2 = core.sem("weights_loaded_act")
    with nc.Block() as block:
        @block.sync
        def _(sp):
            for out, in_ in pairs[0::2]:
                sp.dma_start(out, in_).then_inc(loaded, 16)
            sp.wait_ge(loaded, 16 * len(pairs[0::2]))

        @block.scalar
        def _(act):
            for out, in_ in pairs[1::2]:
                act.dma_start(out, in_).then_inc(loaded2, 16)
            if pairs[1::2]:
                act.wait_ge(loaded2, 16 * len(pairs[1::2]))
    core.fresh()


def load_ahead(core, pairs):
    with core.nc.Block() as block:
        @block.gpsimd
        def _(pool):
            for out, in_ in pairs:
                pool.dma_start(out, in_).then_inc(core.ahead_loaded, 16)


def await_ahead(core, count):
    with core.nc.Block() as block:
        @block.gpsimd
        def _(pool):
            pool.wait_ge(core.ahead_loaded, 16 * count)
    core.fresh()


def norm_dve(core, dve, b, xn, stats, mv, rstd, keep_sum=False, extra=None, tiles=QT):
    x = core.x
    chain = Chain(dve, core.sem("norm_chain"))
    for q in range(tiles):
        last = dve.bn_stats(stats[:, q, :], x[:, ds(b * tiles + q, 1), :])
    chain(last)
    for q in range(tiles):
        last = dve.bn_aggr(mv[:, q, :], stats[:, q, :])
    chain(last)
    dve.tensor_scalar(rstd[:, :], mv[:, :, 1], LN_EPS, None, ALU.add).then_inc(core.sem("var_ready"), 1)
    dve.wait_ge(core.sem("rstd_ready"), 1)
    for q in range(tiles):
        ins = dve.tensor_scalar(xn[:, q, :], x[:, ds(b * tiles + q, 1), :], mv[:, q, 0:1], rstd[:, q:q + 1],
                                ALU.subtract, ALU.mult)
        if extra is None:
            ins.then_inc(core.sem("xn_ready"), 1)
    if extra is not None:
        chain(ins)
        extra(chain)
    elif keep_sum:
        dve.wait_ge(core.sem("xn_ready"), QT)
        xb = x[:, ds(b * QT, QT), :]
        dve.tensor_tensor(xb, xb, xn[:, :, :], ALU.add)


def norm_pool(core, pool, rstd, tiles=QT):
    pool.wait_ge(core.sem("var_ready"), 1)
    pool.tensor_tensor(rstd[:, :], rstd[:, :], core.neg_half[:, 0:tiles], ALU.pow)\
        .then_inc(core.sem("rstd_ready"), 1)


def norm_pe(core, pe, xn, tiles=QT):
    for q in range(tiles):
        pe.wait_ge(core.sem("xn_ready"), q + 1)
        n, t = divmod(q, QT)
        for c in range(KC):
            last = pe.transpose(core.ps[:, n * KC + c, t * P:(t + 1) * P], xn[:, q, c * P:(c + 1) * P],
                                core.ident[:, :])
        if t == QT - 1:
            last.then_inc(core.sem("xn_turned"), 1)


def norm_act(core, act, xT, tiles=QT):
    for n in range(tiles // QT):
        act.wait_ge(core.sem("xn_turned"), n + 1)
        for c in range(KC):
            act.activation(xT[c][:, n * T:(n + 1) * T], core.ps[:, n * KC + c, :], ACT.Copy)\
                .then_inc(core.sem("xT_ready"), 1)




def ssm_stage(core, w, scratch):
    nc = core.nc
    x, ps = core.x, core.ps
    with ExitStack() as ctx:
        def sb(name, shape, dt=F32):
            return ctx.enter_context(nc.sbuf_tensor("ssm_" + name, shape, dt))

        w_in = sb("w_in", [P, KC, 2 * DI])
        w_dt = sb("w_dt", [P, DT, DI])
        w_x = sb("w_x", [P, DT, 2 * DS])
        w_out = sb("w_out", [P, DT, D])
        conv_w = sb("conv_w", [P, DT, DCONV])
        conv_b = sb("conv_b", [P, DT])
        a_log = sb("a_log", [P, DT, DS])
        a_neg = sb("a_neg", [P, DT, DS])
        d_par = sb("d_par", [P, DT])
        b_dt = sb("b_dt", [P, DT])
        bc = sb("bc", [P, 2 * DS, T])
        dA = sb("dA", [P, UR, SU, T])
        hb = sb("hb", [P, UR, SU, T])
        xs = sb("xs", [P, DT, T])
        sz = sb("sz", [P, DT, T])
        dt = sb("dt", [P, DT, T])
        u = sb("u", [P, DT, T])
        xs_next = sb("xs_next", [P, DT, T])
        xT = sb("xT", [P, KC, T])
        xT_next = sb("xT_next", [P, KC, T])
        xn = sb("xn", [P, QT, D])
        soft = sz
        xdbl = sb("xdbl", [2 * DS, T])
        stats = sb("stats", [P, QT, 6])
        mv = sb("mv", [P, QT, 2])
        rstd = sb("rstd", [P, QT])
        load_block(core, [
            (w_in[:, :, :], w["L0_attn_W_in_T"].rearrange("(c p) e -> p c e", p=P)),
            (w_dt[:, :, :], w["L0_attn_W_dt_T"].rearrange("(c p) f -> p c f", p=P)),
            (w_x[:, :, :], w["L0_attn_W_x_T"].rearrange("(c p) s -> p c s", p=P)),
            (w_out[:, :, :], w["L0_attn_W_out_T"].rearrange("(c p) d -> p c d", p=P)),
            (conv_w[:, :, :], w["L0_attn_conv_w"].rearrange("(c p) o k -> p c (o k)", p=P)),
            (conv_b[:, :], w["L0_attn_conv_b_cols"]),
            (a_log[:, :, :], w["L0_attn_A_log"].rearrange("(c p) s -> p c s", p=P)),
            (d_par[:, :], w["L0_attn_D_param_cols"]),
            (b_dt[:, :], w["L0_attn_b_dt_cols"]),
        ])
        a_exp = core.sem("a_exp")
        with nc.Block() as block:
            @block.scalar
            def _(act):
                act.activation(a_neg[:, :, :], a_log[:, :, :], ACT.Exp).then_inc(a_exp, 1)

            @block.vector
            def _(dve):
                dve.wait_ge(a_exp, 1)
                dve.tensor_scalar(a_neg[:, :, :], a_neg[:, :, :], -1.0, None, ALU.mult)
                dve.memset(dA[:, :, :, 0:1], 0.0)
        core.fresh()

        sem = core.sem
        bc_loaded = [sem(f"bc_{part}_loaded") for part in range(DS // SU)]
        NU = DT * DS // SU
        TAP = DT

        def ssm_block(cur, nxt):
            with nc.Block() as block:
                @block.tensor
                def _(pe):
                    def project_in(e, source, done):
                        for c in range(KC):
                            last = pe.matmul(ps[:, 4 + e % DT, :], w_in[:, c, e * P:(e + 1) * P], source[:, c, :],
                                             start=(c == 0), stop=(c == KC - 1))
                        last.then_inc(done, 1)

                    if cur is not None:
                        pe.wait_ge(sem("xs_taken"), 1)
                        for c in range(DT):
                            last = pe.matmul(ps[0:2 * DS, 0, :], w_x[:, c, :], xs[:, c, :],
                                             start=(c == 0), stop=(c == DT - 1))
                        last.then_inc(sem("bc_ready"), 1)
                        for f in range(DT):
                            for c in range(DT):
                                last = pe.matmul(ps[:, 4 + f, :], w_dt[:, c, f * P:(f + 1) * P], xs[:, c, :],
                                                 start=(c == 0), stop=(c == DT - 1))
                            last.then_inc(sem("dt_ready"), 1)
                        pe.wait_ge(sem("xT_taken"), 1)
                        for e in range(DT, 2 * DT):
                            pe.wait_ge(sem("z_ready"), e - DT + 1)
                            project_in(e, xT, sem("gate_ready"))
                        pe.wait_ge(sem("xdbl_out"), 1)
                    if nxt is not None:
                        norm_pe(core, pe, xn)
                    if cur is None:
                        pe.wait_ge(sem("xT_ready"), KC)
                        for e in range(DT):
                            project_in(e, xT_next, sem("inner_ready"))
                        return
                    for n in range(NU):
                        d, part = divmod(n, DS // SU)
                        pe.wait_ge(sem("hc_ready"), n + 1)
                        if part == 0 and d >= 2:
                            pe.wait_ge(sem("y_done"), d - 1)
                        for s in range(SU):
                            last = pe.matmul(ps[:, 2 + d % 2, :], core.ident[:, :], hb[:, n % UR, s, :],
                                             start=(part == 0 and s == 0),
                                             stop=(part == DS // SU - 1 and s == SU - 1))
                        last.then_inc(sem("hc_summed"), 1)
                        if nxt is not None and TAP <= n < TAP + DT:
                            if n == TAP:
                                pe.wait_ge(sem("sz_ready"), 1)
                                pe.wait_ge(sem("xT_ready"), KC)
                            project_in(n - TAP, xT_next, sem("inner_ready"))
                    pe.wait_ge(sem("y_done"), DT)
                    for q in range(QT):
                        for c in range(DT):
                            last = pe.matmul(ps[:, q // 2, (q % 2) * D:(q % 2 + 1) * D],
                                             xs[:, c, q * P:(q + 1) * P], w_out[:, c, :],
                                             start=(c == 0), stop=(c == DT - 1))
                    last.then_inc(sem("out_ready"), 1)

                @block.scalar
                def _(act):
                    def begin_conv(e):
                        act.wait_ge(sem("inner_ready"), e + 1)
                        act.activation(xs_next[:, e, :], ps[:, 4 + e, :], ACT.Identity,
                                       scale=conv_w[:, e, DCONV - 1:DCONV], bias=conv_b[:, e:e + 1])\
                            .then_inc(sem("conv_begun"), 1)

                    def logarithms(tiles):
                        act.wait_ge(sem("z_ready"), tiles.stop)
                        chain(act.activation(soft[:, tiles, :], dt[:, tiles, :], ACT.Abs))
                        chain(act.activation(soft[:, tiles, :], soft[:, tiles, :], ACT.Exp, scale=-1.0))
                        act.activation(soft[:, tiles, :], soft[:, tiles, :], ACT.Ln, bias=1.0)\
                            .then_inc(sem("ln_ready"), 1)

                    if cur is not None:
                        chain = Chain(act, sem("act_chain"))
                        act.activation(xs[:, :, :], xs_next[:, :, :], ACT.Copy).then_inc(sem("xs_taken"), 1)
                        act.wait_ge(sem("bc_ready"), 1)
                        act.activation(xdbl[:, :], ps[0:2 * DS, 0, :], ACT.Copy).then_inc(sem("xdbl_out"), 1)
                        logarithms(slice(0, 1))
                        for n in range(NU):
                            if n == 2:
                                logarithms(slice(1, DT))
                            if n == 3 and nxt is not None:
                                act.wait_ge(sem("xT_taken"), 1)
                                norm_act(core, act, [xT_next[:, c, :] for c in range(KC)])
                            if n % (DS // SU) == 0 and n // (DS // SU) < 2:
                                act.wait_ge(sem("u_ready"), n // (DS // SU) + 1)
                            if n == DS // SU:
                                act.wait_ge(sem("gate_ready"), DT)
                                act.activation(sz[:, :, :], ps[:, 4:4 + DT, :], ACT.Silu)\
                                    .then_inc(sem("sz_ready"), 1)
                            if nxt is not None and TAP + 5 <= n < TAP + 5 + DT:
                                act.wait_ge(sem("xs_taken"), 1)
                                begin_conv(n - TAP - 5)
                            if n >= UR:
                                act.wait_ge(sem("scanned"), n - UR + 1)
                            d, part = divmod(n, DS // SU)
                            for s in range(SU):
                                i = part * SU + s
                                last = act.activation(dA[:, n % UR, s, 1:T], dt[:, d, 1:T], ACT.Exp,
                                                      scale=a_neg[:, d, i:i + 1])
                            last.then_inc(sem("dA_ready"), 1)
                    else:
                        norm_act(core, act, [xT_next[:, c, :] for c in range(KC)])
                        for e in range(DT):
                            begin_conv(e)
                    if nxt is not None:
                        act.wait_ge(sem("conv_done"), 1)
                        act.activation(xs_next[:, :, :], xs_next[:, :, :], ACT.Silu)

                @block.sync
                def _(sp):
                    if cur is None:
                        return
                    sp.wait_ge(sem("xdbl_out"), 1)
                    sp.dma_start(scratch[:, :], xdbl[:, :]).then_inc(sem("xdbl_stored"), 16)
                    sp.wait_ge(sem("xdbl_stored"), 16)
                    for part in range(DS // SU):
                        for rows in (slice(part * SU, (part + 1) * SU),
                                     slice(DS + part * SU, DS + (part + 1) * SU)):
                            sp.dma_start(bc[:, rows, :], scratch[rows, :].partition_broadcast(P))\
                              .then_inc(bc_loaded[part], 16)

                @block.gpsimd
                def _(pool):
                    if nxt is not None:
                        norm_pool(core, pool, rstd)
                    if cur is None:
                        return
                    for n in range(NU):
                        d, part = divmod(n, DS // SU)
                        if d == 0:
                            pool.wait_ge(bc_loaded[part], 32)
                        if part == 0 and d < 2:
                            pool.wait_ge(sem("u_ready"), d + 1)
                        if n >= UR:
                            pool.wait_ge(sem("hc_summed"), n - UR + 1)
                        pool.tensor_tensor(hb[:, n % UR, :, :],
                                           u[:, d, :].unsqueeze(1).broadcast_to([P, SU, T]),
                                           bc[:, part * SU:(part + 1) * SU, :], ALU.mult)\
                            .then_inc(sem("dBx_ready"), 1)

                @block.vector
                def _(dve):
                    chain = Chain(dve, sem("dve_chain"))

                    def finish_conv(e):
                        dve.wait_ge(sem("conv_begun"), e + 1)
                        for k in range(1, DCONV):
                            ins = dve.scalar_tensor_tensor(
                                out=xs_next[:, e, k:T], in0=ps[:, 4 + e, 0:T - k],
                                scalar=conv_w[:, e, DCONV - 1 - k:DCONV - k], in1=xs_next[:, e, k:T],
                                op0=ALU.mult, op1=ALU.add)
                            if k < DCONV - 1:
                                chain(ins)
                        if e == DT - 1:
                            ins.then_inc(sem("conv_done"), 1)

                    def step_sizes(tiles, order):
                        dve.wait_ge(sem("z_ready"), DT)
                        dve.wait_ge(sem("ln_ready"), order)
                        chain(dve.scalar_tensor_tensor(out=dt[:, tiles, :], in0=dt[:, tiles, :], scalar=0.0,
                                                       in1=soft[:, tiles, :], op0=ALU.max, op1=ALU.add))
                        dve.tensor_tensor(u[:, tiles, :], dt[:, tiles, :], xs[:, tiles, :], ALU.mult)\
                            .then_inc(sem("u_ready"), 1)

                    def finish(d):
                        if d == 0:
                            dve.wait_ge(sem("sz_ready"), 1)
                        dve.wait_ge(sem("hc_summed"), (d + 1) * DS // SU)
                        chain(dve.scalar_tensor_tensor(out=xs[:, d, :], in0=xs[:, d, :],
                                                       scalar=d_par[:, d:d + 1], in1=ps[:, 2 + d % 2, :],
                                                       op0=ALU.mult, op1=ALU.add))
                        dve.tensor_tensor(xs[:, d, :], xs[:, d, :], sz[:, d, :], ALU.mult)\
                            .then_inc(sem("y_done"), 1)

                    if cur is not None:
                        dve.tensor_copy(xT[:, :, :], xT_next[:, :, :]).then_inc(sem("xT_taken"), 1)
                    if nxt is not None:
                        norm_dve(core, dve, nxt, xn, stats, mv, rstd, keep_sum=True)
                    if cur is None:
                        for e in range(DT):
                            finish_conv(e)
                        return
                    dve.wait_ge(sem("xs_taken"), 1)
                    for f in range(DT):
                        dve.wait_ge(sem("dt_ready"), f + 1)
                        dve.tensor_scalar(dt[:, f, :], ps[:, 4 + f, :], b_dt[:, f:f + 1], None, ALU.add)\
                            .then_inc(sem("z_ready"), 1)
                    step_sizes(slice(0, 1), 1)
                    for n in range(NU):
                        if n == 2:
                            step_sizes(slice(1, DT), 2)
                        d, part = divmod(n, DS // SU)
                        dve.wait_ge(sem("dA_ready"), n + 1)
                        dve.wait_ge(sem("dBx_ready"), n + 1)
                        h = hb[:, n % UR, :, :]
                        hf = h.rearrange("p s t -> p (s t)")
                        dve.tensor_tensor_scan(hf, dA[:, n % UR, :, :].rearrange("p s t -> p (s t)"), hf,
                                               0.0, ALU.mult, ALU.add).then_inc(sem("scanned"), 1)
                        dve.wait_ge(sem("scanned"), n + 1)
                        dve.tensor_tensor(h, h, bc[:, DS + part * SU:DS + (part + 1) * SU, :], ALU.mult)\
                            .then_inc(sem("hc_ready"), 1)
                        if part == 0 and d >= 1:
                            finish(d - 1)
                        if nxt is not None and TAP + 4 <= n < TAP + 4 + DT:
                            finish_conv(n - TAP - 4)
                    finish(DT - 1)
                    dve.wait_ge(sem("out_ready"), 1)
                    xb = x[:, ds(cur * QT, QT), :]
                    dve.tensor_tensor(xb, xb, ps[:, 0:2, :].rearrange("p a (c d) -> p (a c) d", d=D), ALU.add)
            core.fresh()

        ssm_block(None, 0)
        with nc.Fori(0, B - 1) as b:
            ssm_block(b, b + 1)
        ssm_block(B - 1, None)




def add_bias_rows(core, dve, b, bias):
    dve.wait_ge(core.sem("xn_ready"), QT)
    xb = core.x[:, ds(b * QT, QT), :]
    dve.tensor_tensor(xb, xb, bias[:, :].unsqueeze(1).broadcast_to([P, QT, D]), ALU.add)\
        .then_inc(core.sem("bias_added"), 1)


def copy_sums_act(core, act, q, summed, sums_T):
    act.wait_ge(core.sem("values_summed"), summed)
    if q:
        act.wait_ge(core.sem("heads_T_ready"), q)
    act.activation(sums_T[:, :, :], core.ps[:, 6, :].rearrange("p (g t) -> p g t", g=G), ACT.Copy)\
        .then_inc(core.sem("sums_copied"), 1)


def spread_pe(core, pe, q, sums_T, spread):
    pe.wait_ge(core.sem("sums_copied"), q + 1)
    if q:
        pe.wait_ge(core.sem("x_added"), q)
    pe.matmul(core.ps[:, 7, :], spread[:, :], sums_T[:, :, :].rearrange("p g t -> p (g t)"), start=True, stop=True)\
      .then_inc(core.sem("den_spread"), 1)


def invert_den_dve(core, dve, q, g, inv_den):
    if g == 0:
        dve.wait_ge(core.sem("den_spread"), q + 1)
        if q:
            dve.wait_ge(core.sem("heads_T_ready"), q)
    dve.reciprocal(inv_den[:, g, :], core.ps[:, 7, g * P:(g + 1) * P]).then_inc(core.sem("den_ready"), 1)


def normalise_pool(core, pool, sums_T, inv_den, heads_T):
    for q in range(QT):
        if q:
            pool.wait_ge(core.sem("projected"), q)
        pool.wait_ge(core.sem("den_ready"), G * (q + 1))
        pool.tensor_tensor(heads_T[:, :, :], sums_T[:, :, :], inv_den[:, :, :], ALU.mult)\
            .then_inc(core.sem("heads_T_ready"), 1)


def project_strips_pe(core, pe, q, heads_T, w_o):
    pe.wait_ge(core.sem("heads_T_ready"), q + 1)
    for g in range(G):
        last = pe.matmul(core.ps[:, 7, 0:D], heads_T[:, g, :], w_o[:, g, :], start=(g == 0), stop=(g == G - 1))
    last.then_inc(core.sem("projected"), 1)


def project_strips_dve(core, dve, b, q):
    dve.wait_ge(core.sem("projected"), q + 1)
    if q == 0:
        dve.wait_ge(core.sem("bias_added"), 1)
    xq = core.x[:, ds(b * QT + q, 1), :]
    dve.tensor_tensor(xq, xq, core.ps[:, 7:8, 0:D], ALU.add).then_inc(core.sem("x_added"), 1)




def gather_attn_stage(core, w):
    nc = core.nc
    ps, sem = core.ps, core.sem
    with ExitStack() as ctx:
        def sb(name, shape, dt=F32):
            return ctx.enter_context(nc.sbuf_tensor("ga_" + name, shape, dt))

        w_q = sb("w_q", [P, KC, G * P])
        w_k = sb("w_k", [P, KC, G * P])
        w_v = sb("w_v", [P, KC, G * P])
        w_o = sb("w_o", [P, G, D])
        b_q = sb("b_q", [P, G])
        b_k = sb("b_k", [P, G])
        b_v = sb("b_v", [P, G])
        b_o = sb("b_o", [P, D])
        spread = sb("spread", [P, P])
        cT = sb("cT", [P, KC, STRIDE * P])
        xn = sb("xn", [P, QT, D])
        xT = sb("xT", [P, KC, T])
        qT = sb("qT", [P, G, T])
        kT = sb("kT", [P, G, P])
        vT = sb("vT", [P, G, P])
        v = sb("v", [P, H, STRIP])
        probs = sb("probs", [P, 2, H, CK])
        pT = sb("pT", [P, 2, H, P])
        top = sb("top", [P, 2, H])
        sums_T = sb("sums_T", [P, G, P])
        inv_den = sb("inv_den", [P, G, P])
        heads_T = sb("heads_T", [P, G, P])
        stats = sb("stats", [P, QT, 6])
        mv = sb("mv", [P, QT, 2])
        rstd = sb("rstd", [P, QT])

        load_block(core, [
            (cT[:, :, 0:CTX], w["ctx_T"][0, :, :].rearrange("(c p) k -> p c k", p=P)),
            (w_k[:, :, :], w["L0_xattn_Wk_strips"].rearrange("(c p) e -> p c e", p=P)),
            (w_q[:, :, :], w["L0_xattn_Wq_strips"].rearrange("(c p) e -> p c e", p=P)),
            (w_v[:, :, :], w["L0_xattn_Wv_strips"].rearrange("(c p) e -> p c e", p=P)),
            (w_o[:, :, :], w["L0_xattn_Wo_strips"].rearrange("(g p) e -> p g e", p=P)),
            (spread[:, :], w["spread"]),
            (b_q[:, :], w["L0_xattn_bq_strips"]),
            (b_k[:, :], w["L0_xattn_bk_strips"]),
            (b_v[:, :], w["L0_xattn_bv_one_strips"]),
            (b_o[:, :], w["L0_xattn_bo"].partition_broadcast(P)),
        ])
        with nc.Block() as block:
            @block.vector
            def _(dve):
                dve.memset(cT[:, :, CTX:STRIDE * P], 0.0)
        core.fresh()

        def gather_block(b, last_batch):
            with nc.Block() as block:
                @block.sync
                def _(sp):
                    if not last_batch:
                        sp.wait_ge(sem("kv_ready"), 2)
                        sp.dma_start(cT[:, :, 0:CTX], w["ctx_T"][ds(b + 1, 1), :, :]
                                     .rearrange("o (c p) k -> p (o c) k", p=P)).then_inc(sem("ctx_loaded"), 16)
                        sp.wait_ge(sem("ctx_loaded"), 16)

                @block.tensor
                def _(pe):
                    for bank, wt in ((2, w_k), (3, w_v)):
                        for h in range(H):
                            g, j = divmod(h, G)
                            for c in range(KC):
                                last = pe.matmul(ps[STRIP * j:STRIP * (j + 1), bank, g * P:(g + 1) * P],
                                                 wt[:, c, g * P + STRIP * j:g * P + STRIP * (j + 1)],
                                                 cT[:, c, h:h + STRIDE * (P - 1) + 1:STRIDE],
                                                 start=(c == 0), stop=(c == KC - 1))
                        last.then_inc(sem("kv_ready"), 1)
                    norm_pe(core, pe, xn)
                    pe.wait_ge(sem("vT_stored"), 1)
                    for g in range(G):
                        last = pe.transpose(ps[:, 3, g * P:(g + 1) * P], vT[:, g, :], core.ident[:, :])
                    last.then_inc(sem("v_turned"), 1)
                    pe.wait_ge(sem("xT_ready"), KC)
                    for g in range(G):
                        for c in range(KC):
                            last = pe.matmul(ps[:, 4 + g, :], w_q[:, c, g * P:(g + 1) * P], xT[:, c, :],
                                             start=(c == 0), stop=(c == KC - 1))
                        last.then_inc(sem("q_ready"), 1)

                    def scores(q):
                        if q == 0:
                            pe.wait_ge(sem("k_stored"), 1)
                            pe.wait_ge(sem("v_stored"), 1)
                            pe.wait_ge(sem("q_stored"), G)
                        else:
                            pe.wait_ge(sem("scores_read"), q)
                        for j in range(G):
                            for g in range(G):
                                s = slice(STRIP * j, STRIP * (j + 1))
                                last = pe.matmul(ps[:, j, g * P:(g + 1) * P], qT[s, g, q * P:(q + 1) * P],
                                                 kT[s, g, :], start=True, stop=True)
                        last.then_inc(sem("scores_ready"), 1)

                    def turn_weights(q):
                        pe.wait_ge(sem("probs_ready"), q + 1)
                        for j in range(G):
                            if G * q + j >= 2:
                                pe.wait_ge(sem("pT_stored"), G * q + j - 1)
                            for g in range(G):
                                last = pe.transpose(ps[0:CK, 4 + j % 2, g * P:(g + 1) * P],
                                                    probs[:, q % 2, j * G + g, :], core.ident[:, :])
                            last.then_inc(sem("p_turned"), 1)

                    def sum_values(q):
                        pe.wait_ge(sem("pT_stored"), G * (q + 1))
                        if q:
                            pe.wait_ge(sem("sums_copied"), q)
                        for h in range(H):
                            g, j = divmod(h, G)
                            last = pe.matmul(ps[STRIP * j:STRIP * (j + 1), 6, g * P:(g + 1) * P],
                                             v[0:CK, h, :], pT[0:CK, q % 2, j * G + g, :], start=True, stop=True)
                        last.then_inc(sem("values_summed"), 1)

                    scores(0)
                    for q in range(QT + 2):
                        if q + 1 < QT:
                            scores(q + 1)
                        if q < QT:
                            turn_weights(q)
                        if 0 <= q - 2 < QT:
                            project_strips_pe(core, pe, q - 2, heads_T, w_o)
                        if 0 <= q - 1 < QT:
                            spread_pe(core, pe, q - 1, sums_T, spread)
                        if q < QT:
                            sum_values(q)

                @block.scalar
                def _(act):
                    act.wait_ge(sem("kv_ready"), 2)
                    for g in range(G):
                        last = act.activation(vT[:, g, :], ps[:, 3, g * P:(g + 1) * P], ACT.Identity,
                                              bias=b_v[:, g:g + 1])
                    last.then_inc(sem("vT_stored"), 1)
                    norm_act(core, act, [xT[:, c, :] for c in range(KC)])
                    act.wait_ge(sem("v_turned"), 1)
                    act.activation(v[:, :, :], ps[:, 3, :].rearrange("k (h e) -> k h e", e=STRIP), ACT.Copy)\
                        .then_inc(sem("v_stored"), 1)
                    for g in range(G):
                        act.wait_ge(sem("q_ready"), g + 1)
                        act.activation(qT[:, g, :], ps[:, 4 + g, :], ACT.Identity, bias=b_q[:, g:g + 1])\
                            .then_inc(sem("q_stored"), 1)

                    def weights(q):
                        act.wait_ge(sem("scores_read"), q + 1)
                        pq = probs[:, q % 2, :, :]
                        act.activation(pq, pq, ACT.Exp, scale=DH ** -0.5).then_inc(sem("probs_ready"), 1)

                    weights(0)
                    for q in range(QT):
                        for j in range(G):
                            act.wait_ge(sem("p_turned"), G * q + j + 1)
                            if q >= 2:
                                act.wait_ge(sem("values_summed"), q - 1)
                            act.activation(pT[0:CK, q % 2, j * G:(j + 1) * G, :],
                                           ps[0:CK, 4 + j % 2, :].rearrange("k (g t) -> k g t", g=G), ACT.Copy)\
                                .then_inc(sem("pT_stored"), 1)
                        if q + 1 < QT:
                            weights(q + 1)
                        copy_sums_act(core, act, q, q + 1, sums_T)

                @block.gpsimd
                def _(pool):
                    norm_pool(core, pool, rstd)
                    normalise_pool(core, pool, sums_T, inv_den, heads_T)

                @block.vector
                def _(dve):
                    norm_dve(core, dve, b, xn, stats, mv, rstd)
                    add_bias_rows(core, dve, b, b_o)
                    dve.wait_ge(sem("kv_ready"), 1)
                    dve.tensor_tensor(kT[:, :, :], ps[:, 2, :].rearrange("p (g k) -> p g k", g=G),
                                      b_k[:, :].unsqueeze(2).broadcast_to([P, G, P]), ALU.add)\
                        .then_inc(sem("k_stored"), 1)

                    def subtract_top(q):
                        dve.wait_ge(sem("scores_ready"), q + 1)
                        if q >= 2:
                            dve.wait_ge(sem("p_turned"), G * (q - 1))
                        s = ps[:, 0:G, :].rearrange("p j (g k) -> p j g k", g=G)[:, :, :, 0:CK]
                        t = top[:, q % 2, :].rearrange("p (j g) -> p j g", g=G)
                        dve.tensor_reduce(t, s, AX.X, ALU.max).then_inc(sem("top_ready"), 1)
                        dve.wait_ge(sem("top_ready"), q + 1)
                        dve.tensor_tensor(probs[:, q % 2, :, :].rearrange("p (j g) k -> p j g k", g=G), s,
                                          t.unsqueeze(3).broadcast_to([P, G, G, CK]), ALU.subtract)\
                            .then_inc(sem("scores_read"), 1)

                    subtract_top(0)
                    for q in range(QT + 2):
                        if q + 1 < QT:
                            subtract_top(q + 1)
                        if 0 <= q - 2 < QT:
                            project_strips_dve(core, dve, b, q - 2)
                        if 0 <= q - 1 < QT:
                            for g in range(G):
                                invert_den_dve(core, dve, q - 1, g, inv_den)
            core.fresh()

        with nc.Fori(0, B - 1) as b:
            gather_block(b, False)
        gather_block(B - 1, True)



RELK = 256
PR = 8
SLAB = 640


def self_attn_stage(core, w, scratch):
    nc = core.nc
    ps, sem = core.ps, core.sem
    with ExitStack() as ctx:
        def sb(name, shape, dt=F32):
            return ctx.enter_context(nc.sbuf_tensor("sa_" + name, shape, dt))

        w_q = sb("w_q", [P, KC, G * P])
        w_k = sb("w_k", [P, KC, G * P])
        w_v = sb("w_v", [P, KC, D])
        w_o = sb("w_o", [P, G, D])
        b_q = sb("b_q", [P, G])
        b_qn = sb("b_qn", [P, G])
        b_k = sb("b_k", [P, G])
        b_v = sb("b_v", [P, D])
        b_o = sb("b_o", [P, D])
        emb = sb("emb", [P, RELK // P, H, DH])
        tab = sb("tab", [P, RELK // P, H])
        rows = sb("rows", [H, SLAB])
        slab = sb("slab", [P, H, T])
        flipped = sb("flipped", [P, H, T])
        flip = sb("flip", [P, P])
        xn = sb("xn", [P, QT, D])
        xT = sb("xT", [P, KC, T])
        qT = sb("qT", [P, G, T])
        kT = sb("kT", [P, G, T])
        v = sb("v", [P, QT, H, STRIP])
        probs = sb("probs", [P, PR, T])
        pT = sb("pT", [P, 4, T])
        top = sb("top", [P, PR])
        spread = sb("spread", [P, P])
        sums_T = sb("sums_T", [P, G, P])
        inv_den = sb("inv_den", [P, G, P])
        heads_T = sb("heads_T", [P, G, P])
        stats = sb("stats", [P, QT, 6])
        mv = sb("mv", [P, QT, 2])
        rstd = sb("rstd", [P, QT])

        load_block(core, [
            (emb[:, :, :, :], w["L1_attn_rel_back"].rearrange("(a p) (h e) -> p a h e", p=P, e=DH)),
            (flip[:, :], w["flip"]),
            (w_q[:, :, :], w["L1_attn_Wq_strips"].rearrange("(c p) e -> p c e", p=P)),
            (w_k[:, :, :], w["L1_attn_Wk_strips"].rearrange("(c p) e -> p c e", p=P)),
            (w_v[:, :, :], w["L1_attn_Wv_T"].rearrange("(c p) e -> p c e", p=P)),
            (w_o[:, :, :], w["L1_attn_proj_w_strips"].rearrange("(g p) e -> p g e", p=P)),
            (spread[:, :], w["spread"]),
            (b_q[:, :], w["L1_attn_bq_strips"]),
            (b_k[:, :], w["L1_attn_bk_strips"]),
            (b_v[:, :], w["L1_attn_bv"].partition_broadcast(P)),
            (b_o[:, :], w["L1_attn_proj_b"].partition_broadcast(P)),
        ])
        with nc.Block() as block:
            @block.vector
            def _(dve):
                dve.memset(v[:, :, :, DH:DH + 1], 1.0)
                dve.memset(v[:, :, :, DH + 1:STRIP], 0.0)
                dve.tensor_scalar(b_qn[:, :], b_q[:, :], -DH ** -0.5, None, ALU.mult)
                dve.tensor_reduce(tab[:, :, :], emb[:, :, :, :], AX.X, ALU.add).then_inc(sem("tab_ready"), 1)
                dve.memset(rows[:, T:SLAB], -NEG)
                dve.wait_ge(sem("tab_turned"), 1)
                dve.tensor_scalar(rows[:, T - RELK:T], ps[0:H, 0, 0:RELK], -1.0, None, ALU.mult)
                dve.tensor_scalar(rows[:, 0:T - RELK],
                                  ps[0:H, 0, 0:1].broadcast_to([H, T - RELK]), -1.0, None, ALU.mult)\
                    .then_inc(sem("rows_ready"), 1)

            @block.tensor
            def _(pe):
                pe.wait_ge(sem("tab_ready"), 1)
                for a in range(RELK // P):
                    last = pe.transpose(ps[0:H, 0, a * P:(a + 1) * P], tab[:, a, :], core.ident[:, :])
                last.then_inc(sem("tab_turned"), 1)
                pe.wait_ge(sem("slab_loaded"), 16)
                for h in range(H):
                    if h >= 6:
                        pe.wait_ge(sem("slab_ready"), h - 5)
                    pe.matmul(ps[:, 1 + h % 6, :], flip[:, :], flipped[:, h, :], start=True, stop=True)\
                      .then_inc(sem("slab_flipped"), 1)

            @block.scalar
            def _(act):
                for h in range(H):
                    act.wait_ge(sem("slab_flipped"), h + 1)
                    act.activation(slab[:, h, :], ps[:, 1 + h % 6, :], ACT.Copy).then_inc(sem("slab_ready"), 1)

            @block.sync
            def _(sp):
                sp.wait_ge(sem("rows_ready"), 1)
                sp.dma_start(scratch, rows[:, :]).then_inc(sem("rows_stored"), 16)
                sp.wait_ge(sem("rows_stored"), 16)
                sp.dma_start(flipped[:, :, :], bass.AP(scratch.tensor, scratch.offset,
                                                       [[1, P], [SLAB, H], [1, T]]))\
                  .then_inc(sem("slab_loaded"), 16)
                sp.wait_ge(sem("slab_loaded"), 16)
        core.fresh()

        NU = QT * H
        with nc.Fori(0, B) as b:
            with nc.Block() as block:
                @block.tensor
                def _(pe):
                    norm_pe(core, pe, xn)
                    pe.wait_ge(sem("xT_ready"), KC)
                    for g in range(G):
                        for c in range(KC):
                            last = pe.matmul(ps[:, 4 + g, :], w_q[:, c, g * P:(g + 1) * P], xT[:, c, :],
                                             start=(c == 0), stop=(c == KC - 1))
                        last.then_inc(sem("q_ready"), 1)
                    for g in range(G):
                        for c in range(KC):
                            last = pe.matmul(ps[:, g, :], w_k[:, c, g * P:(g + 1) * P], xT[:, c, :],
                                             start=(c == 0), stop=(c == KC - 1))
                        last.then_inc(sem("k_ready"), 1)
                    pe.wait_ge(sem("q_stored"), G)
                    for q in range(QT):
                        for c in range(KC):
                            last = pe.matmul(ps[:, 4 + q // 2, (q % 2) * D:(q % 2 + 1) * D],
                                             xT[:, c, q * P:(q + 1) * P], w_v[:, c, :],
                                             start=(c == 0), stop=(c == KC - 1))
                    last.then_inc(sem("v_ready"), 1)
                    pe.wait_ge(sem("k_stored"), G)

                    for n in range(NU + 13):
                        if n < NU:
                            q, h = divmod(n, H)
                            g, j = divmod(h, G)
                            if n >= 4:
                                pe.wait_ge(sem("scores_read"), n - 3)
                            s = slice(STRIP * j, STRIP * (j + 1))
                            pe.matmul(ps[:, j, 0:(q + 1) * P], qT[s, g, q * P:(q + 1) * P],
                                      kT[s, g, 0:(q + 1) * P], start=True, stop=True)\
                              .then_inc(sem("scores_ready"), 1)
                        if n == 0:
                            pe.wait_ge(sem("v_stored"), 1)
                        m = n - 4
                        if 0 <= m < NU:
                            pe.wait_ge(sem("probs_ready"), m + 1)
                            if m >= 2:
                                pe.wait_ge(sem("pT_act") if m % 2 == 0 else sem("pT_dve"), m // 2)
                            for k in range(m // H + 1):
                                last = pe.matmul(ps[:, 4 + m % 2, k * P:(k + 1) * P],
                                                 probs[:, m % PR, k * P:(k + 1) * P], core.ident[:, :],
                                                 start=True, stop=True)
                            last.then_inc(sem("p_turned"), 1)
                        m = n - 6
                        if 0 <= m < NU:
                            q, h = divmod(m, H)
                            g, j = divmod(h, G)
                            pe.wait_ge(sem("pT_act") if m % 2 == 0 else sem("pT_dve"), m // 2 + 1)
                            if h == 0 and q:
                                pe.wait_ge(sem("sums_copied"), q)
                            for k in range(q + 1):
                                last = pe.matmul(ps[STRIP * j:STRIP * (j + 1), 6, g * P:(g + 1) * P],
                                                 v[:, k, h, :], pT[:, m % 4, k * P:(k + 1) * P],
                                                 start=(k == 0), stop=(k == q))
                            last.then_inc(sem("values_summed"), 1)
                        if n - 7 >= 0 and (n - 7) % H == H - 1:
                            spread_pe(core, pe, (n - 7) // H, sums_T, spread)
                        if n - 12 >= 0 and (n - 12) % H == H - 1:
                            project_strips_pe(core, pe, (n - 12) // H, heads_T, w_o)

                @block.scalar
                def _(act):
                    norm_act(core, act, [xT[:, c, :] for c in range(KC)])
                    for g in range(G):
                        act.wait_ge(sem("q_ready"), g + 1)
                        act.activation(qT[:, g, :], ps[:, 4 + g, :], ACT.Identity, bias=b_qn[:, g:g + 1],
                                       scale=-DH ** -0.5).then_inc(sem("q_stored"), 1)
                    for g in range(G):
                        act.wait_ge(sem("k_ready"), g + 1)
                        act.activation(kT[:, g, :], ps[:, g, :], ACT.Identity, bias=b_k[:, g:g + 1])\
                            .then_inc(sem("k_stored"), 1)
                    for n in range(NU + 7):
                        if n < NU:
                            nk = (n // H + 1) * P
                            act.wait_ge(sem("scores_read"), n + 1)
                            pn = probs[:, n % PR, 0:nk]
                            act.activation(pn, pn, ACT.Exp, bias=top[:, n % PR:n % PR + 1], scale=-1.0)\
                                .then_inc(sem("probs_ready"), 1)
                        m = n - 4
                        if 0 <= m < NU and m % 2 == 0:
                            nk = (m // H + 1) * P
                            act.wait_ge(sem("p_turned"), m + 1)
                            if m >= 4:
                                act.wait_ge(sem("values_summed"), m - 3)
                            act.activation(pT[:, m % 4, 0:nk], ps[:, 4, 0:nk], ACT.Copy)\
                                .then_inc(sem("pT_act"), 1)
                        if n - 6 >= 0 and (n - 6) % H == H - 1:
                            copy_sums_act(core, act, (n - 6) // H, n - 5, sums_T)

                @block.gpsimd
                def _(pool):
                    norm_pool(core, pool, rstd)
                    normalise_pool(core, pool, sums_T, inv_den, heads_T)

                @block.vector
                def _(dve):
                    norm_dve(core, dve, b, xn, stats, mv, rstd)
                    add_bias_rows(core, dve, b, b_o)
                    dve.wait_ge(sem("v_ready"), 1)
                    dve.tensor_tensor(v[:, :, :, 0:DH],
                                      ps[:, 4:6, :].rearrange("p a (c h e) -> p (a c) h e", c=2, e=DH),
                                      b_v[:, :].rearrange("p (h e) -> p h e", e=DH).unsqueeze(1)
                                      .broadcast_to([P, QT, H, DH]), ALU.add).then_inc(sem("v_stored"), 1)
                    for n in range(NU + 13):
                        if n < NU:
                            q, h = divmod(n, H)
                            nk = (q + 1) * P
                            dve.wait_ge(sem("scores_ready"), n + 1)
                            if n >= PR:
                                dve.wait_ge(sem("p_turned"), n - PR + 1)
                            dve.tensor_tensor_reduce(probs[:, n % PR, 0:nk], ps[:, h % G, 0:nk],
                                                     slab[:, h, T - nk:T], 1.0, -NEG, ALU.add, ALU.min,
                                                     top[:, n % PR:n % PR + 1]).then_inc(sem("scores_read"), 1)
                        m = n - 4
                        if 0 <= m < NU and m % 2 == 1:
                            nk = (m // H + 1) * P
                            dve.wait_ge(sem("p_turned"), m + 1)
                            if m >= 4:
                                dve.wait_ge(sem("values_summed"), m - 3)
                            dve.tensor_copy(pT[:, m % 4, 0:nk], ps[:, 5, 0:nk]).then_inc(sem("pT_dve"), 1)
                        for g in range(G):
                            m = n - 7 - g
                            if m >= 0 and m % H == H - 1:
                                invert_den_dve(core, dve, m // H, g, inv_den)
                        if n - 12 >= 0 and (n - 12) % H == H - 1:
                            project_strips_dve(core, dve, b, (n - 12) // H)
            core.fresh()



CKT = (CTX + P - 1) // P
CLAST = CTX - (CKT - 1) * P


def key_rows(k):
    return P if k < CKT - 1 else CLAST


def cross_attn_stage(core, w):
    nc = core.nc
    ps, sem = core.ps, core.sem
    x = core.x
    with ExitStack() as ctx:
        def sb(name, shape, dt=F32):
            return ctx.enter_context(nc.sbuf_tensor("ca_" + name, shape, dt))

        w_q = sb("w_q", [P, KC, D])
        w_k = sb("w_k", [P, KC, D])
        w_v = sb("w_v", [P, KC, D])
        b_q = sb("b_q", [P, KC])
        b_k = sb("b_k", [P, KC])
        b_v = sb("b_v", [P, D])
        cT = sb("cT", [P, KC, CTX])
        kT = sb("kT", [P, KC, CTX])
        v = sb("v", [P, CKT, D])
        xn = sb("xn", [P, QT, D])
        xT = sb("xT", [P, KC, T])
        qT = sb("qT", [P, KC, T])
        probs = sb("probs", [P, 2, CTX])
        pT = sb("pT", [P, 2, CKT, P])
        top = sb("top", [P, 2])
        bar = sb("bar", [P, 2])
        den = sb("den", [P, 2])
        rden = sb("rden", [P, 2])
        stats = sb("stats", [P, QT, 6])
        mv = sb("mv", [P, QT, 2])
        rstd = sb("rstd", [P, QT])

        load_block(core, [
            (cT[:, :, :], w["ctx_T"][0, :, :].rearrange("(c p) k -> p c k", p=P)),
            (w_q[:, :, :], w["L1_xattn_Wq_T"].rearrange("(c p) e -> p c e", p=P)),
            (w_k[:, :, :], w["L1_xattn_Wk_T"].rearrange("(c p) e -> p c e", p=P)),
            (w_v[:, :, :], w["L1_xattn_Wv_T"].rearrange("(c p) e -> p c e", p=P)),
            (b_q[:, :], w["L1_xattn_bq_cols"]),
            (b_k[:, :], w["L1_xattn_bk_cols"]),
            (b_v[:, :], w["L1_xattn_bv"].partition_broadcast(P)),
        ])
        SCALE = D ** -0.5
        cuts = [(s, min(BANK, CTX - s)) for s in range(0, CTX, BANK)]
        NG = (CKT + 3) // 4

        def cross_block(b, last_batch):
            with nc.Block() as block:
                @block.sync
                def _(sp):
                    if not last_batch:
                        sp.wait_ge(sem("v_ready"), CKT)
                        sp.dma_start(cT[:, :, :], w["ctx_T"][ds(b + 1, 1), :, :]
                                     .rearrange("o (c p) k -> p (o c) k", p=P)).then_inc(sem("ctx_loaded"), 16)
                        sp.wait_ge(sem("ctx_loaded"), 16)

                @block.tensor
                def _(pe):
                    for n in range(KC * len(cuts)):
                        f, r = divmod(n, len(cuts))
                        s, k = cuts[r]
                        if n >= 4:
                            pe.wait_ge(sem("k_stored"), n - 3)
                        for c in range(KC):
                            last = pe.matmul(ps[:, 2 + n % 4, 0:k], w_k[:, c, f * P:(f + 1) * P],
                                             cT[:, c, s:s + k], start=(c == 0), stop=(c == KC - 1))
                        last.then_inc(sem("k_ready"), 1)
                    for k in range(CKT):
                        if k >= 2:
                            pe.wait_ge(sem("v_stored"), k - 1)
                        for c in range(KC):
                            last = pe.matmul(ps[0:key_rows(k), 6 + k % 2, 0:D],
                                             cT[:, c, k * P:k * P + key_rows(k)], w_v[:, c, :],
                                             start=(c == 0), stop=(c == KC - 1))
                        last.then_inc(sem("v_ready"), 1)
                    norm_pe(core, pe, xn)
                    pe.wait_ge(sem("xT_ready"), KC)
                    pe.wait_ge(sem("k_stored"), KC * len(cuts))
                    for f in range(KC):
                        for c in range(KC):
                            last = pe.matmul(ps[:, 4 + f, :], w_q[:, c, f * P:(f + 1) * P], xT[:, c, :],
                                             start=(c == 0), stop=(c == KC - 1))
                        last.then_inc(sem("q_ready"), 1)

                    def scores(q):
                        if q:
                            pe.wait_ge(sem("probs_ready"), q)
                        else:
                            pe.wait_ge(sem("q_stored"), KC)
                        for c in range(KC):
                            for r, (s, k) in enumerate(cuts):
                                last = pe.matmul(ps[:, r, 0:k], qT[:, c, q * P:(q + 1) * P],
                                                 kT[:, c, s:s + k], start=(c == 0), stop=(c == KC - 1))
                        last.then_inc(sem("scores_ready"), 1)

                    scores(0)
                    for q in range(QT):
                        pe.wait_ge(sem("probs_ready"), q + 1)
                        for g in range(NG):
                            if 2 * q + g // 2:
                                pe.wait_ge(sem("pT_act") if g % 2 == 0 else sem("pT_dve"), 2 * q + g // 2)
                            for k in range(4 * g, min(4 * g + 4, CKT)):
                                last = pe.transpose(ps[0:key_rows(k), 4 + g % 2, (k % 4) * P:(k % 4 + 1) * P],
                                                    probs[:, q % 2, k * P:k * P + key_rows(k)],
                                                    core.ident[:, :])
                            last.then_inc(sem("p_turned"), 1)
                        if q + 1 < QT:
                            scores(q + 1)
                        pe.wait_ge(sem("pT_act"), 2 * q + 2)
                        pe.wait_ge(sem("pT_dve"), 2 * q + 2)
                        if q == 0:
                            pe.wait_ge(sem("v_stored"), CKT)
                        else:
                            pe.wait_ge(sem("x_added"), q)
                        for k in range(CKT):
                            n = key_rows(k)
                            last = pe.matmul(ps[:, 6, 0:D], pT[0:n, q % 2, k, :], v[0:n, k, :],
                                             start=(k == 0), stop=(k == CKT - 1))
                        last.then_inc(sem("values_summed"), 1)

                @block.scalar
                def _(act):
                    for n in range(KC * len(cuts)):
                        f, r = divmod(n, len(cuts))
                        s, k = cuts[r]
                        act.wait_ge(sem("k_ready"), n + 1)
                        act.activation(kT[:, f, s:s + k], ps[:, 2 + n % 4, 0:k], ACT.Identity,
                                       bias=b_k[:, f:f + 1]).then_inc(sem("k_stored"), 1)
                    norm_act(core, act, [xT[:, c, :] for c in range(KC)])
                    for f in range(KC):
                        act.wait_ge(sem("q_ready"), f + 1)
                        act.activation(qT[:, f, :], ps[:, 4 + f, :], ACT.Identity, bias=b_q[:, f:f + 1])\
                            .then_inc(sem("q_stored"), 1)
                    for q in range(QT):
                        act.wait_ge(sem("top_ready"), q + 1)
                        if q >= 2:
                            act.wait_ge(sem("p_turned"), NG * (q - 1))
                        act.activation(probs[:, q % 2, :], ps[:, 0:4, :].rearrange("p r k -> p (r k)")[:, 0:CTX],
                                       ACT.Exp, bias=bar[:, q % 2:q % 2 + 1], scale=SCALE,
                                       accum_out=den[:, q % 2:q % 2 + 1]).then_inc(sem("probs_ready"), 1)
                        for g in (0, 2):
                            act.wait_ge(sem("p_turned"), NG * q + g + 1)
                            if q >= 2:
                                act.wait_ge(sem("values_summed"), q - 1)
                            act.activation(pT[:, q % 2, 4 * g:4 * g + 4, :],
                                           ps[:, 4, :].rearrange("k (g t) -> k g t", t=P), ACT.Copy)\
                                .then_inc(sem("pT_act"), 1)

                @block.gpsimd
                def _(pool):
                    norm_pool(core, pool, rstd)

                @block.vector
                def _(dve):
                    norm_dve(core, dve, b, xn, stats, mv, rstd)
                    for k in range(CKT):
                        n = key_rows(k)
                        dve.wait_ge(sem("v_ready"), k + 1)
                        dve.tensor_tensor(v[0:n, k, :], ps[0:n, 6 + k % 2, 0:D], b_v[0:n, :], ALU.add)\
                            .then_inc(sem("v_stored"), 1)

                    def largest(q):
                        dve.wait_ge(sem("scores_ready"), q + 1)
                        dve.tensor_reduce(top[:, q % 2:q % 2 + 1],
                                          ps[:, 0:4, :].rearrange("p r k -> p (r k)")[:, 0:CTX],
                                          AX.X, ALU.max).then_inc(sem("max_found"), 1)
                        dve.wait_ge(sem("max_found"), q + 1)
                        dve.tensor_scalar(bar[:, q % 2:q % 2 + 1], top[:, q % 2:q % 2 + 1], -SCALE, None,
                                          ALU.mult).then_inc(sem("top_ready"), 1)

                    largest(0)
                    for q in range(QT):
                        for g in (1, 3):
                            kt = 4 * g
                            dve.wait_ge(sem("p_turned"), NG * q + g + 1)
                            if q >= 2:
                                dve.wait_ge(sem("values_summed"), q - 1)
                            if kt + 4 <= CKT:
                                ins = dve.tensor_copy(pT[:, q % 2, kt:kt + 4, :],
                                                      ps[:, 5, :].rearrange("k (g t) -> k g t", t=P))
                            else:
                                ins = dve.tensor_copy(pT[0:CLAST, q % 2, kt, :], ps[0:CLAST, 5, 0:P])
                            ins.then_inc(sem("pT_dve"), 1)
                        if q + 1 < QT:
                            largest(q + 1)
                        dve.wait_ge(sem("probs_ready"), q + 1)
                        dve.reciprocal(rden[:, q % 2:q % 2 + 1], den[:, q % 2:q % 2 + 1])\
                            .then_inc(sem("den_ready"), 1)
                        dve.wait_ge(sem("den_ready"), q + 1)
                        dve.wait_ge(sem("values_summed"), q + 1)
                        xq = x[:, ds(b * QT + q, 1), :]
                        dve.scalar_tensor_tensor(out=xq, in0=ps[:, 6:7, 0:D], scalar=rden[:, q % 2:q % 2 + 1],
                                                 in1=xq, op0=ALU.mult, op1=ALU.add)\
                            .then_inc(sem("x_added"), 1)
            core.fresh()

        with nc.Fori(0, B - 1) as b:
            cross_block(b, False)
        cross_block(B - 1, True)



NE = 64
FF = 128
NSH = 2
EG, EPG = 8, 8
TOPG, TOPE = 4, 8
ROUTE_SCALE = 2.5
RB = 2
QR = RB * QT
EL = 8
EB = 32
HALF = B * T // 2
EW = 2 * KC * FF + D


def moe_stage(core, w, coef_rows):
    nc = core.nc
    ps, sem = core.ps, core.sem
    with ExitStack() as ctx:
        def sb(name, shape, dt=F32):
            return ctx.enter_context(nc.sbuf_tensor("moe_" + name, shape, dt))

        router = sb("router", [P, KC, NE])
        e_bias = sb("e_bias", [P, NE])
        earlier = sb("earlier", [P, EG, EG])
        slots = sb("slots", [P, EL, EW])
        coef = sb("coef", [P, EL, HALF])
        xT_all = sb("xT_all", [P, KC, B * T])
        WR = 3
        x_hi = sb("x_hi", [P, KC, HALF], F32R)
        x_lo = sb("x_lo", [P, KC, HALF], F32R)
        w_hi = sb("w_hi", [P, WR, EW], F32R)
        w_lo = sb("w_lo", [P, WR, EW], F32R)
        ones = sb("ones", [NSH, B * T])

        load_block(core, [
            (router[:, :, :], w["L0_ffn_router_T"].rearrange("(c p) e -> p c e", p=P)),
            (e_bias[:, :], w["L0_ffn_e_bias"].partition_broadcast(P)),
            (earlier[:, :, :], w["earlier"].partition_broadcast(P)),
        ])

        with ExitStack() as inner:
            def sb2(name, shape, dt=F32):
                return inner.enter_context(nc.sbuf_tensor("rt_" + name, shape, dt))

            xn = sb2("xn", [P, QR, D])
            xT = sb2("xT", [P, KC, RB * T])
            score = sb2("score", [P, QR, NE])
            biased = sb2("biased", [P, QR, NE])
            best = sb2("best", [P, QR, EG, 8])
            gsum = sb2("gsum", [P, QR, EG])
            above = sb2("above", [P, QR, EG, EG])
            equal = sb2("equal", [P, QR, EG, EG])
            rank = sb2("rank", [P, QR, EG])
            top = sb2("top", [P, QR, 8])
            marked = sb2("marked", [P, QR, NE])
            total = sb2("total", [P, QR])
            coef_T = sb2("coef_T", [NE, RB * T])
            stats = sb2("stats", [P, QR, 6])
            mv = sb2("mv", [P, QR, 2])
            rstd = sb2("rstd", [P, QR])
            with nc.Fori(0, B // RB) as b:
                with nc.Block() as block:
                    @block.tensor
                    def _(pe):
                        norm_pe(core, pe, xn, tiles=QR)
                        pe.wait_ge(sem("xT_ready"), RB * KC)
                        for q in range(QR):
                            for c in range(KC):
                                last = pe.matmul(ps[:, 4, q * NE:(q + 1) * NE], xT[:, c, q * P:(q + 1) * P],
                                                 router[:, c, :], start=(c == 0), stop=(c == KC - 1))
                        last.then_inc(sem("logits_ready"), 1)
                        pe.wait_ge(sem("coef_ready"), 1)
                        for q in range(QR):
                            last = pe.transpose(ps[0:NE, 5 + q // QT, (q % QT) * P:(q % QT + 1) * P], marked[:, q, :],
                                                core.ident[:, :])
                        last.then_inc(sem("coef_turned"), 1)

                    @block.scalar
                    def _(act):
                        norm_act(core, act, [xT[:, c, :] for c in range(KC)], tiles=QR)
                        act.wait_ge(sem("logits_ready"), 1)
                        act.activation(score[:, :, :], ps[:, 4, :].rearrange("p (q e) -> p q e", e=NE),
                                       ACT.Sigmoid).then_inc(sem("score_ready"), 1)
                        act.wait_ge(sem("coef_turned"), 1)
                        act.activation(coef_T[:, :], ps[0:NE, 5:5 + RB, :].rearrange("e n t -> e (n t)"), ACT.Copy).then_inc(sem("coef_T_ready"), 1)

                    @block.gpsimd
                    def _(pool):
                        norm_pool(core, pool, rstd, tiles=QR)
                        pool.wait_ge(sem("xT_ready"), RB * KC)
                        pool.tensor_copy(xT_all[:, :, ds(b * RB * T, RB * T)], xT[:, :, :])

                    @block.sync
                    def _(sp):
                        sp.wait_ge(sem("coef_T_ready"), 1)
                        sp.dma_start(coef_rows[0:NE, ds(b * RB * T, RB * T)], coef_T[:, :]).then_inc(sem("coef_stored"), 16)
                        sp.wait_ge(sem("coef_stored"), 16)

                    @block.vector
                    def _(dve):
                        norm_dve(core, dve, b, xn, stats, mv, rstd, tiles=QR)
                        chain = Chain(dve, sem("dve_chain"))
                        dve.wait_ge(sem("score_ready"), 1)
                        chain(dve.tensor_tensor(biased[:, :, :], score[:, :, :],
                                                e_bias[:, :].unsqueeze(1).broadcast_to([P, QR, NE]), ALU.add))
                        for q in range(QR):
                            for g in range(EG):
                                last = dve.max(best[:, q, g, :], biased[:, q, g * EPG:(g + 1) * EPG])
                        chain(last)
                        chain(dve.tensor_tensor(gsum[:, :, :], best[:, :, :, 0], best[:, :, :, 1], ALU.add))
                        mine = gsum[:, :, :].unsqueeze(3).broadcast_to([P, QR, EG, EG])
                        theirs = gsum[:, :, :].unsqueeze(2).broadcast_to([P, QR, EG, EG])
                        dve.tensor_tensor(above[:, :, :, :], theirs, mine, ALU.is_gt)
                        chain(dve.tensor_tensor(equal[:, :, :, :], theirs, mine, ALU.is_equal))
                        chain(dve.tensor_tensor(equal[:, :, :, :], equal[:, :, :, :],
                                                earlier[:, :, :].unsqueeze(1).broadcast_to([P, QR, EG, EG]),
                                                ALU.mult))
                        chain(dve.tensor_tensor(above[:, :, :, :], above[:, :, :, :], equal[:, :, :, :], ALU.add))
                        chain(dve.tensor_reduce(rank[:, :, :], above[:, :, :, :], AX.X, ALU.add))
                        chain(dve.tensor_scalar(rank[:, :, :], rank[:, :, :], TOPG - 0.5, None, ALU.is_lt))
                        chain(dve.tensor_tensor(biased[:, :, :].rearrange("p q (g e) -> p q g e", e=EPG),
                                                biased[:, :, :].rearrange("p q (g e) -> p q g e", e=EPG),
                                                rank[:, :, :].unsqueeze(3).broadcast_to([P, QR, EG, EPG]),
                                                ALU.mult))
                        for q in range(QR):
                            last = dve.max(top[:, q, :], biased[:, q, :])
                        chain(last)
                        for q in range(QR):
                            last = dve.match_replace(marked[:, q, :], top[:, q, :], biased[:, q, :], NEG)
                        chain(last)
                        chain(dve.tensor_tensor(marked[:, :, :], marked[:, :, :], biased[:, :, :], ALU.not_equal))
                        chain(dve.tensor_tensor(marked[:, :, :], marked[:, :, :], score[:, :, :], ALU.mult))
                        chain(dve.tensor_reduce(total[:, :], marked[:, :, :], AX.X, ALU.add))
                        chain(dve.tensor_scalar(total[:, :], total[:, :], 1e-20, None, ALU.add))
                        chain(dve.reciprocal(total[:, :], total[:, :]))
                        chain(dve.tensor_tensor(marked[:, :, :], marked[:, :, :],
                                                total[:, :].unsqueeze(2).broadcast_to([P, QR, NE]), ALU.mult))
                        dve.tensor_scalar(marked[:, :, :], marked[:, :, :], ROUTE_SCALE, None, ALU.mult)\
                            .then_inc(sem("coef_ready"), 1)
                core.fresh()

        gate = sb("gate", [P, 2, T])
        prod = sb("prod", [P, 2, T])
        hid = sb("hid", [P, 2, T])
        HR = 3
        hid_hi = sb("hid_hi", [P, HR, T], F32R)
        hid_lo = sb("hid_lo", [P, HR, T], F32R)
        experts = w["L0_ffn_experts"]
        KEEP = NSH
        slot_loaded = [sem(f"slot_{i}_loaded") for i in range(EL)]

        def load_slot(sp, half, e, slot):
            loaded = slot_loaded[slot]
            sp.dma_start(slots[:, slot:slot + 1, :], experts[ds(e, 1), :, :].rearrange("o p n -> p o n"))\
              .then_inc(loaded, 16)
            row = bass.AP(coef_rows.tensor, coef_rows.offset, [[0, P], [B * T, NE + EL], [1, B * T]])
            sp.dma_start(coef[:, slot:slot + 1, :], row[:, ds(e, 1), ds(half * HALF, HALF)])\
              .then_inc(loaded, 16)

        def expert_block(half, step, n_experts, shared):
            units = [(e, t) for e in range(n_experts) for t in range(HALF // T)]
            with nc.Block() as block:
                @block.sync
                def _(sp):
                    if shared:
                        return
                    for e in range(KEEP, EL):
                        load_slot(sp, half, step * EB + e, e)
                    for e in range(EL, EB + KEEP):
                        sp.wait_ge(sem("w_lo_ready"), e - EL + 1)
                        sp.wait_ge(sem("hid_ready"), (e - EL + 1) * (HALF // T))
                        load_slot(sp, half, step * EB + e, e % EL)
                    for i in range(KEEP):
                        sp.wait_ge(slot_loaded[i], 32 * (EB // EL))

                TB = HALF // T

                @block.tensor
                def _(pe):
                    def down(m):
                        e, t = units[m]
                        pe.wait_ge(sem("hid_lo_ready"), m + 1)
                        wd = slice(2 * KC * FF, EW)
                        for q in range(QT):
                            i = t * QT + q
                            hs = slice(q * P, (q + 1) * P)
                            for h, v in ((hid_hi, w_hi), (hid_hi, w_lo), (hid_lo, w_hi)):
                                last = pe.matmul(ps[:, i // 2, (i % 2) * D:(i % 2 + 1) * D],
                                                 h[:, m % HR, hs], v[:, e % WR, wd],
                                                 start=False, stop=False, skip_group_check=True)
                        last.then_inc(sem("unit_done"), 1)

                    for m, (e, t) in enumerate(units):
                        if t == 0:
                            pe.wait_ge(sem("w_lo_ready"), e + 1)
                        for i in range(2):
                            if m >= 2:
                                pe.wait_ge(sem("gate_ready") if i == 0 else sem("prod_ready"), m - 1)
                            n = 0
                            for c in range(KC):
                                ws = slice((i * KC + c) * FF, (i * KC + c + 1) * FF)
                                xs = slice(t * T, (t + 1) * T)
                                for v, y in ((w_hi, x_hi), (w_hi, x_lo), (w_lo, x_hi)):
                                    last = pe.matmul(ps[:, 4 + 2 * (m % 2) + i, :], v[:, e % WR, ws], y[:, c, xs],
                                                     start=(n == 0), stop=(n == 3 * KC - 1))
                                    n += 1
                            last.then_inc(sem("g_ready") if i == 0 else sem("u_ready"), 1)
                        if m >= 2:
                            down(m - 2)
                    down(len(units) - 2)
                    down(len(units) - 1)

                @block.scalar
                def _(act):
                    def split(e):
                        loads = e // EL + (e % EL >= KEEP)
                        if loads:
                            act.wait_ge(slot_loaded[e % EL], 32 * loads)
                        if e >= WR:
                            act.wait_ge(sem("unit_done"), (e - WR + 1) * TB)
                        act.activation(w_hi[:, e % WR, :], slots[:, e % EL, :], ACT.Copy).then_inc(sem("w_hi_ready"), 1)

                    def high(m):
                        act.wait_ge(sem("hid_ready"), m + 1)
                        if m >= HR:
                            act.wait_ge(sem("unit_done"), m - HR + 1)
                        act.activation(hid_hi[:, m % HR, :], hid[:, m % 2, :], ACT.Copy)\
                            .then_inc(sem("hid_hi_ready"), 1)

                    split(0)
                    for m, (e, t) in enumerate(units):
                        act.wait_ge(sem("g_ready"), m + 1)
                        if m >= 2:
                            act.wait_ge(sem("prod_ready"), m - 1)
                        act.activation(gate[:, m % 2, :], ps[:, 4 + 2 * (m % 2), :], ACT.Silu)\
                            .then_inc(sem("gate_ready"), 1)
                        if m:
                            high(m - 1)
                        if t == 0 and e < n_experts - 1:
                            split(e + 1)
                    high(len(units) - 1)

                @block.vector
                def _(dve):
                    def split(e):
                        dve.wait_ge(sem("w_hi_ready"), e + 1)
                        dve.tensor_tensor(w_lo[:, e % WR, :], slots[:, e % EL, :], w_hi[:, e % WR, :].bitcast(F32),
                                          ALU.subtract).then_inc(sem("w_lo_ready"), 1)

                    def low(m):
                        dve.wait_ge(sem("hid_hi_ready"), m + 1)
                        dve.tensor_tensor(hid_lo[:, m % HR, :], hid[:, m % 2, :],
                                          hid_hi[:, m % HR, :].bitcast(F32), ALU.subtract)\
                            .then_inc(sem("hid_lo_ready"), 1)

                    split(0)
                    for m, (e, t) in enumerate(units):
                        dve.wait_ge(sem("u_ready"), m + 1)
                        dve.wait_ge(sem("gate_ready"), m + 1)
                        if m >= 2:
                            dve.wait_ge(sem("hid_ready"), m - 1)
                        dve.tensor_tensor(prod[:, m % 2, :], gate[:, m % 2, :], ps[:, 5 + 2 * (m % 2), :],
                                          ALU.mult).then_inc(sem("prod_ready"), 1)
                        if m:
                            low(m - 1)
                        if t == 0 and e < n_experts - 1:
                            split(e + 1)
                    low(len(units) - 1)

                @block.gpsimd
                def _(pool):
                    for m, (e, t) in enumerate(units):
                        pool.wait_ge(sem("prod_ready"), m + 1)
                        if m >= 2:
                            pool.wait_ge(sem("hid_lo_ready"), m - 1)
                        if shared:
                            ins = pool.tensor_copy(hid[:, m % 2, :], prod[:, m % 2, :])
                        else:
                            ins = pool.tensor_tensor(hid[:, m % 2, :], prod[:, m % 2, :],
                                                     coef[:, e % EL, t * T:(t + 1) * T], ALU.mult)
                        ins.then_inc(sem("hid_ready"), 1)
            core.fresh()

        with nc.Block() as block:
            @block.vector
            def _(dve):
                dve.memset(ones[:, :], 1.0).then_inc(sem("ones_set"), 1)

            @block.sync
            def _(sp):
                sp.wait_ge(sem("ones_set"), 1)
                for e in range(NE, NE + EL, NSH):
                    sp.dma_start(coef_rows[e:e + NSH, :], ones[:, :]).then_inc(sem("ones_stored"), 16)
                sp.wait_ge(sem("ones_stored"), 16 * EL // NSH)
        core.fresh()

        with nc.Fori(0, 2) as half:
            with nc.Block() as block:
                @block.sync
                def _(sp):
                    for e in range(KEEP):
                        load_slot(sp, half, e, e)
                    for i in range(KEEP):
                        sp.wait_ge(slot_loaded[i], 32)

                @block.scalar
                def _(act):
                    act.activation(x_hi[:, :, :], xT_all[:, :, ds(half * HALF, HALF)], ACT.Copy)\
                        .then_inc(sem("x_hi_ready"), 1)

                @block.vector
                def _(dve):
                    dve.memset(ps[:, 0:4, :], 0.0)
                    dve.wait_ge(sem("x_hi_ready"), 1)
                    dve.tensor_tensor(x_lo[:, :, :], xT_all[:, :, ds(half * HALF, HALF)],
                                      x_hi[:, :, :].bitcast(F32), ALU.subtract)
            core.fresh()
            with nc.Fori(0, NE // EB) as step:
                expert_block(half, step, EB, False)
            expert_block(half, None, NSH, True)
            with nc.Block() as block:
                @block.vector
                def _(dve):
                    xh = core.x[:, ds(half * (NT // 2), NT // 2), :]
                    dve.tensor_tensor(xh, xh, ps[:, 0:4, :].rearrange("p a (c d) -> p (a c) d", d=D), ALU.add)
            core.fresh()



PH = 8
NK = 64
DK = 128
PK = 8
NSLOT = PH * PK
ET = NK * NK // P
RMS_EPS = 1e-6
CG = 16
RN = P // (2 * CG)
ROWS = 3
PARTS = 3


class PeerWeights:

    def __init__(self, core, ctx, w):
        def sb(name, shape):
            return ctx.enter_context(core.nc.sbuf_tensor("pr_" + name, shape, F32))

        self.down = sb("down", [P, KC, ET, P])
        self.up = sb("up", [P, ET, D])
        self.norm_w = sb("norm_w", [P, D])
        self.iota = sb("iota", [P, P])
        self.w_q = sb("w_q", [P, 2 * PH, D])
        self.keys = sb("keys", [P, 2 * PH, NK])
        self.loads = [
            (self.w_q[:, :, :], w["L1_ffn_w_q"].rearrange("(s p) d -> p s d", p=P)),
            (self.keys[:, :, :], w["L1_ffn_keys_T"]),
            (self.down[:, :, :, :], w["L1_ffn_down_T"].rearrange("(c p) (i e) -> p c i e", p=P, e=P)),
            (self.up[:, :, :], w["L1_ffn_up"]),
            (self.norm_w[:, :], w["L1_ffn_norm_w"].partition_broadcast(P)),
            (self.iota[:, :], w["iota"].partition_broadcast(P)),
        ]
        load_ahead(core, self.loads)


def peer_stage(core, w, weights):
    nc = core.nc
    ps, sem = core.ps, core.sem
    with ExitStack() as ctx:
        def sb(name, shape, dt=F32):
            return ctx.enter_context(nc.sbuf_tensor("pr_" + name, shape, dt))

        w_sim = sb("w_sim", [P, KC, 2 * PH * NK])
        down, up, norm_w, iota = weights.down, weights.up, weights.norm_w, weights.iota
        w_q, keys = weights.w_q, weights.keys
        act_h = sb("act_h", [P, 2, ET, P])
        hot_part = sb("hot_part", [P, 2, CG, P], BF16)
        hot_tile = sb("hot_tile", [P, 2, CG, ET], BF16)
        hot_w = sb("hot_w", [P, 2, PARTS, CG, ET], BF16)
        w_parts = sb("w_parts", [P, PARTS, QT, NK], BF16)
        w_rest = sb("w_rest", [P, QT, NK])
        xT = sb("xT", [P, KC, T])
        xT_old = sb("xT_old", [P, KC, T])
        turned = sb("turned", [P, ROWS, QT, NK])
        turned_old = sb("turned_old", [P, 2, QT, NK])
        sims = sb("sims", [P, QT, PH, 2, NK])
        key1 = sb("key1", [P, NSLOT])
        key2 = sb("key2", [P, NSLOT])
        upper = sb("upper", [P, NSLOT])
        lists = sb("lists", [P, ROWS, NSLOT])
        twice = sb("twice", [P, ROWS, 2, NSLOT])
        s8 = sb("s8", [P, PH, 2, PK])
        i8 = sb("i8", [P, PH, 2, PK], U32)
        i8f = sb("i8f", [P, PH, 2, PK])
        sums = sb("sums", [P, PH, PK * PK])
        f8 = sb("f8", [P, PH, PK])
        pk = sb("pk", [P, PH, PK], U32)
        ab = sb("ab", [P, 2, NSLOT], U32)
        abf = sb("abf", [P, 2, NSLOT])
        pick = sums[:, :, :].rearrange("p h (k a) -> p (h k) a", a=PK)
        stats = sb("stats", [P, QT, 6])
        mv = sb("mv", [P, QT, 2])
        rstd = sb("rstd", [P, QT])
        ssq = sb("ssq", [P, QT])
        xn = sims[:, 0, :, :, :].rearrange("p h a k -> p (h a k)").rearrange("p (q d) -> p q d", d=D)
        square = sims[:, 1, 0:2, :, :].rearrange("p h a k -> p (h a k)")

        await_ahead(core, len(weights.loads))
        with nc.Block() as block:
            @block.tensor
            def _(pe):
                for c in range(KC):
                    for s in range(2 * PH):
                        last = pe.matmul(ps[:, 2 * c + s // PH, (s % PH) * NK:(s % PH + 1) * NK],
                                         w_q[:, s, c * P:(c + 1) * P], keys[:, s, :], start=True, stop=True)
                        if s % PH == PH - 1:
                            last.then_inc(sem("w_sim_ready"), 1)

            @block.scalar
            def _(act):
                for i in range(2 * KC):
                    act.wait_ge(sem("w_sim_ready"), i + 1)
                    act.activation(w_sim[:, i // 2, (i % 2) * BANK:(i % 2 + 1) * BANK], ps[:, i, :], ACT.Copy)
        core.fresh()

        def rms(dve, chain):
            for q in range(QT):
                chain(dve.tensor_tensor_reduce(square, xn[:, q, :], xn[:, q, :], 1.0, 0.0,
                                               ALU.mult, ALU.add, ssq[:, q:q + 1]))
            dve.tensor_scalar(ssq[:, :], ssq[:, :], 1.0 / D, RMS_EPS, ALU.mult, ALU.add)\
                .then_inc(sem("ssq_ready"), 1)
            dve.wait_ge(sem("rms_ready"), 1)
            for q in range(QT):
                dve.scalar_tensor_tensor(out=xn[:, q, :], in0=xn[:, q, :], scalar=ssq[:, q:q + 1],
                                         in1=norm_w[:, :], op0=ALU.mult, op1=ALU.mult)\
                    .then_inc(sem("xn_ready"), 1)

        ED = BANK // P
        NDOWN = ET // ED

        def weight_bank(r, a):
            return (6, 4)[r % 2] + a

        def peer_block(new, old):
            with nc.Block() as block:
                @block.tensor
                def _(pe):
                    def down_products(q, steps):
                        for n in steps:
                            m = q * NDOWN + n
                            if m >= 2:
                                pe.wait_ge(sem("gelu_done"), m - 1)
                            for i in range(ED):
                                for c in range(KC):
                                    last = pe.matmul(ps[:, 2 + n % 2, i * P:(i + 1) * P],
                                                     down[:, c, ED * n + i, :], xT_old[:, c, q * P:(q + 1) * P],
                                                     start=(c == 0), stop=(c == KC - 1))
                            last.then_inc(sem("down_ready"), 1)

                    def outer(r):
                        pe.wait_ge(sem("hot_part_ready"), r + 1)
                        pe.wait_ge(sem("hot_w_ready"), r + 1)
                        if r >= 2:
                            pe.wait_ge(sem("weighted"), 2 * (r - 1))
                        for t in range(CG):
                            for part in range(PARTS):
                                for a in range(2):
                                    s = slice(NK * a, NK * (a + 1))
                                    last = pe.matmul(ps[:, weight_bank(r, a), t * ET:(t + 1) * ET],
                                                     hot_part[s, r % 2, t, :], hot_w[s, r % 2, part, t, :],
                                                     start=(part == 0), stop=(part == PARTS - 1))
                        last.then_inc(sem("outer_ready"), 1)

                    def up_products(q):
                        pe.wait_ge(sem("weighted"), 2 * RN * (q + 1))
                        if q >= 2:
                            pe.wait_ge(sem("x_added"), q - 1)
                        elif q == 0 and new is not None:
                            pe.wait_ge(sem("sims_stored"), 2 * QT)
                        for i in range(ET):
                            last = pe.matmul(ps[:, 1, (q % 2) * D:(q % 2 + 1) * D], act_h[:, q % 2, i, :],
                                             up[:, i, :], start=(i == 0), stop=(i == ET - 1))
                        last.then_inc(sem("up_ready"), 1)

                    def similarities(q):
                        if q:
                            pe.wait_ge(sem("sims_stored"), 2 * q)
                        for a in range(2):
                            for c in range(KC):
                                last = pe.matmul(ps[:, a, :], xT[:, c, q * P:(q + 1) * P],
                                                 w_sim[:, c, a * BANK:(a + 1) * BANK],
                                                 start=(c == 0), stop=(c == KC - 1))
                            last.then_inc(sem("sims_ready"), 1)

                    def turn_lists(q):
                        pe.wait_ge(sem("lists_ready"), q + 1)
                        if q:
                            pe.wait_ge(sem("turned_stored"), 2 * q)
                        else:
                            pe.wait_ge(sem("sims_stored"), 2 * QT)
                        for i in range(ROWS):
                            last = pe.transpose(ps[:, 0, i * P:(i + 1) * P],
                                                twice[:, i, :, :].rearrange("p a s -> p (a s)"),
                                                core.ident[:, :])
                        last.then_inc(sem("lists_turned"), 1)

                    if old is not None:
                        down_products(0, range(NDOWN))
                    if new is not None:
                        norm_pe(core, pe, xn)
                        pe.wait_ge(sem("xT_ready"), KC)
                    for q in range(QT):
                        for n in range(RN):
                            if old is not None:
                                outer(q * RN + n)
                            if new is not None and q == 0:
                                similarities(n)
                            if new is not None and q and n == 1:
                                turn_lists(q - 1)
                            if old is not None and q + 1 < QT:
                                k = NDOWN // RN
                                down_products(q + 1, range(n * k, (n + 1) * k))
                        if old is not None:
                            up_products(q)
                    if new is not None:
                        turn_lists(QT - 1)

                @block.scalar
                def _(act):
                    def gelu(q, steps):
                        if q >= 2 and steps.start == 0:
                            act.wait_ge(sem("up_ready"), q - 1)
                        for n in steps:
                            act.wait_ge(sem("down_ready"), q * NDOWN + n + 1)
                            act.activation(act_h[:, q % 2, ED * n:ED * (n + 1), :],
                                           ps[:, 2 + n % 2, :].rearrange("p (i t) -> p i t", i=ED), ACT.Gelu)\
                                .then_inc(sem("gelu_done"), 1)

                    def store_turned(q):
                        act.wait_ge(sem("lists_turned"), q + 1)
                        for a in range(2):
                            s = slice(NK * a, NK * (a + 1))
                            act.activation(turned[s, :, q, :],
                                           ps[s, 0, 0:ROWS * P].rearrange("p (i t) -> p i t", i=ROWS)[:, :, s],
                                           ACT.Copy).then_inc(sem("turned_stored"), 1)

                    if old is not None:
                        gelu(0, range(NDOWN))
                    if new is not None:
                        norm_act(core, act, [xT[:, c, :] for c in range(KC)])
                    for q in range(QT):
                        for n in range(RN):
                            if new is not None and q == 0:
                                for a in range(2):
                                    act.wait_ge(sem("sims_ready"), 2 * n + a + 1)
                                    act.activation(sims[:, n, a * PH // 2:(a + 1) * PH // 2, :, :],
                                                   ps[:, a, :].rearrange("p (h a k) -> p h a k", a=2, k=NK),
                                                   ACT.Copy).then_inc(sem("sims_stored"), 1)
                            if new is not None and q and n == 1:
                                store_turned(q - 1)
                            if old is not None and q + 1 < QT:
                                k = NDOWN // RN
                                gelu(q + 1, range(n * k, (n + 1) * k))
                    if new is not None:
                        store_turned(QT - 1)

                @block.gpsimd
                def _(pool):
                    if new is not None:
                        norm_pool(core, pool, rstd)
                        pool.wait_ge(sem("ssq_ready"), 1)
                        pool.tensor_tensor(ssq[:, :], ssq[:, :], core.neg_half[:, 0:QT], ALU.pow)\
                            .then_inc(sem("rms_ready"), 1)
                    if old is not None:
                        for r in range(QT * RN):
                            q, c = divmod(r, RN)
                            pool.wait_ge(sem("hot_tile_ready"), r + 1)
                            if r >= 2:
                                pool.wait_ge(sem("outer_ready"), r - 1)
                            for part in range(PARTS):
                                last = pool.tensor_tensor(
                                    hot_w[:, r % 2, part, :, :], hot_tile[:, r % 2, :, :],
                                    w_parts[:, part, q, c * CG:(c + 1) * CG].unsqueeze(2)
                                    .broadcast_to([P, CG, ET]), ALU.mult)
                            last.then_inc(sem("hot_w_ready"), 1)
                    if new is not None:
                        if old is not None:
                            pool.wait_ge(sem("down_ready"), QT * NDOWN)
                        pool.wait_ge(sem("xT_ready"), KC)
                        pool.tensor_copy(xT_old[:, :, :], xT[:, :, :])
                        pool.wait_ge(sem("turned_stored"), 2 * QT)
                        if old is not None:
                            pool.wait_ge(sem("hot_w_ready"), QT * RN)
                            pool.wait_ge(sem("hot_part_ready"), QT * RN)
                        pool.tensor_copy(turned_old[:, :, :, :], turned[:, 0:2, :, :])
                        chain = Chain(pool, sem("parts_chain"))
                        chain(pool.tensor_copy(w_parts[:, 0, :, :], turned[:, 2, :, :]))
                        chain(pool.tensor_tensor(w_rest[:, :, :], turned[:, 2, :, :], w_parts[:, 0, :, :],
                                                 ALU.subtract))
                        chain(pool.tensor_copy(w_parts[:, 1, :, :], w_rest[:, :, :]))
                        pool.tensor_tensor(w_parts[:, 2, :, :], w_rest[:, :, :], w_parts[:, 1, :, :], ALU.subtract)

                @block.vector
                def _(dve):
                    chain = Chain(dve, sem("dve_chain"))

                    def make_lists(q):
                        dve.wait_ge(sem("sims_stored"), 2 * (q + 1))
                        for h in range(PH):
                            for a in range(2):
                                last = dve.max(s8[:, h, a, :], sims[:, q, h, a, :])
                        chain(last)
                        for h in range(PH):
                            for a in range(2):
                                last = dve.max_index(i8[:, h, a, :], s8[:, h, a, :], sims[:, q, h, a, :])
                        chain(last)
                        dve.tensor_copy(i8f[:, :, :, :], i8[:, :, :, :])
                        chain(dve.tensor_tensor(
                            sums[:, :, :].rearrange("p h (a b) -> p h a b", a=PK),
                            s8[:, :, 0, :].unsqueeze(3).broadcast_to([P, PH, PK, PK]),
                            s8[:, :, 1, :].unsqueeze(2).broadcast_to([P, PH, PK, PK]), ALU.add))
                        for h in range(PH):
                            last = dve.max(f8[:, h, :], sums[:, h, :])
                        chain(last)
                        for h in range(PH):
                            last = dve.max_index(pk[:, h, :], f8[:, h, :], sums[:, h, :])
                        chain(last)
                        pkf = pk[:, :, :].rearrange("p h k -> p (h k)")
                        dve.tensor_scalar(ab[:, 0, :], pkf, 3, None, ALU.logical_shift_right)
                        chain(dve.tensor_scalar(ab[:, 1, :], pkf, PK - 1, None, ALU.bitwise_and))
                        chain(dve.tensor_copy(abf[:, :, :], ab[:, :, :]))
                        for a in range(2):
                            chain(dve.tensor_tensor(pick,
                                                    abf[:, a, :].unsqueeze(2).broadcast_to([P, NSLOT, PK]),
                                                    iota[:, 0:PK].unsqueeze(1).broadcast_to([P, NSLOT, PK]),
                                                    ALU.is_equal))
                            p4 = pick.rearrange("p (h k) a -> p h k a", h=PH)
                            chain(dve.tensor_tensor(p4, p4, i8f[:, :, a, :].unsqueeze(2)
                                                    .broadcast_to([P, PH, PK, PK]), ALU.mult))
                            chain(dve.tensor_reduce((key1, key2)[a][:, :], pick, AX.X, ALU.add))
                        dve.tensor_scalar(lists[:, 2, :], f8[:, :, :].rearrange("p h k -> p (h k)"),
                                          0.0, None, ALU.max)
                        chain(dve.tensor_scalar(upper[:, :], key1[:, :], ET - 0.5, None, ALU.is_ge))
                        dve.scalar_tensor_tensor(out=lists[:, 0, :], in0=upper[:, :], scalar=float(NK),
                                                 in1=key2[:, :], op0=ALU.mult, op1=ALU.add)
                        chain(dve.scalar_tensor_tensor(out=lists[:, 1, :], in0=upper[:, :], scalar=-float(ET),
                                                       in1=key1[:, :], op0=ALU.mult, op1=ALU.add))
                        if q:
                            dve.wait_ge(sem("lists_turned"), q)
                        dve.tensor_copy(twice[:, :, :, :],
                                        lists[:, :, :].unsqueeze(2).broadcast_to([P, ROWS, 2, NSLOT]))\
                            .then_inc(sem("lists_ready"), 1)

                    def one_hot(r):
                        q, c = divmod(r, RN)
                        cols = slice(c * CG, (c + 1) * CG)
                        if r >= 2:
                            dve.wait_ge(sem("hot_w_ready"), r - 1)
                            dve.wait_ge(sem("outer_ready"), r - 1)
                        dve.tensor_tensor(hot_tile[:, r % 2, :, :], iota[:, 0:ET].unsqueeze(1).broadcast_to([P, CG, ET]),
                                          turned_old[:, 1, q, cols].unsqueeze(2).broadcast_to([P, CG, ET]),
                                          ALU.is_equal).then_inc(sem("hot_tile_ready"), 1)
                        dve.tensor_tensor(hot_part[:, r % 2, :, :], iota[:, :].unsqueeze(1).broadcast_to([P, CG, P]),
                                          turned_old[:, 0, q, cols].unsqueeze(2).broadcast_to([P, CG, P]),
                                          ALU.is_equal).then_inc(sem("hot_part_ready"), 1)

                    def weigh(r):
                        q, n = divmod(r, RN)
                        if n == 0:
                            dve.wait_ge(sem("gelu_done"), (q + 1) * NDOWN)
                        dve.wait_ge(sem("outer_ready"), r + 1)
                        for a in range(2):
                            t0 = a * NK + n * CG
                            hs = act_h[:, q % 2, :, t0:t0 + CG].rearrange("p i t -> p t i")
                            dve.tensor_tensor(hs, hs, ps[:, weight_bank(r, a), :].rearrange("p (t i) -> p t i", i=ET),
                                              ALU.mult).then_inc(sem("weighted"), 1)

                    def add_x(q):
                        dve.wait_ge(sem("up_ready"), q + 1)
                        xq = core.x[:, ds(old * QT + q, 1), :]
                        dve.tensor_tensor(xq, xq, ps[:, 1:2, (q % 2) * D:(q % 2 + 1) * D], ALU.add)\
                            .then_inc(sem("x_added"), 1)

                    if new is not None:
                        norm_dve(core, dve, new, xn, stats, mv, rstd, extra=lambda c: rms(dve, c))
                    if old is not None:
                        one_hot(0)
                    for q in range(QT):
                        if old is not None:
                            for n in range(RN):
                                r = q * RN + n
                                if r + 1 < QT * RN:
                                    one_hot(r + 1)
                                weigh(r)
                                if n == 0 and q:
                                    add_x(q - 1)
                        if new is not None:
                            make_lists(q)
                    if old is not None:
                        add_x(QT - 1)
            core.fresh()

        peer_block(0, None)
        with nc.Fori(1, B) as b:
            peer_block(b, b - 1)
        peer_block(None, B - 1)




def build(nc, w, out, stages):
    with ExitStack() as ctx:
        core = Core(nc, ctx)
        scratch = {
            "xdbl": nc.dram_tensor("xdbl_scratch", (2 * DS, T), F32, kind="Internal").ap(),
            "coef": nc.dram_tensor("coef_scratch", (NE + EL, B * T), F32, kind="Internal").ap(),
            "rel_rows": nc.dram_tensor("rel_rows_scratch", (H, SLAB), F32, kind="Internal").ap(),
        }
        load_block(core, [
            (core.x[:, :, :], w["x"].rearrange("b (q p) d -> p (b q) d", p=P)),
            (core.ident[:, :], w["ident"]),
        ])
        with nc.Block() as block:
            @block.vector
            def _(dve):
                dve.memset(core.neg_half[:, :], -0.5)
        if "ssm" in stages:
            ssm_stage(core, w, scratch["xdbl"])
        if "gather_attn" in stages:
            gather_attn_stage(core, w)
        if "moe" in stages:
            moe_stage(core, w, scratch["coef"])
        if "self_attn" in stages:
            self_attn_stage(core, w, scratch["rel_rows"])
        with ExitStack() as ahead:
            if "peer" in stages:
                peer_weights = PeerWeights(core, ahead, w)
            if "cross_attn" in stages:
                cross_attn_stage(core, w)
            if "peer" in stages:
                peer_stage(core, w, peer_weights)
        stored = core.sem("out_stored")
        with nc.Block() as block:
            @block.sync
            def _(sp):
                sp.dma_start(out.rearrange("b (q p) d -> p (b q) d", p=P), core.x[:, :, :]).then_inc(stored, 16)
                sp.wait_ge(stored, 16)


def layouts(inputs):
    import numpy as np

    w = {k: np.ascontiguousarray(v) for k, v in inputs.items()}
    out = {"ident": np.eye(P, dtype=np.float32), "x": w["x"]}
    def columns(v):
        return np.ascontiguousarray(v.reshape(-1, P).T)

    for k in ("conv_w", "A_log"):
        out["L0_attn_" + k] = w["L0_attn_" + k]
    for k in ("conv_b", "D_param", "b_dt"):
        out["L0_attn_" + k + "_cols"] = columns(w["L0_attn_" + k])
    for k in ("W_in", "W_dt", "W_x", "W_out"):
        out["L0_attn_" + k + "_T"] = np.ascontiguousarray(w["L0_attn_" + k].T)
    def strips(wt):
        return np.pad(wt.reshape(wt.shape[0], H, DH), ((0, 0), (0, 0), (0, STRIP - DH))).reshape(wt.shape[0], -1)

    def strip_columns(v):
        return np.ascontiguousarray(strips(v.reshape(1, -1)).reshape(G, P).T)

    def strip_rows(wt):
        return np.pad(wt.reshape(H, DH, D), ((0, 0), (0, STRIP - DH), (0, 0))).reshape(-1, D)

    out["spread"] = np.repeat(np.eye(P, dtype=np.float32)[:, DH::STRIP], STRIP, axis=1)
    out["ctx_T"] = np.ascontiguousarray(w["ctx_1024"].transpose(0, 2, 1))
    for k in ("q", "k"):
        out[f"L0_xattn_W{k}_strips"] = strips(w[f"L0_xattn_W{k}"].T)
        out[f"L0_xattn_b{k}_strips"] = strip_columns(w[f"L0_xattn_b{k}"])
    out["L0_xattn_Wv_strips"] = strips(w["L0_xattn_Wv"].T)
    bv_one = np.pad(w["L0_xattn_bv"].reshape(H, DH), ((0, 0), (0, 1)), constant_values=1)
    out["L0_xattn_bv_one_strips"] = np.ascontiguousarray(
        np.pad(bv_one, ((0, 0), (0, STRIP - DH - 1))).reshape(G, P).T)
    out["L0_xattn_Wo_strips"] = strip_rows(w["L0_xattn_Wo"].T)
    out["L0_xattn_bo"] = w["L0_xattn_bo"]
    wq, wk, wv = (w["L1_attn_qkv_w"][i * D:(i + 1) * D] for i in range(3))
    bq, bk, bv = (w["L1_attn_qkv_b"][i * D:(i + 1) * D] for i in range(3))
    out["L1_attn_Wq_strips"], out["L1_attn_Wk_strips"] = strips(wq.T), strips(wk.T)
    out["L1_attn_bq_strips"], out["L1_attn_bk_strips"] = strip_columns(bq), strip_columns(bk)
    out["L1_attn_Wv_T"], out["L1_attn_bv"] = np.ascontiguousarray(wv.T), np.ascontiguousarray(bv)
    out["L1_attn_proj_w_strips"] = strip_rows(w["L1_attn_proj_w"].T)
    out["L1_attn_proj_b"] = w["L1_attn_proj_b"]
    out["L1_attn_rel_back"] = np.ascontiguousarray(w["L1_attn_rel_pos_emb"][::-1][:RELK])
    for k in ("q", "k", "v"):
        out[f"L1_xattn_W{k}_T"] = np.ascontiguousarray(w[f"L1_xattn_W{k}"].T)
    for k in ("q", "k"):
        out[f"L1_xattn_b{k}_cols"] = columns(w[f"L1_xattn_b{k}"])
    out["L1_xattn_bv"] = w["L1_xattn_bv"]

    def expert_parts(wg, wu, wd):
        n = wg.shape[0]
        halves = [m.reshape(n, KC, P, FF).transpose(0, 2, 1, 3).reshape(n, P, KC * FF) for m in (wg, wu)]
        return np.concatenate(halves + [wd], axis=2)

    routed = expert_parts(w["L0_ffn_Wg"], w["L0_ffn_Wu"], w["L0_ffn_Wd"])
    shared = expert_parts(w["L0_ffn_SWg"].reshape(D, NSH, FF).transpose(1, 0, 2),
                          w["L0_ffn_SWu"].reshape(D, NSH, FF).transpose(1, 0, 2),
                          w["L0_ffn_SWd"].reshape(NSH, FF, D))
    out["L0_ffn_experts"] = np.pad(np.concatenate([routed, shared]), ((0, EL - NSH), (0, 0), (0, 0)))
    out["L0_ffn_router_T"] = np.ascontiguousarray(w["L0_ffn_router_w"].T)
    out["L0_ffn_e_bias"] = w["L0_ffn_e_bias"]
    out["earlier"] = np.tril(np.ones((EG, EG), np.float32), -1)

    out["flip"] = np.ascontiguousarray(np.eye(P, dtype=np.float32)[::-1])
    out["iota"] = np.arange(P, dtype=np.float32)
    out["L1_ffn_norm_w"] = w["L1_ffn_norm_w"]
    out["L1_ffn_w_q"] = w["L1_ffn_w_q"]
    out["L1_ffn_keys_T"] = np.ascontiguousarray(w["L1_ffn_keys"].transpose(3, 0, 2, 1).reshape(DK, 2 * PH, NK))
    tiles = (2, ET, NK, D)
    out["L1_ffn_down_T"] = np.ascontiguousarray(
        w["L1_ffn_expert_down"].reshape(tiles).transpose(3, 1, 0, 2).reshape(D, NK * NK))
    out["L1_ffn_up"] = np.ascontiguousarray(
        w["L1_ffn_expert_up"].reshape(tiles).transpose(0, 2, 1, 3).reshape(P, ET, D))
    return out


def kernel(**inputs):
    import numpy as _np
    import concourse.bacc as _bacc
    from concourse import mybir as _mybir
    from concourse.bass_utils import run_bass_kernel_spmd as _run

    nc = _bacc.Bacc("TRN2", target_bir_lowering=False, num_devices=1)
    arrays, aps = {}, {}
    for name, a in layouts({k: _np.asarray(v) for k, v in inputs.items()}).items():
        arrays[name + "_dram"] = a
        aps[name] = nc.dram_tensor(name + "_dram", a.shape, _mybir.dt.from_np(a.dtype), kind="ExternalInput").ap()
    out = nc.dram_tensor("out_dram", (B, T, D), F32, kind="ExternalOutput").ap()
    build(nc, aps, out, STAGES)
    r = _run(nc, [arrays], core_ids=[0])
    return r.results[0]["out_dram"]
```
